# Optimizing a Trainium2 kernel written in Bass

```python
import numpy as np
import jax
import jax.numpy as jnp

def _softmax(x, axis=-1):
    return jax.nn.softmax(x, axis=axis)

def _gelu(x):
    return jax.nn.gelu(x, approximate=True)

def _silu(x):
    return jax.nn.silu(x)

def _sigmoid(x):
    return jax.nn.sigmoid(x)

def _layernorm(x, axis=-1, eps=1e-05):
    m = jnp.mean(x, axis=axis, keepdims=True)
    v = jnp.var(x, axis=axis, keepdims=True)
    return (x - m) / jnp.sqrt(v + eps)

def _scatter_add(tgt, idx, src, axis=0):
    return tgt.at[idx].add(src)

def _segment_sum(src, seg, n):
    return jax.ops.segment_sum(src, seg, n)
kernel_name = 'mk_gnn_preln_d4_gnn_r32_385ddd'

def setup_inputs(seed: int=0):
    np.random.seed(seed)
    _w = jnp.asarray

    def _rec_inputs():
        import jax
        import jax.numpy as jnp
        _gk = jax.random.key(seed)
        x = -0.0005121 + 1.001 * jax.random.normal(jax.random.fold_in(_gk, 1), (50000, 64), jnp.float32)
        src = jax.random.randint(jax.random.fold_in(_gk, 2), (50000,), 0, 50000, jnp.int32)
        dst = jax.random.randint(jax.random.fold_in(_gk, 3), (50000,), 0, 50000, jnp.int32)
        _o = jnp.argsort(dst, stable=True)
        src = src[_o]
        dst = dst[_o]
        edge_attr_64 = 0.000102155 + 1.00015 * jax.random.normal(jax.random.fold_in(_gk, 13), (50000, 64), jnp.float32)
        edge_type_2 = jax.random.randint(jax.random.fold_in(_gk, 15), (50000,), 0, 2, jnp.int32)
        return (x, src, dst, edge_attr_64, edge_type_2)
    x, src, dst, edge_attr_64, edge_type_2 = _rec_inputs()

    def _L0_gnn_setup():
        import jax, jax.numpy as jnp
        import numpy as np
        N_NODES = 50000
        N_EDGES = 25000
        IN_FEATS = 64
        OUT_FEATS = 64
        key = jax.random.key(seed)
        k_h, k_norm, k_w, k_b, k_src, k_dst = jax.random.split(key, 6)
        h = jax.random.normal(k_h, (N_NODES, IN_FEATS), dtype=jnp.float32)
        norm = jax.random.uniform(k_norm, (N_NODES, 1), dtype=jnp.float32, minval=0.05, maxval=1.0)
        stdv = 1.0 / np.sqrt(OUT_FEATS)
        weight = jax.random.uniform(k_w, (IN_FEATS, OUT_FEATS), dtype=jnp.float32, minval=-stdv, maxval=stdv)
        bias = jax.random.uniform(k_b, (OUT_FEATS,), dtype=jnp.float32, minval=-stdv, maxval=stdv)
        src = jax.random.randint(k_src, (N_EDGES,), 0, N_NODES, dtype=jnp.int64)
        dst = jax.random.randint(k_dst, (N_EDGES,), 0, N_NODES, dtype=jnp.int64)
        return {'h': h, 'norm': norm, 'weight': weight, 'bias': bias, 'src': src, 'dst': dst}
    _L0_gnn_all = _L0_gnn_setup()
    _L0_gnn_in = {k: v for k, v in _L0_gnn_all.items() if k in ('weight', 'bias')}
    del _L0_gnn_all

    def _L1_gnn_setup():
        import jax, jax.numpy as jnp
        import numpy as np
        N_NODES = 3125
        N_EDGES = 50000
        D_FEAT = 64
        EMB_DIM = 64

        def _norm_by_degree(x, degree):
            return x * jax.lax.rsqrt(jnp.maximum(degree.astype(x.dtype), 1.0))[:, None]
        key = jax.random.key(seed)
        k1, k2, k3, k4 = jax.random.split(key, 4)
        x = jax.random.normal(k1, (N_NODES, D_FEAT), dtype=jnp.float32)
        senders = jax.random.randint(k2, (N_EDGES,), 0, N_NODES, dtype=jnp.int32)
        receivers = jax.random.randint(k3, (N_EDGES,), 0, N_NODES, dtype=jnp.int32)
        W = jax.random.normal(k4, (2 * D_FEAT, EMB_DIM), dtype=jnp.float32) * (1.0 / np.sqrt(2 * D_FEAT))
        b = jnp.zeros((EMB_DIM,), dtype=jnp.float32)
        return {'x': x, 'senders': senders, 'receivers': receivers, 'W': W, 'b': b}
    _L1_gnn_all = _L1_gnn_setup()
    _L1_gnn_in = {k: v for k, v in _L1_gnn_all.items() if k in ('W', 'b')}
    del _L1_gnn_all

    def _L2_gnn_setup():
        import jax, jax.numpy as jnp
        import numpy as np
        N, E, F, H, ED = (50000, 15625, 64, 4, 64)
        NEG_SLOPE = 0.2
        BN_EPS = 1e-05
        SM_EPS = 1e-16

        def gatv2_layer(x, edge_index, edge_attr, W_l, b_l, W_r, b_r, W_e, att, bias, gamma, beta):
            n = x.shape[0]
            x_l = (x @ W_l + b_l).reshape(n, H, F)
            x_r = (x @ W_r + b_r).reshape(n, H, F)
            src0, dst0 = (edge_index[0], edge_index[1])
            cnt = jax.ops.segment_sum(jnp.ones((edge_attr.shape[0],), x.dtype), dst0, num_segments=n)
            loop_attr = jax.ops.segment_sum(edge_attr, dst0, num_segments=n) / jnp.maximum(cnt, 1.0)[:, None]
            src = jnp.concatenate([src0, jnp.arange(n, dtype=src0.dtype)])
            dst = jnp.concatenate([dst0, jnp.arange(n, dtype=dst0.dtype)])
            ea = jnp.concatenate([edge_attr, loop_attr], axis=0)
            e_emb = (ea @ W_e).reshape(-1, H, F)
            m = jax.nn.leaky_relu(x_l[src] + x_r[dst] + e_emb, NEG_SLOPE)
            alpha = jnp.einsum('ehf,hf->eh', m, att)
            amax = jax.ops.segment_max(alpha, dst, num_segments=n)
            ex = jnp.exp(alpha - amax[dst])
            denom = jax.ops.segment_sum(ex, dst, num_segments=n)
            alpha = ex / (denom[dst] + SM_EPS)
            out = jax.ops.segment_sum(x_l[src] * alpha[..., None], dst, num_segments=n)
            out = out.mean(axis=1) + bias
            mu = out.mean(axis=0)
            var = out.var(axis=0)
            out = gamma * (out - mu) * jax.lax.rsqrt(var + BN_EPS) + beta
            return jax.nn.relu(out)
        key = jax.random.key(seed)
        ks = jax.random.split(key, 12)
        s = 1.0 / np.sqrt(F)
        se = 1.0 / np.sqrt(ED)
        return {'x': jax.random.normal(ks[0], (N, F), jnp.float32), 'edge_index': jax.random.randint(ks[1], (2, E), 0, N, jnp.int32), 'edge_attr': jax.random.normal(ks[2], (E, ED), jnp.float32), 'W_l': jax.random.normal(ks[3], (F, H * F), jnp.float32) * s, 'b_l': jnp.zeros((H * F,), jnp.float32), 'W_r': jax.random.normal(ks[4], (F, H * F), jnp.float32) * s, 'b_r': jnp.zeros((H * F,), jnp.float32), 'W_e': jax.random.normal(ks[5], (ED, H * F), jnp.float32) * se, 'att': jax.random.normal(ks[6], (H, F), jnp.float32) * s, 'bias': jnp.zeros((F,), jnp.float32), 'gamma': jnp.ones((F,), jnp.float32), 'beta': jnp.zeros((F,), jnp.float32)}
    _L2_gnn_all = _L2_gnn_setup()
    _L2_gnn_in = {k: v for k, v in _L2_gnn_all.items() if k in ('W_l', 'b_l', 'W_r', 'b_r', 'W_e', 'att', 'bias', 'gamma', 'beta')}
    del _L2_gnn_all

    def _L3_gnn_setup():
        import jax, jax.numpy as jnp
        import numpy as np
        N_NODES = 3125
        N_EDGES = 31250
        DIM = 64

        def rel_graph_conv(x, src, dst, etype, W, Ws, b, act):
            h = jnp.einsum('nd,rdo->rno', x, W)
            m = jnp.where((etype == 0)[:, None], h[0][src], h[1][src])
            agg = jax.ops.segment_sum(m, dst, num_segments=x.shape[0])
            out = agg + x @ Ws + b
            return act(out) if act is not None else out
        key = jax.random.key(seed)
        ks = jax.random.split(key, 16)
        scale = 1.0 / np.sqrt(DIM)
        inp = {'features': jax.random.normal(ks[0], (N_NODES, DIM), dtype=jnp.float32), 'src': jax.random.randint(ks[1], (N_EDGES,), 0, N_NODES, dtype=jnp.int32), 'dst': jax.random.randint(ks[2], (N_EDGES,), 0, N_NODES, dtype=jnp.int32), 'etype': jax.random.randint(ks[3], (N_EDGES,), 0, 2, dtype=jnp.int32)}
        for i in range(3):
            inp[f'W{i}'] = jax.random.normal(ks[4 + 3 * i], (2, DIM, DIM), dtype=jnp.float32) * scale
            inp[f'Ws{i}'] = jax.random.normal(ks[5 + 3 * i], (DIM, DIM), dtype=jnp.float32) * scale
            inp[f'b{i}'] = jnp.zeros((DIM,), dtype=jnp.float32)
        return inp
    _L3_gnn_all = _L3_gnn_setup()
    _L3_gnn_in = {k: v for k, v in _L3_gnn_all.items() if k in ('W0', 'Ws0', 'b0', 'W1', 'Ws1', 'b1', 'W2', 'Ws2', 'b2')}
    del _L3_gnn_all
    return {'x': x, 'src': src, 'dst': dst, 'edge_attr_64': edge_attr_64, 'edge_type_2': edge_type_2, 'L0_gnn_weight': _L0_gnn_in['weight'], 'L0_gnn_bias': _L0_gnn_in['bias'], 'L1_gnn_W': _L1_gnn_in['W'], 'L1_gnn_b': _L1_gnn_in['b'], 'L2_gnn_W_l': _L2_gnn_in['W_l'], 'L2_gnn_b_l': _L2_gnn_in['b_l'], 'L2_gnn_W_r': _L2_gnn_in['W_r'], 'L2_gnn_b_r': _L2_gnn_in['b_r'], 'L2_gnn_W_e': _L2_gnn_in['W_e'], 'L2_gnn_att': _L2_gnn_in['att'], 'L2_gnn_bias': _L2_gnn_in['bias'], 'L2_gnn_gamma': _L2_gnn_in['gamma'], 'L2_gnn_beta': _L2_gnn_in['beta'], 'L3_gnn_W0': _L3_gnn_in['W0'], 'L3_gnn_Ws0': _L3_gnn_in['Ws0'], 'L3_gnn_b0': _L3_gnn_in['b0'], 'L3_gnn_W1': _L3_gnn_in['W1'], 'L3_gnn_Ws1': _L3_gnn_in['Ws1'], 'L3_gnn_b1': _L3_gnn_in['b1'], 'L3_gnn_W2': _L3_gnn_in['W2'], 'L3_gnn_Ws2': _L3_gnn_in['Ws2'], 'L3_gnn_b2': _L3_gnn_in['b2']}

def reference(x, src, dst, edge_attr_64, edge_type_2, L0_gnn_weight, L0_gnn_bias, L1_gnn_W, L1_gnn_b, L2_gnn_W_l, L2_gnn_b_l, L2_gnn_W_r, L2_gnn_b_r, L2_gnn_W_e, L2_gnn_att, L2_gnn_bias, L2_gnn_gamma, L2_gnn_beta, L3_gnn_W0, L3_gnn_Ws0, L3_gnn_b0, L3_gnn_W1, L3_gnn_Ws1, L3_gnn_b1, L3_gnn_W2, L3_gnn_Ws2, L3_gnn_b2):
    import jax
    import jax.numpy as jnp

    def _L0_gnn_ref(h, norm, weight, bias, src, dst):
        import jax, jax.numpy as jnp
        import numpy as np
        N_NODES = 50000
        N_EDGES = 25000
        IN_FEATS = 64
        OUT_FEATS = 64
        x = jnp.matmul(h, weight)
        x = x * norm
        agg = jax.ops.segment_sum(x[src], dst, num_segments=N_NODES)
        out = agg * norm + bias
        return jax.nn.relu(out)

    def _L1_gnn_ref(x, senders, receivers, W, b):
        import jax, jax.numpy as jnp
        import numpy as np
        N_NODES = 3125
        N_EDGES = 50000
        D_FEAT = 64
        EMB_DIM = 64

        def _norm_by_degree(x, degree):
            return x * jax.lax.rsqrt(jnp.maximum(degree.astype(x.dtype), 1.0))[:, None]
        n = x.shape[0]
        all_nodes = jnp.arange(n, dtype=senders.dtype)
        s = jnp.concatenate([senders, all_nodes])
        r = jnp.concatenate([receivers, all_nodes])
        ones = jnp.ones_like(s)
        deg_s = jax.ops.segment_sum(ones, s, num_segments=n)
        deg_r = jax.ops.segment_sum(ones, r, num_segments=n)
        xn = _norm_by_degree(x, deg_s)
        summed = jax.ops.segment_sum(xn[s], r, num_segments=n)
        mean = summed / jnp.maximum(deg_r.astype(x.dtype), 1.0)[:, None]
        x_updated = _norm_by_degree(mean, deg_r)
        combined = jnp.concatenate([x, x_updated], axis=-1)
        return combined @ W + b

    def _L2_gnn_ref(x, edge_index, edge_attr, W_l, b_l, W_r, b_r, W_e, att, bias, gamma, beta):
        import jax, jax.numpy as jnp
        import numpy as np
        N, E, F, H, ED = (50000, 15625, 64, 4, 64)
        NEG_SLOPE = 0.2
        BN_EPS = 1e-05
        SM_EPS = 1e-16

        def gatv2_layer(x, edge_index, edge_attr, W_l, b_l, W_r, b_r, W_e, att, bias, gamma, beta):
            n = x.shape[0]
            x_l = (x @ W_l + b_l).reshape(n, H, F)
            x_r = (x @ W_r + b_r).reshape(n, H, F)
            src0, dst0 = (edge_index[0], edge_index[1])
            cnt = jax.ops.segment_sum(jnp.ones((edge_attr.shape[0],), x.dtype), dst0, num_segments=n)
            loop_attr = jax.ops.segment_sum(edge_attr, dst0, num_segments=n) / jnp.maximum(cnt, 1.0)[:, None]
            src = jnp.concatenate([src0, jnp.arange(n, dtype=src0.dtype)])
            dst = jnp.concatenate([dst0, jnp.arange(n, dtype=dst0.dtype)])
            ea = jnp.concatenate([edge_attr, loop_attr], axis=0)
            e_emb = (ea @ W_e).reshape(-1, H, F)
            m = jax.nn.leaky_relu(x_l[src] + x_r[dst] + e_emb, NEG_SLOPE)
            alpha = jnp.einsum('ehf,hf->eh', m, att)
            amax = jax.ops.segment_max(alpha, dst, num_segments=n)
            ex = jnp.exp(alpha - amax[dst])
            denom = jax.ops.segment_sum(ex, dst, num_segments=n)
            alpha = ex / (denom[dst] + SM_EPS)
            out = jax.ops.segment_sum(x_l[src] * alpha[..., None], dst, num_segments=n)
            out = out.mean(axis=1) + bias
            mu = out.mean(axis=0)
            var = out.var(axis=0)
            out = gamma * (out - mu) * jax.lax.rsqrt(var + BN_EPS) + beta
            return jax.nn.relu(out)
        return gatv2_layer(x, edge_index, edge_attr, W_l, b_l, W_r, b_r, W_e, att, bias, gamma, beta)

    def _L3_gnn_ref(features, src, dst, etype, W0, Ws0, b0, W1, Ws1, b1, W2, Ws2, b2):
        import jax, jax.numpy as jnp
        import numpy as np
        N_NODES = 3125
        N_EDGES = 31250
        DIM = 64

        def rel_graph_conv(x, src, dst, etype, W, Ws, b, act):
            h = jnp.einsum('nd,rdo->rno', x, W)
            m = jnp.where((etype == 0)[:, None], h[0][src], h[1][src])
            agg = jax.ops.segment_sum(m, dst, num_segments=x.shape[0])
            out = agg + x @ Ws + b
            return act(out) if act is not None else out
        h = rel_graph_conv(features, src, dst, etype, W0, Ws0, b0, jax.nn.relu)
        h = rel_graph_conv(h, src, dst, etype, W1, Ws1, b1, jax.nn.relu)
        h = rel_graph_conv(h, src, dst, etype, W2, Ws2, b2, None)
        return h
    edge_index = jnp.stack([src, dst])
    deg = jnp.maximum(jax.ops.segment_sum(jnp.ones(dst.shape, jnp.float32), dst, num_segments=50000), 1.0)
    deg_isqrt = deg ** (-0.5)
    h = jnp.maximum(_layernorm(x, axis=-1), 0.0)
    x = x + _L0_gnn_ref(h, deg_isqrt[:, None], L0_gnn_weight, L0_gnn_bias, src, dst)
    h = jnp.maximum(_layernorm(x, axis=-1), 0.0)
    x = x + _L1_gnn_ref(h, src, dst, L1_gnn_W, L1_gnn_b)
    h = jnp.maximum(_layernorm(x, axis=-1), 0.0)
    x = x + _L2_gnn_ref(h, edge_index, edge_attr_64, L2_gnn_W_l, L2_gnn_b_l, L2_gnn_W_r, L2_gnn_b_r, L2_gnn_W_e, L2_gnn_att, L2_gnn_bias, L2_gnn_gamma, L2_gnn_beta)
    h = jnp.maximum(_layernorm(x, axis=-1), 0.0)
    x = x + _L3_gnn_ref(h, src, dst, edge_type_2, L3_gnn_W0, L3_gnn_Ws0, L3_gnn_b0, L3_gnn_W1, L3_gnn_Ws1, L3_gnn_b1, L3_gnn_W2, L3_gnn_Ws2, L3_gnn_b2)
    return x

_drawn_inputs = setup_inputs


def setup_inputs(seed=0):
    import zlib

    import numpy as np

    out = dict(_drawn_inputs(seed))
    spreads = {'L1_gnn_b': (0.0, 0.1),
     'L2_gnn_b_l': (0.0, 0.8),
     'L2_gnn_b_r': (0.0, 0.8),
     'L2_gnn_bias': (0.0, 0.8),
     'L2_gnn_gamma': (1.0, 0.2),
     'L2_gnn_beta': (0.0, 0.1),
     'L3_gnn_b0': (0.0, 0.1),
     'L3_gnn_b1': (0.0, 0.1),
     'L3_gnn_b2': (0.0, 0.1)}
    factors = {}
    for name, (base, spread) in spreads.items():
        noise = np.random.default_rng([zlib.crc32(name.encode()), seed]).standard_normal(out[name].shape)
        drawn = base * np.exp(spread * noise) if base else spread * noise
        out[name] = jnp.asarray(drawn.astype(out[name].dtype))
    for name, factor in factors.items():
        out[name] = (out[name] * factor).astype(out[name].dtype)
    return out
```

```python
import concourse.bass as bass
from concourse import mybir
from contextlib import ExitStack

P = 128
F = 64
HEADS = 4
HF = HEADS * F
HS = 7
BODY = 2 * HS
NBLK = 4
NEG = -1.0e30
SKIP = 2 ** 20
LN_EPS = 1e-5
BN_EPS = 1e-5
SM_EPS = 1e-16
SLOPE = 0.2
GATW = HF + 2 * HEADS


def build_gnn(nc, a, out):
    f32, bf16, i32 = mybir.dt.float32, mybir.dt.bfloat16, mybir.dt.int32
    ALU, ACT, AX = mybir.AluOpType, mybir.ActivationFunctionType, mybir.AxisListType

    N = a["x"].shape[0]
    FULL, REM = N // P, N % P
    T = -(-N // (P * 2 * BODY)) * 2 * BODY
    NP = T * P
    R = T // NBLK
    GI = T // BODY
    HI = NP // 256
    assert a["src"].shape[0] == N and HI == 2 * R and R <= P

    def scratch(name, shape, dt=f32):
        return nc.dram_tensor(name, shape, dt, kind="Internal").ap()

    dst_rows = scratch("dst_rows", (NP + P,))
    node_h = scratch("node_h", (NP, F))
    node_g = scratch("node_g", (NP, F))
    edge_h = scratch("edge_h", (NP, F))
    sums_w = scratch("sums_w", (NP, 2 * F))
    sums_n = scratch("sums_n", (NP, F))
    sums_a = scratch("sums_a", (NP, GATW))
    loop_at = scratch("loop_at", (NP, F))
    gat_out = scratch("gat_out", (NP, F))
    ends_d = scratch("ends_d", (HEADS, T, 2))
    ends_k = scratch("ends_k", (T, 2))
    ends_m = scratch("ends_m", (HEADS, T, 2))

    tiles = lambda ap: ap.rearrange("(t p) f -> p t f", p=P)

    ctx = ExitStack()
    with ctx:
        sb = lambda name, shape, dt=f32: ctx.enter_context(nc.sbuf_tensor(name, shape, dt))
        sem = lambda name: ctx.enter_context(nc.semaphore(name))
        bank = [ctx.enter_context(nc.psum_tensor(f"bank{i}", [P, 512], f32)) for i in range(8)]

        ident = sb("ident", [P, P])
        x_sb = sb("x_sb", [P, T, F])
        src_i = sb("src_i", [P, T + BODY], i32)
        dst_i = sb("dst_i", [P, T + BODY], i32)
        put_i = sb("put_i", [P, T], i32)
        dst_f = sb("dst_f", [P, T])
        is_last = sb("is_last", [P, T])
        prev_f = sb("prev_f", [P, T])
        rel = sb("rel", [P, 2, T])
        cnt = sb("cnt", [P, T])
        norm = sb("norm", [P, T])
        rs_send = sb("rs_send", [P, T])
        upd_scale = sb("upd_scale", [P, T])
        inv_cnt = sb("inv_cnt", [P, T])
        no_edge = sb("no_edge", [P, T])
        real = sb("real", [P, T])
        eps = sb("eps", [P, 1])
        alpha = sb("alpha", [P, T, HEADS])
        amax = sb("amax", [P, T, HEADS])

        W0 = sb("W0", [F, F]); b0 = sb("b0", [P, F])
        W1 = sb("W1", [2 * F, F]); b1 = sb("b1", [P, F])
        Wlr = sb("Wlr", [2 * F, HF]); Wea = sb("Wea", [F + 1, HF]); Wself = sb("Wself", [2 * F, HF])
        Wr0 = sb("Wr0", [F, HF]); blr = sb("blr", [1, 3, HF]); brow = sb("brow", [F + 1, 2, HF])
        attb = sb("attb", [P, HF]); Wst = sb("Wst", [P, 2, F]); blb = sb("blb", [P, HF])
        b2 = sb("b2", [P, F]); gamma = sb("gamma", [P, F]); beta = sb("beta", [P, F])
        W3 = sb("W3", [P, 3, F]); Ws3 = sb("Ws3", [F, 3, F]); b3 = sb("b3", [P, 3, F])
        mu = sb("mu", [P, F]); bn_a = sb("bn_a", [P, F])
        ones1 = sb("ones1", [1, P]); onesP = sb("onesP", [P, P]); zeros_w = sb("zeros_w", [P, HS * F])


        def prepare():
            with nc.cleanup_on_exit(), ExitStack() as c, nc.Block() as block:
                tb = lambda name, shape, dt=f32: c.enter_context(nc.sbuf_tensor(name, shape, dt))
                sm = lambda name: nc.alloc_semaphore("pre_" + name)
                BP = NBLK * P
                work = tb("work", [P, max(9 * BP, 8 * T)])
                blocks = lambda lo, n: work[0:R, lo * BP:(lo + n) * BP].rearrange("r (j b p) -> r j b p", b=NBLK, p=P)
                raw = blocks(0, 3).bitcast(i32)
                rows = blocks(3, 4)
                nxt, last = blocks(7, 1)[:, 0], blocks(8, 1)[:, 0]
                row_i = tb("row_i", [P, P], i32); col_i = tb("col_i", [P, 1], i32)
                row_f = tb("row_f", [P, P]); col_f = tb("col_f", [P, 1]); m127 = tb("m127", [P, 2])
                end_row = tb("end_row", [1, P])
                zero = tb("zero", [P, 28 * F])
                digits = lambda buf: buf[:, :, :].rearrange("p t h -> p (t h)").rearrange("p (j t) -> p j t", j=4)
                dig_i, dig = digits(amax).bitcast(i32), digits(alpha)
                iota_i = tb("iota_i", [P, 256], i32); iota_b = tb("iota_b", [P, 256], bf16)
                hi = tb("hi", [P, 2, 2, HS, HI], bf16)
                lo = tb("lo", [P, 2, 2, HS, 256], bf16)
                zb = tb("zb", [P, 512], bf16)
                hist = lo[0:R, 0, :, :, :].rearrange("p j t n -> p (j t n)")[:, 0:2048].bitcast(f32).rearrange("p (j n) -> p j n", j=2)
                cols = lambda lo, n: work[:, lo * T:(lo + n) * T].rearrange("p (j t) -> p j t", t=T)
                deg, sq, tmp = cols(0, 2), cols(2, 3), cols(5, 3)
                filled = sm("filled"); raw_in = sm("raw_in"); floats = sm("floats"); sent = sm("sent")
                dst_out = sm("dst_out"); nxt_in = sm("nxt_in"); put = sm("put"); ident_ok = sm("ident_ok")
                iotas = sm("iotas"); turned = sm("turned"); taken = sm("taken"); w_in = sm("w_in")
                x_in = sm("x_in"); oh = sm("oh"); counted = sm("counted"); hist_ok = sm("hist_ok")
                cleared = sm("cleared"); hist_t = sm("hist_t"); sq_in = sm("sq_in"); sq_out = sm("sq_out")
                zeroed = sm("zeroed"); summed = sm("summed"); w_n = sm("w_n")
                x_parts = [(k * FULL // 4, (k + 1) * FULL // 4) for k in range(4)]
                names = ["src", "dst", "edge_type_2"]
                whole = (N // (R * P))
                rem_rows = (N - whole * R * P) // P

                @block.sync
                def _(sp):
                    sp.wait_ge(filled, 1)
                    n = 0
                    for j, name in enumerate(names):
                        v = a[name]
                        sp.dma_start(raw[:, j, 0:whole, :], v[0:whole * R * P].rearrange("(b r p) -> r b p", r=R, p=P)).then_inc(raw_in, 16)
                        at = whole * R * P
                        if rem_rows:
                            sp.dma_start(raw[0:rem_rows, j, whole, :], v[at:at + rem_rows * P].rearrange("(r p) -> r p", p=P)).then_inc(raw_in, 16)
                            n += 1
                        if REM:
                            sp.dma_start(raw[rem_rows:rem_rows + 1, j, whole, 0:REM], v[FULL * P:N].rearrange("(o p) -> o p", o=1)).then_inc(raw_in, 16)
                            n += 1
                        n += 1
                    sp.sem_inc(w_n, 1)
                    for lo_t, hi_t in x_parts:
                        sp.dma_start(x_sb[:, lo_t:hi_t, :], tiles(a["x"][lo_t * P:hi_t * P, :])).then_inc(x_in, 16)
                    if REM:
                        sp.dma_start(x_sb[0:REM, FULL, :], a["x"][FULL * P:N, :]).then_inc(x_in, 16)
                    sp.wait_ge(floats, 1)
                    sp.dma_start(dst_rows[0:NP].rearrange("(b r p) -> r b p", r=R, p=P), rows[:, 1, :, :]).then_inc(dst_out, 16)
                    sp.dma_start(dst_rows[NP:NP + P].rearrange("(o p) -> o p", o=1), end_row[:, :]).then_inc(dst_out, 16)
                    sp.wait_ge(dst_out, 32)
                    sp.dma_start(nxt[:, :, :], dst_rows[1:NP + 1].rearrange("(b r p) -> r b p", r=R, p=P)).then_inc(nxt_in, 16)
                    wide = sums_w.rearrange("(g p r) f -> g p (r f)", p=P, r=14)
                    for g in range(wide.shape[0]):
                        sp.dma_start(wide[g], zero[:, 0:14 * 2 * F]).then_inc(zeroed, 16)
                    narrow = sums_n.rearrange("(g p r) f -> g p (r f)", p=P, r=28)
                    for g in range(narrow.shape[0]):
                        sp.dma_start(narrow[g], zero[:, 0:28 * F]).then_inc(zeroed, 16)
                    sp.wait_ge(zeroed, 16 * (wide.shape[0] + narrow.shape[0]))
                    sp.wait_ge(x_in, 16 * (len(x_parts) + (1 if REM else 0)))

                n_raw = 3 * (1 + (1 if rem_rows else 0) + (1 if REM else 0))

                @block.scalar
                def _(act):
                    bc = lambda v: v.rearrange("(o f) -> o f", o=1).to_broadcast((P, v.shape[0]))
                    att = a["L2_gnn_att"].rearrange("h f -> (h f)")
                    wl = a["L2_gnn_W_l"]
                    loads = [
                        (W0[:, :], a["L0_gnn_weight"]), (b0[:, :], bc(a["L0_gnn_bias"])),
                        (W1[:, :], a["L1_gnn_W"]), (b1[:, :], bc(a["L1_gnn_b"])),
                        (Wlr[0:F, :], wl), (Wlr[F:2 * F, :], a["L2_gnn_W_r"]), (Wr0[:, :], a["L2_gnn_W_r"]),
                        (Wea[0:F, :], a["L2_gnn_W_e"]), (Wself[0:F, :], wl), (Wself[F:2 * F, :], a["L2_gnn_W_e"]),
                        (blr[:, 0, :], a["L2_gnn_b_l"].rearrange("(o f) -> o f", o=1)),
                        (blr[:, 1, :], a["L2_gnn_b_r"].rearrange("(o f) -> o f", o=1)),
                        (brow[F:F + 1, 0, :], a["L2_gnn_b_l"].rearrange("(o f) -> o f", o=1)),
                        (brow[F:F + 1, 1, :], a["L2_gnn_b_r"].rearrange("(o f) -> o f", o=1)),
                        (attb[:, :], bc(att)), (blb[:, :], bc(a["L2_gnn_b_l"])),
                        (b2[:, :], bc(a["L2_gnn_bias"])), (gamma[:, :], bc(a["L2_gnn_gamma"])), (beta[:, :], bc(a["L2_gnn_beta"])),
                    ]
                    for h in range(HEADS):
                        loads.append((Wst[(h % 2) * F:(h % 2 + 1) * F, h // 2, :], wl[:, h * F:(h + 1) * F]))
                    for k in range(3):
                        loads.append((W3[:, k, :], a[f"L3_gnn_W{k}"].rearrange("r d o -> (r d) o")))
                        loads.append((Ws3[:, k, :], a[f"L3_gnn_Ws{k}"]))
                        loads.append((b3[:, k, :], bc(a[f"L3_gnn_b{k}"])))
                    for to, of in loads:
                        act.dma_start(to, of).then_inc(w_in, 16)
                    act.wait_ge(w_in, 16 * len(loads))
                    act.sem_inc(w_n, 1)
                    act.wait_ge(sq_in, 1)
                    nc.scalar.activation(sq[:, :, :], tmp[:, :, :], ACT.Sqrt).then_inc(sq_out, 1)

                @block.gpsimd
                def _(pool):
                    nc.gpsimd.iota(row_i[:, :], pattern=[[1, P]], base=0, channel_multiplier=0)
                    nc.gpsimd.iota(col_i[:, :], pattern=[[0, 1]], base=0, channel_multiplier=1)
                    nc.gpsimd.iota(iota_i[:, :], pattern=[[1, 256]], base=0, channel_multiplier=0).then_inc(iotas, 1)

                @block.vector
                def _(dve):
                    v = nc.vector
                    for j in range(2):
                        v.memset(raw[:, j, :, :], NP - 1)
                    v.memset(raw[:, 2, :, :], 0)
                    v.memset(x_sb[:, FULL:T, :], 0.0)
                    v.memset(end_row[:, :], float(NP))
                    v.memset(src_i[:, T:], 0)
                    v.memset(dst_i[:, T:], 0)
                    v.memset(eps[:, :], LN_EPS)
                    v.memset(ones1[:, :], 1.0)
                    v.memset(onesP[:, :], 1.0)
                    v.memset(zero[:, :], 0.0)
                    v.memset(zeros_w[:, :], 0.0)
                    v.memset(zb[:, :], 0.0).then_inc(filled, 1)
                    dve.wait_ge(iotas, 1)
                    v.tensor_copy(row_f[:, :], row_i[:, :])
                    v.tensor_copy(col_f[:, :], col_i[:, :])
                    v.tensor_copy(iota_b[:, :], iota_i[:, :])
                    v.drain()
                    v.tensor_scalar(ident[:, :], row_f[:, :], col_f[:, 0:1], None, ALU.is_equal).then_inc(ident_ok, 1)
                    v.tensor_scalar(m127[:, 0:1], col_f[:, :], float(P - 1), None, ALU.is_equal)
                    v.tensor_scalar(m127[:, 1:2], col_f[:, :], float(P - 1), -1.0, ALU.not_equal, ALU.mult)
                    dve.wait_ge(raw_in, 16 * n_raw)
                    v.tensor_copy(rows[:, 0:3, :, :].rearrange("r j b p -> r (j b p)"), raw[:, :, :, :].rearrange("r j b p -> r (j b p)")).then_inc(floats, 1)
                    dve.wait_ge(nxt_in, 16)
                    v.tensor_tensor(last[:, :, :], rows[:, 1, :, :], nxt[:, :, :], ALU.is_equal)
                    v.drain()
                    v.scalar_tensor_tensor(rows[:, 3, :, :], last[:, :, :], float(SKIP), rows[:, 1, :, :], ALU.mult, ALU.add).then_inc(put, 1)
                    dve.wait_ge(turned, 1)
                    v.tensor_copy(src_i[:, 0:T], bank[0][:, 0:T])
                    v.tensor_copy(dst_f[:, :], bank[1][:, 0:T])
                    v.tensor_copy(dst_i[:, 0:T], bank[1][:, 0:T])
                    v.tensor_scalar(rel[:, 0, :], bank[2][:, 0:T], 0.0, None, ALU.is_equal)
                    v.tensor_scalar(rel[:, 1, :], bank[2][:, 0:T], 0.0, None, ALU.not_equal)
                    v.tensor_copy(put_i[:, :], bank[3][:, 0:T])
                    v.tensor_scalar(is_last[:, :], bank[3][:, 0:T], float(SKIP), None, ALU.is_lt)
                    v.drain()
                    v.memset(prev_f[:, 0:1], -1.0)
                    v.tensor_scalar(prev_f[:, 1:T], dst_f[:, 0:T - 1], m127[:, 0:1], m127[:, 1:2], ALU.mult, ALU.add)
                    for j, idx in enumerate((src_i, dst_i)):
                        v.tensor_scalar(dig_i[:, 2 * j, :], idx[:, 0:T], 8, None, ALU.arith_shift_right)
                        v.tensor_scalar(dig_i[:, 2 * j + 1, :], idx[:, 0:T], 255, None, ALU.bitwise_and)
                    v.drain()
                    v.tensor_copy(dig[:, :, :], dig_i[:, :, :])
                    v.memset(real[:, 0:FULL], 1.0)
                    v.memset(real[:, FULL:T], 0.0)
                    v.drain()
                    if REM:
                        v.memset(real[0:REM, FULL:FULL + 1], 1.0)
                    v.drain()
                    v.sem_inc(cleared, 1)

                    def body(i, first):
                        for s in range(2):
                            if not first:
                                dve.wait_ge(counted, 2 * i + s - 1)
                            for t in range(HS):
                                for j in range(2):
                                    g = i * BODY + s * HS + t
                                    v.tensor_scalar(hi[:, s, j, t, :], iota_b[:, 0:HI], dig[:, 2 * j, bass.ds(g, 1)], None, ALU.is_equal)
                                    ins = v.tensor_scalar(lo[:, s, j, t, :], iota_b[:, :], dig[:, 2 * j + 1, bass.ds(g, 1)], None, ALU.is_equal)
                            ins.then_inc(oh, 1)
                    body(0, True)
                    with v.Fori(1, GI) as i:
                        body(i, False)
                    dve.wait_ge(summed, 1)
                    for j in range(2):
                        ins = v.tensor_copy(hist[:, j, :], bank[4 + j][0:R, :])
                    ins.then_inc(hist_ok, 1)
                    dve.wait_ge(hist_t, 1)
                    for j in range(2):
                        for k in range(2):
                            for half in range(2):
                                d0 = deg[:, j, :].rearrange("p (k r h) -> p k r h", k=2, h=2)[:, k, :, half]
                                v.tensor_copy(d0, bank[j][:, (2 * k + half) * R:(2 * k + half + 1) * R])
                    v.drain()
                    v.tensor_copy(cnt[:, :], deg[:, 1, :])
                    v.tensor_scalar(tmp[:, 0, :], deg[:, 1, :], 1.0, None, ALU.max)
                    v.tensor_scalar(tmp[:, 1, :], deg[:, 0, :], 1.0, None, ALU.add)
                    v.tensor_scalar(tmp[:, 2, :], deg[:, 1, :], 1.0, None, ALU.add)
                    v.tensor_scalar(no_edge[:, :], deg[:, 1, :], 0.0, NEG, ALU.is_equal, ALU.mult)
                    v.drain()
                    v.sem_inc(sq_in, 1)
                    v.reciprocal(inv_cnt[:, :], tmp[:, 0, :])
                    dve.wait_ge(sq_out, 1)
                    v.reciprocal(norm[:, :], sq[:, 0, :])
                    v.reciprocal(rs_send[:, :], sq[:, 1, :])
                    v.tensor_tensor(upd_scale[:, :], sq[:, 2, :], tmp[:, 2, :], ALU.mult)
                    v.drain()
                    v.reciprocal(upd_scale[:, :], upd_scale[:, :])
                    dve.wait_ge(w_n, 2)
                    v.tensor_tensor(Wself[0:F, :], Wself[0:F, :], Wr0[:, :], ALU.add)
                    v.tensor_tensor(blr[:, 2, :], blr[:, 0, :], blr[:, 1, :], ALU.add)
                    v.tensor_tensor(Wea[F:F + 1, :], brow[F:F + 1, 0, :], brow[F:F + 1, 1, :], ALU.add)
                    v.tensor_reduce(mu[:, :], blb[:, :].rearrange("p (h o) -> p o h", h=HEADS), AX.X, ALU.add)
                    v.drain()
                    v.scalar_tensor_tensor(b2[:, :], mu[:, :], 1.0 / HEADS, b2[:, :], ALU.mult, ALU.add)

                @block.tensor
                def _(pe):
                    pe.wait_ge(ident_ok, 1)
                    pe.wait_ge(floats, 1)
                    pe.wait_ge(put, 1)
                    for j in range(4):
                        for b in range(NBLK):
                            ins = nc.tensor.transpose(bank[j][:, b * R:(b + 1) * R], rows[:, j, b, :], ident[0:R, 0:R])
                    ins.then_inc(turned, 1)
                    pe.wait_ge(cleared, 1)
                    for j in range(2):
                        nc.tensor.matmul(bank[4 + j][0:R, :], zb[:, 0:R], zb[:, :], start=True, stop=False)

                    def body(i, first):
                        for s in range(2):
                            pe.wait_ge(oh, 2 * i + s + 1)
                            for t in range(HS):
                                for j in range(2):
                                    for k in range(2):
                                        ins = nc.tensor.matmul(bank[4 + j][0:R, k * 256:(k + 1) * 256], hi[:, s, j, t, k * R:(k + 1) * R],
                                                               lo[:, s, j, t, :], start=False, stop=False)
                            ins.then_inc(counted, 1)
                    with nc.tensor.Fori(0, GI) as i:
                        body(i, False)
                    for j in range(2):
                        ins = nc.tensor.matmul(bank[4 + j][0:R, :], zb[:, 0:R], zb[:, :], start=False, stop=True)
                    ins.then_inc(summed, 1)
                    pe.wait_ge(hist_ok, 1)
                    for j in range(2):
                        for k in range(2):
                            for half in range(2):
                                ins = nc.tensor.transpose(bank[j][:, (2 * k + half) * R:(2 * k + half + 1) * R],
                                                          hist[:, j, k * 256 + half * P:k * 256 + (half + 1) * P], ident[0:R, 0:R])
                    ins.then_inc(hist_t, 1)

        def edge_sums(tag, kind, W, sums):
            with nc.cleanup_on_exit(), ExitStack() as c, nc.Block() as block:
                tb = lambda name, shape, dt=f32: c.enter_context(nc.sbuf_tensor(tag + name, shape, dt))
                sm = lambda name: nc.alloc_semaphore(tag + name)
                two = lambda name: [sm(f"{name}{s}") for s in range(2)]
                drow = tb("drow", [P, 2, HS, P])
                same = tb("same", [P, 2, HS, P]); carry = tb("carry", [P, 2, HS, P])
                got = tb("got", [P, 2, HS, F]) if kind in ("typed", "gat") else None
                msg = tb("msg", [P, 2, HS, W])
                tot = tb("tot", [P, 2, HS, W])
                src_st = tb("src_st", [P, 2, HS], i32); put_st = tb("put_st", [P, 2, HS], i32)
                ex = tb("ex", [P, 2, HS, HEADS]) if kind == "gat" else None
                zero = tb("zero", [P, 1848]) if kind == "wide" else None
                rows_in, side_in, gathered, src_ok, put_ok = two("rows_in"), two("side_in"), two("gathered"), two("src_ok"), two("put_ok")
                built, msg_ok, scat = two("built"), two("msg_ok"), two("scat")
                sums_ok, tot_ok, start0, go, exp_in, exp_ok = sm("sums_ok"), sm("tot_ok"), sm("start0"), sm("go"), two("exp_in"), two("exp_ok")
                zeroed = sm("zeroed"); z0 = sm("z0")
                uses_gather = kind != "gat"
                direct = kind in ("wide", "plain")
                gbuf = msg if direct else got
                PER = 16 * HS

                @block.sync
                def _(sp):
                    if kind == "wide":
                        sp.wait_ge(z0, 1)
                        per = 1848 // GATW
                        za = sums_a.rearrange("(g p r) f -> g p (r f)", p=P, r=per)
                        for g in range(za.shape[0]):
                            sp.dma_start(za[g], zero[:, 0:per * GATW]).then_inc(zeroed, 16)

                    def body(i, first, last):
                        for s in range(2):
                            at = i * BODY + s * HS
                            if not first:
                                sp.wait_ge(built[s], i)
                            sp.dma_start(drow[:, s, :, :].rearrange("p t q -> p (t q)"),
                                         dst_rows[bass.ds(at * P, HS * P)].rearrange("(o n) -> o n", o=1).to_broadcast((P, HS * P))).then_inc(rows_in[s], 16)
                            if kind == "wide":
                                if not first:
                                    sp.wait_ge(sums_ok, (i - 1) * BODY + (s + 1) * HS)
                                if not last or (i * BODY + s * HS + HS) <= FULL:
                                    sp.dma_start(msg[:, s, :, F:2 * F], tiles(a["edge_attr_64"][bass.ds(at * P, HS * P), :])).then_inc(side_in[s], 16)
                                else:
                                    n = FULL - at
                                    if n > 0:
                                        sp.dma_start(msg[:, s, 0:n, F:2 * F], tiles(a["edge_attr_64"][at * P:FULL * P, :])).then_inc(side_in[s], 16)
                                    if REM:
                                        sp.dma_start(msg[0:REM, s, n, F:2 * F], a["edge_attr_64"][FULL * P:N, :]).then_inc(side_in[s], 16)
                            if kind == "gat":
                                if not first:
                                    sp.wait_ge(msg_ok[s], i)
                                sp.dma_start(got[:, s, :, :], tiles(edge_h[bass.ds(at * P, HS * P), :])).then_inc(side_in[s], 16)
                    body(0, True, False)
                    with nc.sync.Fori(1, GI - 1) as i:
                        body(i, False, False)
                    body(GI - 1, False, True)
                    if kind == "wide":
                        sp.wait_ge(zeroed, 16 * (NP // P // (1848 // GATW)))

                def side_total(i, s, last):
                    if last and kind == "wide" and (i * BODY + s * HS + HS) > FULL:
                        n = FULL - (i * BODY + s * HS)
                        return 16 * i + 16 * ((1 if n > 0 else 0) + (1 if REM else 0))
                    return 16 * (i + 1)

                @block.gpsimd
                def _(pool):
                    def gather(i, s, first):
                        pool.wait_ge(src_ok[s], i + 1)
                        if not first:
                            if direct:
                                pool.wait_ge(sums_ok, (i - 1) * BODY + (s + 1) * HS)
                            else:
                                pool.wait_ge(msg_ok[s], i)
                        pool.sem_inc(go, 1)
                        for t in range(HS):
                            pool.indirect_dma_start(out=gbuf[:, s, t, 0:F], out_offset=None, in_=node_g,
                                                    in_offset=bass.IndirectOffsetOnAxis(ap=src_st[:, s, t:t + 1], axis=0)).then_inc(gathered[s], 16)

                    def scatter(i, s):
                        pool.wait_ge(put_ok[s], i + 1)
                        pool.wait_ge(tot_ok, i * BODY + (s + 1) * HS)
                        pool.sem_inc(go, 1)
                        for t in range(HS):
                            pool.indirect_dma_start(out=sums, out_offset=bass.IndirectOffsetOnAxis(ap=put_st[:, s, t:t + 1], axis=0),
                                                    in_=tot[:, s, t, :], in_offset=None, bounds_check=NP - 1, oob_is_err=False).then_inc(scat[s], 16)

                    def body(i, first, last):
                        if uses_gather:
                            gather(i, 1, first)
                        scatter(i, 0)
                        if uses_gather and not last:
                            gather(i + 1, 0, False)
                        scatter(i, 1)
                    if uses_gather:
                        gather(0, 0, True)
                    body(0, True, False)
                    with nc.gpsimd.Fori(1, GI - 1) as i:
                        body(i, False, False)
                    body(GI - 1, False, True)
                    for s in range(2):
                        pool.wait_ge(scat[s], PER * GI)

                @block.vector
                def _(dve):
                    v = nc.vector
                    if kind == "wide":
                        v.memset(zero[:, :], 0.0).then_inc(z0, 1)
                    v.memset(tot[:, 1, HS - 1, :], 0.0)
                    v.drain()
                    v.sem_inc(start0, 1)
                    if uses_gather:
                        for s in range(2):
                            v.tensor_copy(src_st[:, s, :], src_i[:, s * HS:(s + 1) * HS]).then_inc(src_ok[s], 1)

                    def body(i, first):
                        for s in range(2):
                            at = i * BODY + s * HS
                            dve.wait_ge(rows_in[s], 16 * (i + 1))
                            if not first:
                                dve.wait_ge(sums_ok, (i - 1) * BODY + (s + 1) * HS)
                            v.tensor_tensor(same[:, s, :, :], drow[:, s, :, :], dst_f[:, bass.ds(at, HS)].unsqueeze(2).to_broadcast((P, HS, P)), ALU.is_equal)
                            v.tensor_tensor(carry[:, s, :, :], drow[:, s, :, :], prev_f[:, bass.ds(at, HS)].unsqueeze(2).to_broadcast((P, HS, P)), ALU.is_equal).then_inc(built[s], 1)
                            if not first:
                                dve.wait_ge(scat[s], PER * i)
                                dve.wait_ge(start0, 1)
                            v.tensor_copy(put_st[:, s, :], put_i[:, bass.ds(at, HS)]).then_inc(put_ok[s], 1)
                            if kind == "typed":
                                dve.wait_ge(gathered[s], PER * (i + 1))
                                for r in range(2):
                                    ins = v.tensor_tensor(msg[:, s, :, r * F:(r + 1) * F], got[:, s, :, :],
                                                          rel[:, r, bass.ds(at, HS)].unsqueeze(2).to_broadcast((P, HS, F)), ALU.mult)
                                ins.then_inc(msg_ok[s], 1)
                            if kind == "gat":
                                v.tensor_tensor(ex[:, s, :, :], alpha[:, bass.ds(at, HS), :], amax[:, bass.ds(at, HS), :], ALU.subtract).then_inc(exp_in[s], 1)
                                v.tensor_tensor(msg[:, s, :, HF + HEADS:GATW], amax[:, bass.ds(at, HS), :],
                                                is_last[:, bass.ds(at, HS)].unsqueeze(2).to_broadcast((P, HS, HEADS)), ALU.mult)
                                dve.wait_ge(exp_ok[s], i + 1)
                                v.tensor_copy(msg[:, s, :, HF:HF + HEADS], ex[:, s, :, :])
                                dve.wait_ge(side_in[s], 16 * (i + 1))
                                for h in range(HEADS):
                                    ins = v.tensor_tensor(msg[:, s, :, h * F:(h + 1) * F], got[:, s, :, :],
                                                          ex[:, s, :, h:h + 1].to_broadcast((P, HS, F)), ALU.mult)
                                ins.then_inc(msg_ok[s], 1)
                            if uses_gather:
                                dve.wait_ge(gathered[s], PER * (i + 1))
                                dve.wait_ge(start0, 1)
                                v.tensor_copy(src_st[:, s, :], src_i[:, bass.ds(at + BODY, HS)]).then_inc(src_ok[s], 1)
                    body(0, True)
                    with v.Fori(1, GI) as i:
                        body(i, False)

                @block.tensor
                def _(pe):
                    pe.wait_ge(start0, 1)

                    def tile_sums(i, s, t, first):
                        k = i * BODY + s * HS + t
                        if not (first and s == 0):
                            pe.wait_ge(tot_ok, k - HS + 1)
                        nc.tensor.matmul(bank[t][:, 0:W], same[:, s, t, :], msg[:, s, t, :], start=True, stop=False)

                    def tile_carry(i, s, t, first):
                        k = i * BODY + s * HS + t
                        if not (first and s == 0 and t == 0):
                            pe.wait_ge(tot_ok, k)
                        prev = tot[:, s, t - 1, :] if t else tot[:, 1 - s, HS - 1, :]
                        nc.tensor.matmul(bank[t][:, 0:W], carry[:, s, t, :], prev, start=False, stop=True).then_inc(sums_ok, 1)

                    def body(i, first, last):
                        for s in range(2):
                            pe.wait_ge(built[s], i + 1)
                            if direct:
                                pe.wait_ge(gathered[s], PER * (i + 1))
                            if kind == "wide":
                                pe.wait_ge(side_in[s], side_total(i, s, last))
                            if not direct:
                                pe.wait_ge(msg_ok[s], i + 1)
                            tile_sums(i, s, 0, first)
                            for t in range(HS):
                                if t + 1 < HS:
                                    tile_sums(i, s, t + 1, first)
                                tile_carry(i, s, t, first)
                    body(0, True, False)
                    with nc.tensor.Fori(1, GI - 1) as i:
                        body(i, False, False)
                    body(GI - 1, False, True)

                @block.scalar
                def _(act):
                    act.wait_ge(start0, 1)

                    def body(i, first):
                        for s in range(2):
                            if kind == "gat":
                                act.wait_ge(exp_in[s], i + 1)
                                nc.scalar.activation(ex[:, s, :, :], ex[:, s, :, :], ACT.Exp).then_inc(exp_ok[s], 1)
                            if not first:
                                act.wait_ge(scat[s], PER * i)
                            for t in range(HS):
                                act.wait_ge(sums_ok, i * BODY + s * HS + t + 1)
                                nc.scalar.copy(tot[:, s, t, :], bank[t][:, 0:W]).then_inc(tot_ok, 1)
                    body(0, True)
                    with nc.scalar.Fori(1, GI) as i:
                        body(i, False)

        def nodes(tag, kind, layer=0):
            with nc.cleanup_on_exit(), ExitStack() as c, nc.Block() as block:
                tb = lambda name, shape, dt=f32: c.enter_context(nc.sbuf_tensor(tag + name, shape, dt))
                sm = lambda name: nc.alloc_semaphore(tag + name)
                two = lambda name: [sm(f"{name}{s}") for s in range(2)]
                adds = kind in ("conv", "sage", "bn")
                norms = kind in ("start", "conv", "sage", "bn")
                turn = {"conv": F, "sage": 2 * F, "rel": 2 * F}.get(kind, 0)
                inp = tb("inp", [P, 2, HS, turn or F])
                inp2 = tb("inp2", [P, 2, HS, F])
                inpT = tb("inpT", [P, 2, HS, P]); inp2T = tb("inp2T", [F, 2, HS, P])
                o = tb("o", [P, 2, HS, F])
                xc = tb("xc", [P, 2, HS, F]); sq = tb("sq", [P, 2, HS, F])
                st = tb("st", [P, 2, 4, HS])
                h = tb("h", [P, 2, HS, F]); g = tb("g", [P, 2, HS, F])
                loaded, tin, turned, tout = two("loaded"), two("tin"), two("turned"), two("tout")
                prod, xc_ok, sq_ok, var_ok, sd_ok, z_ok, h_ok, g_ok, stored = (two(n) for n in ("prod", "xc_ok", "sq_ok", "var_ok", "sd_ok", "z_ok", "h_ok", "g_ok", "stored"))
                used, o_free, go = two("used"), two("o_free"), sm("go")
                scaled = {"start": norm, "conv": rs_send}.get(kind)
                n_in = {"start": 0, "conv": 1, "sage": 3, "bn": 1, "rel": 2}[kind]
                n_out = 2 if kind == "conv" else 1
                final = kind == "rel" and layer == 2
                CH = [(0, 4), (4, HS)]

                @block.sync
                def _(sp):
                    def body(i, first):
                        for s in range(2):
                            at = bass.ds((i * BODY + s * HS) * P, HS * P)
                            if not first and n_in:
                                sp.wait_ge(used[s], i)
                            if kind == "conv":
                                sp.dma_start(inp[:, s, :, :], tiles(sums_w[at, 0:F])).then_inc(loaded[s], 16)
                            if kind == "sage":
                                sp.dma_start(inp[:, s, :, 0:F], tiles(node_h[at, :])).then_inc(loaded[s], 16)
                                sp.dma_start(inp[:, s, :, F:2 * F], tiles(sums_n[at, :])).then_inc(loaded[s], 16)
                                sp.dma_start(inp2[:, s, :, :], tiles(node_g[at, :])).then_inc(loaded[s], 16)
                            if kind == "bn":
                                sp.dma_start(inp2[:, s, :, :], tiles(gat_out[at, :])).then_inc(loaded[s], 16)
                            if kind == "rel":
                                sp.dma_start(inp[:, s, :, :], tiles(sums_w[at, :])).then_inc(loaded[s], 16)
                                sp.dma_start(inp2[:, s, :, :], tiles(node_g[at, :])).then_inc(loaded[s], 16)
                    if n_in:
                        body(0, True)
                        with nc.sync.Fori(1, GI) as i:
                            body(i, False)

                @block.gpsimd
                def _(pool):
                    pool.drain()
                    def body(i, first):
                        for s in range(2):
                            at = bass.ds((i * BODY + s * HS) * P, HS * P)
                            tl = bass.ds(i * BODY + s * HS, HS)
                            pool.wait_ge(h_ok[s], i + 1)
                            if scaled is not None:
                                pool.wait_ge(g_ok[s], i + 1)
                            pool.sem_inc(go, 1)
                            if kind == "conv":
                                pool.dma_start(tiles(node_h[at, :]), h[:, s, :, :]).then_inc(stored[s], 16)
                            if scaled is not None:
                                pool.dma_start(tiles(node_g[at, :]), g[:, s, :, :]).then_inc(stored[s], 16)
                            else:
                                pool.dma_start(tiles(node_g[at, :]), h[:, s, :, :]).then_inc(stored[s], 16)
                    if not final:
                        body(0, True)
                        with nc.gpsimd.Fori(1, GI) as i:
                            body(i, False)
                        for s in range(2):
                            pool.wait_ge(stored[s], 16 * n_out * GI)
                    else:
                        def tail(i, last):
                            for s in range(2):
                                at = i * BODY + s * HS
                                pool.wait_ge(h_ok[s], i + 1)
                                pool.sem_inc(go, 1)
                                if not last or at + HS <= FULL:
                                    pool.dma_start(tiles(out[bass.ds(at * P, HS * P), :]), h[:, s, :, :]).then_inc(stored[s], 16)
                                else:
                                    n = FULL - at
                                    if n > 0:
                                        pool.dma_start(tiles(out[at * P:FULL * P, :]), h[:, s, 0:n, :]).then_inc(stored[s], 16)
                                    if REM:
                                        pool.dma_start(out[FULL * P:N, :], h[0:REM, s, n, :]).then_inc(stored[s], 16)
                        with nc.gpsimd.Fori(0, GI - 1) as i:
                            tail(i, False)
                        tail(GI - 1, True)
                        for s in range(2):
                            at = (GI - 1) * BODY + s * HS
                            extra = 1 if at + HS <= FULL else (1 if FULL > at else 0) + (1 if REM else 0)
                            pool.wait_ge(stored[s], 16 * (GI - 1 + extra))

                @block.tensor
                def _(pe):
                    if not turn:
                        return
                    W = {"conv": W0[:, :], "sage": W1[:, :], "rel": W3[:, layer, :]}[kind]

                    def body(i, first):
                        for s in range(2):
                            pe.wait_ge(loaded[s], 16 * n_in * (i + 1))
                            if kind == "sage":
                                pe.wait_ge(tin[s], i + 1)
                            if not (first and s == 0):
                                pe.wait_ge(tout[1 - s], i + s)
                            pe.sem_inc(go, 1)
                            for b, (t0, t1) in enumerate(CH):
                                for t in range(t0, t1):
                                    ins = nc.tensor.transpose(bank[b][0:turn, (t - t0) * P:(t - t0 + 1) * P], inp[:, s, t, :], ident[:, :])
                            if kind == "rel":
                                for b, (t0, t1) in enumerate(CH):
                                    for t in range(t0, t1):
                                        ins = nc.tensor.transpose(bank[2 + b][0:F, (t - t0) * P:(t - t0 + 1) * P], inp2[:, s, t, :], ident[:, :])
                            ins.then_inc(turned[s], 1)
                            pe.wait_ge(tout[s], i + 1)
                            if not first:
                                pe.wait_ge(o_free[s], i)
                            for t in range(HS):
                                ins = nc.tensor.matmul(bank[4 + s][:, t * F:(t + 1) * F], inpT[0:turn, s, t, :], W, start=True, stop=kind != "rel")
                                if kind == "rel":
                                    ins = nc.tensor.matmul(bank[4 + s][:, t * F:(t + 1) * F], inp2T[:, s, t, :], Ws3[:, layer, :], start=False, stop=True)
                            ins.then_inc(prod[s], 1)
                    body(0, True)
                    with nc.tensor.Fori(1, GI) as i:
                        body(i, False)

                @block.scalar
                def _(act):
                    A = nc.scalar

                    def body(i, first):
                        if turn:
                            for s in range(2):
                                act.wait_ge(turned[s], i + 1)
                                if not first:
                                    act.wait_ge(prod[s], i)
                                for b, (t0, t1) in enumerate(CH):
                                    ins = A.copy(inpT[0:turn, s, t0:t1, :].rearrange("p t q -> p (t q)"), bank[b][0:turn, 0:(t1 - t0) * P])
                                    if kind == "rel":
                                        ins = A.copy(inp2T[:, s, t0:t1, :].rearrange("p t q -> p (t q)"), bank[2 + b][0:F, 0:(t1 - t0) * P])
                                ins.then_inc(tout[s], 1)
                        if norms:
                            for s in range(2):
                                act.wait_ge(xc_ok[s], i + 1)
                                A.activation(sq[:, s, :, :], xc[:, s, :, :], ACT.Square).then_inc(sq_ok[s], 1)
                            for s in range(2):
                                act.wait_ge(var_ok[s], i + 1)
                                A.activation(st[:, s, 2, :], st[:, s, 1, :], ACT.Sqrt, bias=eps[:, 0:1], scale=1.0 / F).then_inc(sd_ok[s], 1)
                        for s in range(2):
                            act.wait_ge(z_ok[s], i + 1)
                            if not first:
                                act.wait_ge(stored[s], 16 * n_out * i)
                            A.activation(h[:, s, :, :], xc[:, s, :, :], ACT.Copy if final else ACT.Relu).then_inc(h_ok[s], 1)
                    body(0, True)
                    with A.Fori(1, GI) as i:
                        body(i, False)

                @block.vector
                def _(dve):
                    v = nc.vector

                    def body(i, first):
                        tl = [bass.ds(i * BODY + s * HS, HS) for s in range(2)]
                        wide = lambda ap: ap.unsqueeze(2).to_broadcast((P, HS, F))
                        rowb = lambda ap: ap.unsqueeze(1).to_broadcast((P, HS, F))
                        if kind == "sage":
                            for s in range(2):
                                dve.wait_ge(loaded[s], 16 * n_in * (i + 1))
                                v.tensor_tensor(inp2[:, s, :, :], inp2[:, s, :, :], inp[:, s, :, F:2 * F], ALU.add)
                            v.drain()
                            for s in range(2):
                                v.tensor_tensor(inp[:, s, :, F:2 * F], inp2[:, s, :, :], wide(upd_scale[:, tl[s]]), ALU.mult).then_inc(tin[s], 1)
                        po = [bank[4 + s][:, 0:HS * F].rearrange("p (t f) -> p t f", t=HS) for s in range(2)]
                        if kind == "conv":
                            for s in range(2):
                                dve.wait_ge(prod[s], i + 1)
                                v.tensor_tensor(o[:, s, :, :], po[s], wide(norm[:, tl[s]]), ALU.mult).then_inc(o_free[s], 1)
                            v.drain()
                            for s in range(2):
                                v.tensor_tensor(o[:, s, :, :], o[:, s, :, :], rowb(b0[:, :]), ALU.add)
                            v.drain()
                            for s in range(2):
                                v.scalar_tensor_tensor(x_sb[:, tl[s], :], o[:, s, :, :], 0.0, x_sb[:, tl[s], :], ALU.max, ALU.add).then_inc(used[s], 1)
                            v.drain()
                        if kind == "sage":
                            for s in range(2):
                                dve.wait_ge(prod[s], i + 1)
                                v.tensor_tensor(o[:, s, :, :], po[s], rowb(b1[:, :]), ALU.add).then_inc(o_free[s], 1)
                            v.drain()
                            for s in range(2):
                                v.tensor_tensor(x_sb[:, tl[s], :], o[:, s, :, :], x_sb[:, tl[s], :], ALU.add).then_inc(used[s], 1)
                            v.drain()
                        if kind == "rel":
                            for s in range(2):
                                dve.wait_ge(prod[s], i + 1)
                                if not first:
                                    dve.wait_ge(h_ok[s], i)
                                v.tensor_tensor(o[:, s, :, :] if final else xc[:, s, :, :], po[s], rowb(b3[:, layer, :]), ALU.add).then_inc(o_free[s], 1)
                            v.drain()
                            for s in range(2):
                                if final:
                                    v.tensor_tensor(xc[:, s, :, :], o[:, s, :, :], x_sb[:, tl[s], :], ALU.add).then_inc(z_ok[s], 1)
                                else:
                                    v.sem_inc(z_ok[s], 1)
                                v.sem_inc(used[s], 1)
                            return
                        if kind == "bn":
                            for s in range(2):
                                dve.wait_ge(loaded[s], 16 * n_in * (i + 1))
                                v.tensor_tensor(o[:, s, :, :], inp2[:, s, :, :], rowb(mu[:, :]), ALU.subtract).then_inc(used[s], 1)
                            v.drain()
                            for s in range(2):
                                v.tensor_tensor(o[:, s, :, :], o[:, s, :, :], rowb(bn_a[:, :]), ALU.mult)
                            v.drain()
                            for s in range(2):
                                v.tensor_tensor(o[:, s, :, :], o[:, s, :, :], rowb(beta[:, :]), ALU.add)
                            v.drain()
                            for s in range(2):
                                v.scalar_tensor_tensor(x_sb[:, tl[s], :], o[:, s, :, :], 0.0, x_sb[:, tl[s], :], ALU.max, ALU.add)
                            v.drain()
                        for s in range(2):
                            v.tensor_reduce(st[:, s, 0, :], x_sb[:, tl[s], :], AX.X, ALU.add)
                        v.drain()
                        for s in range(2):
                            if not first:
                                dve.wait_ge(h_ok[s], i)
                            v.scalar_tensor_tensor(xc[:, s, :, :], wide(st[:, s, 0, :]), -1.0 / F, x_sb[:, tl[s], :], ALU.mult, ALU.add).then_inc(xc_ok[s], 1)
                        for s in range(2):
                            dve.wait_ge(sq_ok[s], i + 1)
                            v.tensor_reduce(st[:, s, 1, :], sq[:, s, :, :], AX.X, ALU.add).then_inc(var_ok[s], 1)
                        for s in range(2):
                            dve.wait_ge(sd_ok[s], i + 1)
                            v.reciprocal(st[:, s, 3, :], st[:, s, 2, :])
                        v.drain()
                        for s in range(2):
                            v.tensor_tensor(xc[:, s, :, :], xc[:, s, :, :], wide(st[:, s, 3, :]), ALU.mult).then_inc(z_ok[s], 1)
                        if scaled is not None:
                            for s in range(2):
                                dve.wait_ge(h_ok[s], i + 1)
                                if not first:
                                    dve.wait_ge(stored[s], 16 * n_out * i)
                                v.tensor_tensor(g[:, s, :, :], h[:, s, :, :], wide(scaled[:, tl[s]]), ALU.mult).then_inc(g_ok[s], 1)
                    body(0, True)
                    with v.Fori(1, GI) as i:
                        body(i, False)

        def edge_scores(tag):
            with nc.cleanup_on_exit(), ExitStack() as c, nc.Block() as block:
                tb = lambda name, shape, dt=f32: c.enter_context(nc.sbuf_tensor(tag + name, shape, dt))
                sm = lambda name: nc.alloc_semaphore(tag + name)
                two = lambda name: [sm(f"{name}{s}") for s in range(2)]
                PAIRS, ZB = BODY // 2, 4
                cat = tb("cat", [P, 2, HS, 2 * F]); ea = tb("ea", [P, 2, HS, F])
                catT = tb("catT", [P, 2, P]); eaT = tb("eaT", [F + 1, 2, P])
                y = tb("y", [P, ZB, 2 * HF]); act_z = tb("act_z", [P, 2 * HF]); prod = tb("prod", [P, 2 * HF])
                al = tb("al", [P, BODY, HEADS])
                src_st = tb("src_st", [P, 2, HS], i32); dst_st = tb("dst_st", [P, 2, HS], i32)
                gathered, idx_ok, ea_in, kept = two("gathered"), two("idx_ok"), two("ea_in"), two("kept")
                ones_ok, tr_ok, copied, z_ok, y_ok, z_used, go = (sm(n) for n in ("ones_ok", "tr_ok", "copied", "z_ok", "y_ok", "z_used", "go"))
                PER = 2 * 16 * HS

                def ea_total(i, s, last):
                    n = FULL - (GI - 1) * BODY - s * HS
                    if last and n < HS:
                        return 16 * (GI - 1) + 16 * ((1 if n > 0 else 0) + (1 if REM else 0))
                    return 16 * (i + 1)

                @block.sync
                def _(sp):
                    def body(i, first, last):
                        for s in range(2):
                            at = i * BODY + s * HS
                            if not first:
                                sp.wait_ge(tr_ok, (i - 1) * BODY + (s + 1) * HS)
                            if not last or at + HS <= FULL:
                                sp.dma_start(ea[:, s, :, :], tiles(a["edge_attr_64"][bass.ds(at * P, HS * P), :])).then_inc(ea_in[s], 16)
                            else:
                                n = FULL - at
                                if n > 0:
                                    sp.dma_start(ea[:, s, 0:n, :], tiles(a["edge_attr_64"][at * P:FULL * P, :])).then_inc(ea_in[s], 16)
                                if REM:
                                    sp.dma_start(ea[0:REM, s, n, :], a["edge_attr_64"][FULL * P:N, :]).then_inc(ea_in[s], 16)
                        for s in range(2):
                            sp.wait_ge(gathered[s], PER * (i + 1))
                            sp.dma_start(tiles(edge_h[bass.ds((i * BODY + s * HS) * P, HS * P), :]), cat[:, s, :, 0:F]).then_inc(kept[s], 16)
                    body(0, True, False)
                    with nc.sync.Fori(1, GI - 1) as i:
                        body(i, False, False)
                    body(GI - 1, False, True)
                    for s in range(2):
                        sp.wait_ge(kept[s], 16 * GI)

                @block.gpsimd
                def _(pool):
                    def gather(i, s, first):
                        pool.wait_ge(idx_ok[s], i + 1)
                        if not first:
                            pool.wait_ge(kept[s], 16 * i)
                            pool.wait_ge(tr_ok, (i - 1) * BODY + (s + 1) * HS)
                        pool.sem_inc(go, 1)
                        for t in range(HS):
                            pool.indirect_dma_start(out=cat[:, s, t, 0:F], out_offset=None, in_=node_g,
                                                    in_offset=bass.IndirectOffsetOnAxis(ap=src_st[:, s, t:t + 1], axis=0)).then_inc(gathered[s], 16)
                            pool.indirect_dma_start(out=cat[:, s, t, F:2 * F], out_offset=None, in_=node_g,
                                                    in_offset=bass.IndirectOffsetOnAxis(ap=dst_st[:, s, t:t + 1], axis=0)).then_inc(gathered[s], 16)
                    for s in range(2):
                        gather(0, s, True)
                    with nc.gpsimd.Fori(1, GI) as i:
                        for s in range(2):
                            gather(i, s, False)

                @block.tensor
                def _(pe):
                    pe.wait_ge(ones_ok, 1)

                    def turn(i, k, first, last):
                        s, t = k // HS, k % HS
                        if t == 0:
                            pe.wait_ge(gathered[s], PER * (i + 1))
                            pe.wait_ge(ea_in[s], ea_total(i, s, last))
                        if not (first and k < 2):
                            pe.wait_ge(copied, i * BODY + k - 1)
                        nc.tensor.transpose(bank[k % 2][:, 0:P], cat[:, s, t, :], ident[:, :])
                        nc.tensor.transpose(bank[k % 2][0:F, P:2 * P], ea[:, s, t, :], ident[:, :]).then_inc(tr_ok, 1)

                    def score(i, k, first):
                        q = k // 2
                        if k % 2 == 0 and not (first and q < ZB):
                            before = q - ZB + 1 if q >= ZB else max(j for j in range(PAIRS) if j % ZB == q % ZB) + 1 - PAIRS
                            pe.wait_ge(z_used, i * PAIRS + before)
                        pe.wait_ge(copied, i * BODY + k + 1)
                        zk = bank[2 + q % ZB][:, (k % 2) * HF:(k % 2 + 1) * HF]
                        nc.tensor.matmul(zk, catT[:, k % 2, :], Wlr[:, :], start=True, stop=False)
                        nc.tensor.matmul(zk, eaT[:, k % 2, :], Wea[:, :], start=False, stop=True).then_inc(z_ok, 1)

                    def body(i, first, last):
                        turn(i, 0, first, last)
                        for k in range(BODY):
                            if k + 1 < BODY:
                                turn(i, k + 1, first, last)
                            score(i, k, first)
                    body(0, True, False)
                    with nc.tensor.Fori(1, GI - 1) as i:
                        body(i, False, False)
                    body(GI - 1, False, True)

                @block.scalar
                def _(act):
                    A = nc.scalar

                    def slopes(i, q, first):
                        act.wait_ge(z_ok, i * BODY + 2 * q + 2)
                        if not (first and q < ZB):
                            before = q - ZB + 1 if q >= ZB else max(j for j in range(PAIRS) if j % ZB == q % ZB) + 1 - PAIRS
                            act.wait_ge(z_used, i * PAIRS + before)
                        A.mul(y[:, q % ZB, :], bank[2 + q % ZB][:, :], SLOPE).then_inc(y_ok, 1)

                    def body(i, first):
                        for k in range(BODY):
                            act.wait_ge(tr_ok, i * BODY + k + 1)
                            if not (first and k < 2):
                                act.wait_ge(z_ok, i * BODY + k - 1)
                            A.copy(catT[:, k % 2, :], bank[k % 2][:, 0:P])
                            A.copy(eaT[0:F, k % 2, :], bank[k % 2][0:F, P:2 * P]).then_inc(copied, 1)
                            if k % 2 == 0 and k:
                                slopes(i, k // 2 - 1, first)
                        slopes(i, PAIRS - 1, first)
                    body(0, True)
                    with A.Fori(1, GI) as i:
                        body(i, False)

                @block.vector
                def _(dve):
                    v = nc.vector
                    v.memset(eaT[F:F + 1, :, :], 1.0).then_inc(ones_ok, 1)
                    for s in range(2):
                        v.tensor_copy(src_st[:, s, :], src_i[:, s * HS:(s + 1) * HS])
                        v.tensor_copy(dst_st[:, s, :], dst_i[:, s * HS:(s + 1) * HS]).then_inc(idx_ok[s], 1)

                    def body(i, first):
                        for q in range(PAIRS):
                            dve.wait_ge(y_ok, i * PAIRS + q + 1)
                            v.tensor_tensor(act_z[:, :], bank[2 + q % ZB][:, :], y[:, q % ZB, :], ALU.max).then_inc(z_used, 1)
                            v.drain()
                            v.tensor_tensor(prod[:, :].rearrange("p (t c) -> p t c", t=2), act_z[:, :].rearrange("p (t c) -> p t c", t=2),
                                            attb[:, :].unsqueeze(1).to_broadcast((P, 2, HF)), ALU.mult)
                            v.drain()
                            v.tensor_reduce(al[:, 2 * q:2 * q + 2, :], prod[:, :].rearrange("p (t h f) -> p t h f", t=2, h=HEADS), AX.X, ALU.add)
                            if q in (3, PAIRS - 1):
                                s = 0 if q == 3 else 1
                                at = i * BODY + s * HS + BODY
                                v.drain()
                                dve.wait_ge(gathered[s], PER * (i + 1))
                                v.tensor_copy(src_st[:, s, :], src_i[:, bass.ds(at, HS)])
                                v.tensor_copy(dst_st[:, s, :], dst_i[:, bass.ds(at, HS)]).then_inc(idx_ok[s], 1)
                        v.drain()
                        v.tensor_copy(alpha[:, bass.ds(i * BODY, BODY), :], al[:, :, :])
                        v.drain()
                    body(0, True)
                    with v.Fori(1, GI) as i:
                        body(i, False)

        def segment_max(tag):
            with nc.cleanup_on_exit(), ExitStack() as c, nc.Block() as block:
                tb = lambda name, shape, dt=f32: c.enter_context(nc.sbuf_tensor(tag + name, shape, dt))
                sm = lambda name: nc.alloc_semaphore(tag + name)
                W = NBLK * P
                key = tb("key", [R, NBLK, P]); penf = tb("penf", [R, NBLK, P]); penb = tb("penb", [R, NBLK, P])
                mf = tb("mf", [R, HEADS, W]); mb = tb("mb", [R, HEADS, W]); m = tb("m", [R, HEADS, NBLK, P])
                ekey = tb("ekey", [HEADS, 2 * T]); e = tb("e", [HEADS, 2 * T]); ef = tb("ef", [HEADS, 2 * T]); eb = tb("eb", [HEADS, 2 * T])
                epf = tb("epf", [HEADS, 2 * T]); epb = tb("epb", [HEADS, 2 * T])
                back = tb("back", [R, HEADS, NBLK, 2]); off = tb("off", [R, 2, NBLK, P])
                cand = mf[:, 0:2, :].rearrange("r s (b p) -> r s b p", p=P)
                key_in, turned, ends_ok, ends_out, e_in, em_ok, em_out, back_in, m_ok, backT = (
                    sm(n) for n in ("key_in", "turned", "ends_ok", "ends_out", "e_in", "em_ok", "em_out", "back_in", "m_ok", "backT"))

                @block.sync
                def _(sp):
                    sp.dma_start(key[:, :, :], dst_rows[0:NP].rearrange("(b r p) -> r b p", r=R, p=P)).then_inc(key_in, 16)
                    sp.wait_ge(key_in, 16)
                    with nc.allow_non_contiguous_dma(reason="two values a tile"):
                        for side in range(2):
                            col = side * (P - 1)
                            sp.dma_start(ends_k[:, side].rearrange("(b r) -> r b", r=R), key[:, :, col]).then_inc(ends_out, 16)
                        sp.wait_ge(ends_ok, 1)
                        for h in range(HEADS):
                            for side in range(2):
                                col = side * (P - 1)
                                sp.dma_start(ends_d[h, :, side].rearrange("(b r) -> r b", r=R), m[:, h, :, col]).then_inc(ends_out, 16)
                        sp.wait_ge(ends_out, 16 * (2 + 2 * HEADS))
                        sp.dma_start(e[:, :], ends_d.rearrange("h t l -> h (t l)")).then_inc(e_in, 16)
                        sp.dma_start(ekey[:, :], ends_k.rearrange("(o t) l -> o (t l)", o=1).to_broadcast((HEADS, 2 * T))).then_inc(e_in, 16)
                        sp.wait_ge(em_ok, 1)
                        sp.dma_start(ends_m.rearrange("h t l -> h (t l)"), e[:, :]).then_inc(em_out, 16)
                        sp.wait_ge(em_out, 16)
                        for h in range(HEADS):
                            sp.dma_start(back[:, h, :, :], ends_m[h].rearrange("(b r) l -> r b l", r=R)).then_inc(back_in, 16)

                @block.tensor
                def _(pe):
                    for h in range(HEADS):
                        for b in range(NBLK):
                            ins = nc.tensor.transpose(bank[h][0:R, b * P:(b + 1) * P], alpha[:, b * R:(b + 1) * R, h], ident[:, :])
                    ins.then_inc(turned, 1)
                    pe.wait_ge(m_ok, 1)
                    for h in range(HEADS):
                        for b in range(NBLK):
                            ins = nc.tensor.transpose(bank[4 + h][:, b * R:(b + 1) * R], m[:, h, b, :], ident[0:R, 0:R])
                    ins.then_inc(backT, 1)

                @block.vector
                def _(dve):
                    v = nc.vector
                    dve.wait_ge(key_in, 16)
                    v.memset(penf[:, :, 0:1], NEG)
                    v.memset(penb[:, :, P - 1:P], NEG)
                    v.tensor_tensor(penf[:, :, 1:P], key[:, :, 1:P], key[:, :, 0:P - 1], ALU.not_equal)
                    v.tensor_tensor(penb[:, :, 0:P - 1], key[:, :, 0:P - 1], key[:, :, 1:P], ALU.not_equal)
                    v.drain()
                    v.tensor_scalar(penf[:, :, 1:P], penf[:, :, 1:P], NEG, None, ALU.mult)
                    v.tensor_scalar(penb[:, :, 0:P - 1], penb[:, :, 0:P - 1], NEG, None, ALU.mult)
                    dve.wait_ge(turned, 1)
                    v.drain()
                    pf, pb = penf[:, :, :].rearrange("r b p -> r (b p)"), penb[:, :, :].rearrange("r b p -> r (b p)")
                    for h in range(HEADS):
                        v.tensor_tensor_scan(mf[:, h, :], pf, bank[h][0:R, :], NEG, ALU.add, ALU.max)
                        v.tensor_tensor_scan(mb[:, h, W - 1::-1], pb[:, W - 1::-1], bank[h][0:R, W - 1::-1], NEG, ALU.add, ALU.max)
                    v.drain()
                    v.tensor_tensor(m[:, :, :, :].rearrange("r h b p -> r (h b p)"), mf[:, :, :].rearrange("r h w -> r (h w)"),
                                    mb[:, :, :].rearrange("r h w -> r (h w)"), ALU.max).then_inc(ends_ok, 1)
                    for side in range(2):
                        col = side * (P - 1)
                        v.tensor_tensor(off[:, side, :, :], key[:, :, :], key[:, :, col:col + 1].to_broadcast((R, NBLK, P)), ALU.not_equal)
                    dve.wait_ge(e_in, 32)
                    L = 2 * T
                    v.memset(epf[:, 0:1], NEG)
                    v.memset(epb[:, L - 1:L], NEG)
                    v.tensor_tensor(epf[:, 1:L], ekey[:, 1:L], ekey[:, 0:L - 1], ALU.not_equal)
                    v.tensor_tensor(epb[:, 0:L - 1], ekey[:, 0:L - 1], ekey[:, 1:L], ALU.not_equal)
                    v.drain()
                    v.tensor_scalar(epf[:, 1:L], epf[:, 1:L], NEG, None, ALU.mult)
                    v.tensor_scalar(epb[:, 0:L - 1], epb[:, 0:L - 1], NEG, None, ALU.mult)
                    v.drain()
                    v.tensor_tensor_scan(ef[:, :], epf[:, :], e[:, :], NEG, ALU.add, ALU.max)
                    v.tensor_tensor_scan(eb[:, L - 1::-1], epb[:, L - 1::-1], e[:, L - 1::-1], NEG, ALU.add, ALU.max)
                    v.drain()
                    v.tensor_tensor(e[:, :], ef[:, :], eb[:, :], ALU.max).then_inc(em_ok, 1)
                    dve.wait_ge(back_in, 16 * HEADS)
                    for h in range(HEADS):
                        for side in range(2):
                            v.drain()
                            v.scalar_tensor_tensor(cand[:, side, :, :], off[:, side, :, :], NEG, back[:, h, :, side:side + 1].to_broadcast((R, NBLK, P)), ALU.mult, ALU.add)
                            v.drain()
                            ins = v.tensor_tensor(m[:, h, :, :], m[:, h, :, :], cand[:, side, :, :], ALU.max)
                    ins.then_inc(m_ok, 1)
                    dve.wait_ge(backT, 1)
                    for h in range(HEADS):
                        v.tensor_copy(amax[:, :, h], bank[4 + h][:, 0:T])

        def attend(tag):
            with nc.cleanup_on_exit(), ExitStack() as c, nc.Block() as block:
                tb = lambda name, shape, dt=f32: c.enter_context(nc.sbuf_tensor(tag + name, shape, dt))
                sm = lambda name: nc.alloc_semaphore(tag + name)
                two = lambda name: [sm(f"{name}{s}") for s in range(2)]
                cat = tb("cat", [P, 2, HS, 2 * F]); sums = tb("sums", [P, 2, HS, GATW])
                catT = tb("catT", [P, HS, P]); aggT = tb("aggT", [P, HS, 2, P])
                y = tb("y", [P, HS * HF]); z = tb("z", [P, HS * HF])
                own = tb("own", [P, HS, HEADS]); me = tb("me", [P, HS, HEADS]); mm = tb("mm", [P, HS, HEADS])
                d = tb("d", [P, 2, HS, HEADS]); den = tb("den", [P, HS, HEADS]); cc = tb("cc", [P, 2, HS, HEADS])
                o = tb("o", [P, 2, HS, F])
                loaded, scaled, turned, copied, z_ok, y_ok, z_used, d_ok, e_ok, agg_ok, aT, aT_copied, prod, o_ok, stored, stat, used, first_z, stat_end, go = (
                    sm(n) for n in ("loaded", "scaled", "turned", "copied", "z_ok", "y_ok", "z_used", "d_ok", "e_ok", "agg_ok", "aT", "aT_copied", "prod", "o_ok",
                                    "stored", "stat", "used", "first_z", "stat_end", "go"))
                loads, st_s = two("loads"), two("st_s")
                GROUPS = [(0, 2), (2, 4), (4, 6), (6, HS)]
                CH = [(0, 4), (4, HS)]
                AC = [(0, 4), (4, 8), (8, 12), (12, 14)]

                @block.sync
                def _(sp):
                    def body(i, first):
                        for s in range(2):
                            at = bass.ds((i * BODY + s * HS) * P, HS * P)
                            if not first:
                                sp.wait_ge(used, 2 * i + s - 1)
                            sp.dma_start(cat[:, s, :, 0:F], tiles(node_g[at, :])).then_inc(loads[s], 16)
                            sp.dma_start(cat[:, s, :, F:2 * F], tiles(sums_w[at, F:2 * F])).then_inc(loads[s], 16)
                            sp.dma_start(sums[:, s, :, :], tiles(sums_a[at, :])).then_inc(loads[s], 16)
                    body(0, True)
                    with nc.sync.Fori(1, GI) as i:
                        body(i, False)

                @block.gpsimd
                def _(pool):
                    with nc.gpsimd.Fori(0, GI) as i:
                        for s in range(2):
                            pool.wait_ge(o_ok, 2 * i + s + 1)
                            pool.sem_inc(go, 1)
                            pool.dma_start(tiles(gat_out[bass.ds((i * BODY + s * HS) * P, HS * P), :]), o[:, s, :, :]).then_inc(st_s[s], 16)
                    for s in range(2):
                        pool.wait_ge(st_s[s], 16 * GI)

                @block.tensor
                def _(pe):
                    nc.tensor.matmul(bank[7][:, 0:HS * F], zeros_w[:, 0:P], zeros_w[:, 0:HS * F], start=True, stop=False)

                    def body(i, first):
                        for s in range(2):
                            n = 2 * i + s
                            pe.wait_ge(scaled, n + 1)
                            if not (first and s == 0):
                                pe.wait_ge(aT_copied, 4 * n)
                            pe.sem_inc(go, 1)
                            for b, (t0, t1) in enumerate(CH):
                                for t in range(t0, t1):
                                    ins = nc.tensor.transpose(bank[b][:, (t - t0) * P:(t - t0 + 1) * P], cat[:, s, t, :], ident[:, :])
                            ins.then_inc(turned, 1)
                            pe.wait_ge(copied, n + 1)
                            for j, (t0, t1) in enumerate(GROUPS):
                                if not (first and s == 0):
                                    pe.wait_ge(z_used, n)
                                for t in range(t0, t1):
                                    zt = bank[2 + j][:, (t - t0) * HF:(t - t0 + 1) * HF]
                                    nc.tensor.matmul(zt, catT[:, t, :], Wself[:, :], start=True, stop=False)
                                    ins = nc.tensor.matmul(zt, ones1[:, :], blr[:, 2, :], start=False, stop=True)
                                ins.then_inc(z_ok, 1)
                            pe.wait_ge(agg_ok, n + 1)
                            for j, (k0, k1) in enumerate(AC):
                                if j >= 2:
                                    pe.wait_ge(aT_copied, 4 * n + j - 1)
                                    pe.sem_inc(go, 1)
                                for k in range(k0, k1):
                                    ins = nc.tensor.transpose(bank[j % 2][:, (k - k0) * P:(k - k0 + 1) * P], sums[:, s, k // 2, (k % 2) * P:(k % 2 + 1) * P], ident[:, :])
                                ins.then_inc(aT, 1)
                            pe.wait_ge(aT_copied, 4 * n + 4)
                            for t in range(HS):
                                for q in range(2):
                                    ins = nc.tensor.matmul(bank[6][:, t * F:(t + 1) * F], aggT[:, t, q, :], Wst[:, q, :], start=(q == 0), stop=(q == 1))
                            ins.then_inc(prod, 1)
                            pe.wait_ge(o_ok, n + 1)
                            nc.tensor.matmul(bank[7][:, 0:HS * F], onesP[:, :], o[:, s, :, :].rearrange("p t f -> p (t f)"), start=False, stop=False).then_inc(stat, 1)
                    body(0, True)
                    with nc.tensor.Fori(1, GI) as i:
                        body(i, False)
                    nc.tensor.matmul(bank[7][:, 0:HS * F], zeros_w[:, 0:P], zeros_w[:, 0:HS * F], start=False, stop=True).then_inc(stat_end, 1)

                @block.scalar
                def _(act):
                    A = nc.scalar

                    def body(i, first):
                        for s in range(2):
                            n = 2 * i + s
                            act.wait_ge(turned, n + 1)
                            for b, (t0, t1) in enumerate(CH):
                                ins = A.copy(catT[:, t0:t1, :].rearrange("p t q -> p (t q)"), bank[b][:, 0:(t1 - t0) * P])
                            ins.then_inc(copied, 1)
                            for j, (t0, t1) in enumerate(GROUPS):
                                act.wait_ge(z_ok, 4 * n + j + 1)
                                if not (first and s == 0):
                                    act.wait_ge(z_used, n)
                                A.mul(y[:, t0 * HF:t1 * HF], bank[2 + j][:, 0:(t1 - t0) * HF], SLOPE).then_inc(y_ok, 1)
                            act.wait_ge(d_ok, n + 1)
                            A.activation(d[:, :, :, :], d[:, :, :, :], ACT.Exp).then_inc(e_ok, 1)
                            for j, (k0, k1) in enumerate(AC):
                                act.wait_ge(aT, 4 * n + j + 1)
                                A.copy(aggT[:, :, :, :].rearrange("p t q c -> p (t q c)")[:, k0 * P:k1 * P], bank[j % 2][:, 0:(k1 - k0) * P]).then_inc(aT_copied, 1)
                    body(0, True)
                    with A.Fori(1, GI) as i:
                        body(i, False)

                @block.vector
                def _(dve):
                    v = nc.vector

                    def body(i, first):
                        for s in range(2):
                            n = 2 * i + s
                            at = bass.ds(i * BODY + s * HS, HS)
                            sm_ = sums[:, s, :, :]
                            heads = lambda ap: ap.unsqueeze(2).to_broadcast((P, HS, HEADS))
                            dve.wait_ge(loads[s], 48 * (i + 1))
                            v.tensor_tensor(cat[:, s, :, F:2 * F], cat[:, s, :, F:2 * F], inv_cnt[:, at].unsqueeze(2).to_broadcast((P, HS, F)), ALU.mult).then_inc(scaled, 1)
                            v.tensor_tensor(me[:, :, :], sm_[:, :, HF + HEADS:GATW], heads(no_edge[:, at]), ALU.add)
                            for j, (t0, t1) in enumerate(GROUPS):
                                dve.wait_ge(y_ok, 4 * n + j + 1)
                                ins = v.tensor_tensor(z[:, t0 * HF:t1 * HF], bank[2 + j][:, 0:(t1 - t0) * HF], y[:, t0 * HF:t1 * HF], ALU.max)
                            ins.then_inc(z_used, 1)
                            v.drain()
                            zz = z[:, :].rearrange("p (t c) -> p t c", t=HS)
                            v.tensor_tensor(zz, zz, attb[:, :].unsqueeze(1).to_broadcast((P, HS, HF)), ALU.mult)
                            v.drain()
                            v.tensor_reduce(own[:, :, :], z[:, :].rearrange("p (t h f) -> p t h f", t=HS, h=HEADS), AX.X, ALU.add)
                            v.drain()
                            v.tensor_tensor(mm[:, :, :], me[:, :, :], own[:, :, :], ALU.max)
                            v.drain()
                            v.tensor_tensor(d[:, 0, :, :], me[:, :, :], mm[:, :, :], ALU.subtract)
                            v.tensor_tensor(d[:, 1, :, :], own[:, :, :], mm[:, :, :], ALU.subtract).then_inc(d_ok, 1)
                            dve.wait_ge(e_ok, n + 1)
                            v.tensor_tensor(den[:, :, :], sm_[:, :, HF:HF + HEADS], d[:, 0, :, :], ALU.mult)
                            v.drain()
                            v.tensor_tensor(den[:, :, :], den[:, :, :], d[:, 1, :, :], ALU.add)
                            v.drain()
                            v.tensor_scalar(den[:, :, :], den[:, :, :], SM_EPS, None, ALU.add)
                            v.drain()
                            v.reciprocal(den[:, :, :], den[:, :, :])
                            v.drain()
                            for q in range(2):
                                v.tensor_tensor(cc[:, q, :, :], d[:, q, :, :], den[:, :, :], ALU.mult)
                            v.drain()
                            num = sm_[:, :, 0:HF].rearrange("p t (h f) -> p t h f", h=HEADS)
                            z4 = z[:, :].rearrange("p (t h f) -> p t h f", t=HS, h=HEADS)
                            for h in range(HEADS):
                                v.tensor_tensor(num[:, :, h, :], num[:, :, h, :], cc[:, 0, :, h:h + 1].to_broadcast((P, HS, F)), ALU.mult)
                                v.tensor_tensor(z4[:, :, h, :], cat[:, s, :, 0:F], cc[:, 1, :, h:h + 1].to_broadcast((P, HS, F)), ALU.mult)
                            v.drain()
                            v.tensor_tensor(sm_[:, :, 0:HF], sm_[:, :, 0:HF], zz, ALU.add).then_inc(agg_ok, 1)
                            dve.wait_ge(prod, n + 1)
                            v.sem_inc(used, 1)
                            if not first:
                                dve.wait_ge(st_s[s], 16 * i)
                                dve.wait_ge(stat, n - 1)
                            v.tensor_scalar(o[:, s, :, :].rearrange("p t f -> p (t f)"), bank[6][:, 0:HS * F], 1.0 / HEADS, None, ALU.mult)
                            v.drain()
                            v.tensor_tensor(o[:, s, :, :], o[:, s, :, :], b2[:, :].unsqueeze(1).to_broadcast((P, HS, F)), ALU.add)
                            v.drain()
                            v.tensor_tensor(o[:, s, :, :], o[:, s, :, :], real[:, at].unsqueeze(2).to_broadcast((P, HS, F)), ALU.mult).then_inc(o_ok, 1)
                    body(0, True)
                    with v.Fori(1, GI) as i:
                        body(i, False)
                    dve.wait_ge(stat_end, 1)
                    v.tensor_reduce(mu[:, :], bank[7][:, 0:HS * F].rearrange("p (t f) -> p f t", t=HS), AX.X, ALU.add)
                    v.drain()
                    v.tensor_scalar(mu[:, :], mu[:, :], 1.0 / N, None, ALU.mult)

        def variance(tag):
            with nc.cleanup_on_exit(), ExitStack() as c, nc.Block() as block:
                tb = lambda name, shape, dt=f32: c.enter_context(nc.sbuf_tensor(tag + name, shape, dt))
                sm = lambda name: nc.alloc_semaphore(tag + name)
                o = tb("o", [P, 2, HS, F]); dev = tb("dev", [P, 2, HS, F]); sq = tb("sq", [P, 2, HS, F]); var = tb("var", [P, 2, F])
                o_in = [sm(f"o_in{s}") for s in range(2)]
                dev_ok, sq_ok, summed, done, v_ok, sd_ok = (sm(n) for n in ("dev_ok", "sq_ok", "summed", "done", "v_ok", "sd_ok"))

                @block.sync
                def _(sp):
                    def body(i, first):
                        for s in range(2):
                            if not first:
                                sp.wait_ge(dev_ok, 2 * i + s - 1)
                            sp.dma_start(o[:, s, :, :], tiles(gat_out[bass.ds((i * BODY + s * HS) * P, HS * P), :])).then_inc(o_in[s], 16)
                    body(0, True)
                    with nc.sync.Fori(1, GI) as i:
                        body(i, False)

                @block.vector
                def _(dve):
                    v = nc.vector

                    def body(i, first):
                        for s in range(2):
                            dve.wait_ge(o_in[s], 16 * (i + 1))
                            if not first:
                                dve.wait_ge(sq_ok, 2 * i + s - 1)
                            v.tensor_tensor(dev[:, s, :, :], o[:, s, :, :], mu[:, :].unsqueeze(1).to_broadcast((P, HS, F)), ALU.subtract)
                            v.drain()
                            v.tensor_tensor(dev[:, s, :, :], dev[:, s, :, :], real[:, bass.ds(i * BODY + s * HS, HS)].unsqueeze(2).to_broadcast((P, HS, F)), ALU.mult).then_inc(dev_ok, 1)
                    body(0, True)
                    with v.Fori(1, GI) as i:
                        body(i, False)
                    dve.wait_ge(done, 1)
                    v.tensor_reduce(var[:, 0, :], bank[7][:, 0:HS * F].rearrange("p (t f) -> p f t", t=HS), AX.X, ALU.add).then_inc(v_ok, 1)
                    dve.wait_ge(sd_ok, 1)
                    v.reciprocal(var[:, 0, :], var[:, 1, :])
                    v.drain()
                    v.tensor_tensor(bn_a[:, :], gamma[:, :], var[:, 0, :], ALU.mult)

                @block.scalar
                def _(act):
                    def body(i, first):
                        for s in range(2):
                            act.wait_ge(dev_ok, 2 * i + s + 1)
                            if not first:
                                act.wait_ge(summed, 2 * i + s - 1)
                            nc.scalar.activation(sq[:, s, :, :], dev[:, s, :, :], ACT.Square).then_inc(sq_ok, 1)
                    body(0, True)
                    with nc.scalar.Fori(1, GI) as i:
                        body(i, False)
                    act.wait_ge(v_ok, 1)
                    nc.scalar.activation(var[:, 1, :], var[:, 0, :], ACT.Sqrt, bias=eps[:, 0:1], scale=1.0 / N).then_inc(sd_ok, 1)

                @block.tensor
                def _(pe):
                    nc.tensor.matmul(bank[7][:, 0:HS * F], zeros_w[:, 0:P], zeros_w[:, 0:HS * F], start=True, stop=False)
                    with nc.tensor.Fori(0, GI) as i:
                        for s in range(2):
                            pe.wait_ge(sq_ok, 2 * i + s + 1)
                            nc.tensor.matmul(bank[7][:, 0:HS * F], onesP[:, :], sq[:, s, :, :].rearrange("p t f -> p (t f)"), start=False, stop=False).then_inc(summed, 1)
                    nc.tensor.matmul(bank[7][:, 0:HS * F], zeros_w[:, 0:P], zeros_w[:, 0:HS * F], start=False, stop=True).then_inc(done, 1)

        prepare()
        nodes("n0", "start")
        edge_sums("e0", "wide", 2 * F, sums_w)
        nodes("n1", "conv")
        edge_sums("e1", "plain", F, sums_n)
        nodes("n2", "sage")
        edge_scores("es")
        segment_max("sm")
        edge_sums("e2", "gat", GATW, sums_a)
        attend("at")
        variance("bv")
        nodes("n3", "bn")
        for layer in range(3):
            edge_sums(f"f{layer}", "typed", 2 * F, sums_w)
            nodes(f"r{layer}", "rel", layer)


INPUTS = ["x", "src", "dst", "edge_attr_64", "edge_type_2", "L0_gnn_weight", "L0_gnn_bias", "L1_gnn_W", "L1_gnn_b",
          "L2_gnn_W_l", "L2_gnn_b_l", "L2_gnn_W_r", "L2_gnn_b_r", "L2_gnn_W_e", "L2_gnn_att", "L2_gnn_bias",
          "L2_gnn_gamma", "L2_gnn_beta", "L3_gnn_W0", "L3_gnn_Ws0", "L3_gnn_b0", "L3_gnn_W1", "L3_gnn_Ws1",
          "L3_gnn_b1", "L3_gnn_W2", "L3_gnn_Ws2", "L3_gnn_b2"]


def kernel(**inputs):
    import numpy as np
    import concourse.bacc as bacc
    from concourse.bass_utils import run_bass_kernel_spmd

    nc = bacc.Bacc("TRN2", target_bir_lowering=False, num_devices=1)
    arrays, args = {}, {}
    for name in INPUTS:
        v = np.ascontiguousarray(inputs[name])
        arrays[f"in_{name}"] = v
        args[name] = nc.dram_tensor(f"in_{name}", v.shape, mybir.dt.from_np(v.dtype), kind="ExternalInput").ap()
    shape = tuple(inputs["x"].shape)
    result = nc.dram_tensor("result", shape, mybir.dt.float32, kind="ExternalOutput").ap()
    build_gnn(nc, args, result)
    return run_bass_kernel_spmd(nc, [arrays], core_ids=[0]).results[0]["result"]
```

```python
import concourse.bass as bass
from concourse import mybir
from contextlib import ExitStack

P = 128
F = 64
HEADS = 4
HF = HEADS * F
HS = 7
BODY = 2 * HS
NBLK = 4
NEG = -1.0e30
SKIP = 2 ** 20
WT = HS + 1
WR = WT * P
BAND = 2
FRONT = P
LAG = 2
LN_EPS = 1e-5
BN_EPS = 1e-5
SM_EPS = 1e-16
SLOPE = 0.2
GATW = HF + 2 * HEADS


def build_gnn(nc, a, out):
    f32, bf16, i32 = mybir.dt.float32, mybir.dt.bfloat16, mybir.dt.int32
    ALU, ACT, AX = mybir.AluOpType, mybir.ActivationFunctionType, mybir.AxisListType

    N = a["x"].shape[0]
    FULL, REM = N // P, N % P
    T = -(-N // (P * 2 * BODY)) * 2 * BODY
    NP = T * P
    R = T // NBLK
    GI = T // BODY
    NS = T // HS
    HI = NP // 256
    assert a["src"].shape[0] == N and HI == 2 * R and R <= P

    def scratch(name, shape, dt=f32):
        return nc.dram_tensor(name, shape, dt, kind="Internal").ap()

    ER = FRONT + NP + WR
    dst_all = scratch("dst_rows", (ER,))
    dst_rows = dst_all[FRONT:ER]
    node_h = scratch("node_h", (NP, F))
    node_g = scratch("node_g", (NP, F))
    edge_all = scratch("edge_h", (ER, F))
    edge_h = edge_all[FRONT:ER, :]
    sums_w = scratch("sums_w", (NP, 2 * F))
    sums_n = scratch("sums_n", (NP, F))
    sums_a = scratch("sums_a", (NP, GATW))
    type_all = scratch("type_rows", (ER,))
    type_rows = type_all[FRONT:ER]
    dst_win = scratch("dst_win", (NS * WR,))
    type_win = scratch("type_win", (NS * WR,))
    attr_all = scratch("edge_a", (ER, F))
    node_g2 = scratch("node_g2", (NP, F))
    inv_row = scratch("inv_row", (NP,))
    loop_rows = scratch("loop_rows", (F, NP))
    gat_out = scratch("gat_out", (NP, F))
    gat_rows = scratch("gat_rows", (F, NP))
    exp_all = scratch("edge_x", (2 * HEADS, ER))
    ends_d = scratch("ends_d", (HEADS, T, 2))
    ends_k = scratch("ends_k", (T, 2))
    ends_m = scratch("ends_m", (HEADS, T, 2))

    tiles = lambda ap: ap.rearrange("(t p) f -> p t f", p=P)

    ctx = ExitStack()
    with ctx:
        sb = lambda name, shape, dt=f32: ctx.enter_context(nc.sbuf_tensor(name, shape, dt))
        sem = lambda name: ctx.enter_context(nc.semaphore(name))
        bank = [ctx.enter_context(nc.psum_tensor(f"bank{i}", [P, 512], f32)) for i in range(8)]

        ident = sb("ident", [P, P])
        x_sb = sb("x_sb", [P, T, F])
        src_i = sb("src_i", [P, T + BODY], i32)
        dst_i = sb("dst_i", [P, T + BODY], i32)
        per_tile = sb("per_tile", [P, 10, T])
        put_i = per_tile[:, 0, :].bitcast(i32)
        dst_f, is_last, prev_f, norm, rs_send, upd_scale, inv_cnt = (per_tile[:, k, :] for k in range(1, 8))
        rel = per_tile[:, 8:10, :]
        cnt = sb("cnt", [P, T])
        no_edge = sb("no_edge", [P, T])
        real = sb("real", [P, T])
        eps = sb("eps", [P, 1])
        starts = sb("starts", [1, NS], i32)
        fast = sb("fast", [1, 1], i32)
        node_id = sb("node_id", [P, P])
        edge_id = sb("edge_id", [P, max(NS * HS * BAND, 2 * HF)])
        rel_w = sb("rel_w", [P, 2, NS * WT])
        W1s = sb("W1s", [2 * F, F])
        attc = sb("attc", [P, 2, HEADS])
        Vlr = sb("Vlr", [2 * F, HEADS]); Vea = sb("Vea", [F, HEADS]); Vself = sb("Vself", [2 * F, HEADS])
        a_const = sb("a_const", [P, HEADS]); b_col = sb("b_col", [P, 2])
        o_col = sb("o_col", [F, 1]); bn_col = sb("bn_col", [F, 2])
        alpha = sb("alpha", [P, T, HEADS])
        amax = sb("amax", [P, T, HEADS])

        W0 = sb("W0", [F, F]); b0 = sb("b0", [P, F])
        W1 = sb("W1", [2 * F, F]); b1 = sb("b1", [P, F])
        Wlr = sb("Wlr", [2 * F, HF]); Wea = sb("Wea", [F + 1, HF]); Wself = sb("Wself", [2 * F, HF])
        Wr0 = sb("Wr0", [F, HF]); b_sum = sb("b_sum", [1, HF])
        brow = edge_id[0:F + 1, 0:2 * HF].rearrange("p (j c) -> p j c", j=2)
        attb = sb("attb", [P, HF]); Wst = sb("Wst", [P, 2, F]); blb = sb("blb", [P, HF])
        b2 = sb("b2", [P, F]); gamma = sb("gamma", [P, F]); beta = sb("beta", [P, F])
        W3 = sb("W3", [P, 3, F]); Ws3 = sb("Ws3", [F, 3, F]); b3 = sb("b3", [P, 3, F])
        mu = sb("mu", [P, F]); bn_a = sb("bn_a", [P, F])
        ones1 = sb("ones1", [1, P]); onesP = sb("onesP", [P, P]); zeros_w = sb("zeros_w", [P, HS * F])


        def lent(buf, two_slots, fresh):
            flat = buf[:, :, :].rearrange("p a b -> p (a b)")
            if flat.shape[1] < two_slots:
                flat = fresh([P, two_slots])[:, :]
            return flat[:, 0:two_slots].rearrange("p (s t f) -> p s t f", s=2, f=F)

        def prepare():
            with nc.cleanup_on_exit(), ExitStack() as c, nc.Block() as block:
                tb = lambda name, shape, dt=f32: c.enter_context(nc.sbuf_tensor(name, shape, dt))
                sm = lambda name: nc.alloc_semaphore("pre_" + name)
                BP = NBLK * P
                work = tb("work", [P, max(9 * BP, 8 * T)])
                blocks = lambda lo, n: work[0:R, lo * BP:(lo + n) * BP].rearrange("r (j b p) -> r j b p", b=NBLK, p=P)
                raw = blocks(0, 3).bitcast(i32)
                rows = blocks(3, 4)
                nxt, last = blocks(7, 1)[:, 0], blocks(8, 1)[:, 0]
                row_i = tb("row_i", [P, P], i32); col_i = tb("col_i", [P, 1], i32)
                row_f = node_id; col_f = tb("col_f", [P, 1]); m127 = tb("m127", [P, 2])
                end_row = tb("end_row", [WT, 2, P])
                digits = lambda buf: buf[:, :, :].rearrange("p t h -> p (t h)").rearrange("p (j t) -> p j t", j=4)
                dig_i, dig = digits(amax).bitcast(i32), digits(alpha)
                iota_i = tb("iota_i", [P, 256], i32); iota_b = tb("iota_b", [P, 256], bf16)
                hi = tb("hi", [P, 2, 2, HS, HI], bf16)
                lo = tb("lo", [P, 2, 2, HS, 256], bf16)
                zb = zeros_w[:, 0:256].bitcast(bf16)
                hist = lo[0:R, 0, :, :, :].rearrange("p j t n -> p (j t n)")[:, 0:2048].bitcast(f32).rearrange("p (j n) -> p j n", j=2)
                cols = lambda lo, n: work[:, lo * T:(lo + n) * T].rearrange("p (j t) -> p j t", t=T)
                deg, sq, tmp = cols(0, 2), cols(2, 3), cols(5, 3)
                filled = sm("filled"); raw_in = sm("raw_in"); floats = sm("floats"); sent = sm("sent")
                dst_out = sm("dst_out"); nxt_in = sm("nxt_in"); put = sm("put"); ident_ok = sm("ident_ok")
                iotas = sm("iotas"); turned = sm("turned"); taken = sm("taken"); w_in = sm("w_in")
                x_in = sm("x_in"); oh = sm("oh"); counted = sm("counted"); hist_ok = sm("hist_ok")
                cleared = sm("cleared"); hist_t = sm("hist_t"); sq_in = sm("sq_in"); sq_out = sm("sq_out")
                tails = sm("tails"); types_out = sm("types_out"); summed = sm("summed"); w_n = sm("w_n")
                x_parts = [(k * FULL // 4, (k + 1) * FULL // 4) for k in range(4)]
                names = ["src", "dst", "edge_type_2"]
                whole = (N // (R * P))
                rem_rows = (N - whole * R * P) // P

                @block.sync
                def _(sp):
                    sp.wait_ge(filled, 1)
                    n = 0
                    for j, name in enumerate(names):
                        v = a[name]
                        sp.dma_start(raw[:, j, 0:whole, :], v[0:whole * R * P].rearrange("(b r p) -> r b p", r=R, p=P)).then_inc(raw_in, 16)
                        at = whole * R * P
                        if rem_rows:
                            sp.dma_start(raw[0:rem_rows, j, whole, :], v[at:at + rem_rows * P].rearrange("(r p) -> r p", p=P)).then_inc(raw_in, 16)
                            n += 1
                        if REM:
                            sp.dma_start(raw[rem_rows:rem_rows + 1, j, whole, 0:REM], v[FULL * P:N].rearrange("(o p) -> o p", o=1)).then_inc(raw_in, 16)
                            n += 1
                        n += 1
                    sp.sem_inc(w_n, 1)
                    for lo_t, hi_t in x_parts:
                        sp.dma_start(x_sb[:, lo_t:hi_t, :], tiles(a["x"][lo_t * P:hi_t * P, :])).then_inc(x_in, 16)
                    if REM:
                        sp.dma_start(x_sb[0:REM, FULL, :], a["x"][FULL * P:N, :]).then_inc(x_in, 16)
                    sp.wait_ge(floats, 1)
                    sp.dma_start(dst_rows[0:NP].rearrange("(b r p) -> r b p", r=R, p=P), rows[:, 1, :, :]).then_inc(dst_out, 16)
                    sp.dma_start(dst_rows[NP:NP + WR].rearrange("(q p) -> q p", p=P), end_row[:, 0, :]).then_inc(dst_out, 16)
                    sp.wait_ge(dst_out, 32)
                    sp.dma_start(nxt[:, :, :], dst_rows[1:NP + 1].rearrange("(b r p) -> r b p", r=R, p=P)).then_inc(nxt_in, 16)
                    sp.dma_start(type_rows[0:NP].rearrange("(b r p) -> r b p", r=R, p=P), rows[:, 2, :, :]).then_inc(types_out, 16)
                    sp.dma_start(type_rows[NP:NP + WR].rearrange("(q p) -> q p", p=P), end_row[:, 1, :]).then_inc(tails, 16)
                    n = 1
                    for to, j in ((dst_all, 0), (type_all, 1)):
                        sp.dma_start(to[0:FRONT].rearrange("(o p) -> o p", p=P), end_row[0:1, j, :]).then_inc(tails, 16)
                        n += 1
                    for to, lo, hi_row in ((attr_all, 0, FRONT), (edge_all, 0, FRONT), (attr_all, FRONT + N, ER), (edge_all, FRONT + NP, ER)):
                        for r0 in range(lo, hi_row, P):
                            r1 = min(r0 + P, hi_row)
                            sp.dma_start(to[r0:r1, :], zeros_w[0:r1 - r0, 0:F]).then_inc(tails, 16)
                            n += 1
                    CUT = 16 if N % 16 == 0 else 8
                    sp.dma_start(attr_all[FRONT:FRONT + N, :].rearrange("(c n) f -> c (n f)", c=CUT), a["edge_attr_64"].rearrange("(c n) f -> c (n f)", c=CUT)).then_inc(tails, 16)
                    sp.wait_ge(tails, 16 * (n + 1))
                    sp.wait_ge(x_in, 16 * (len(x_parts) + (1 if REM else 0)))

                n_raw = 3 * (1 + (1 if rem_rows else 0) + (1 if REM else 0))

                @block.scalar
                def _(act):
                    bc = lambda v: v.rearrange("(o f) -> o f", o=1).to_broadcast((P, v.shape[0]))
                    att = a["L2_gnn_att"].rearrange("h f -> (h f)")
                    wl = a["L2_gnn_W_l"]
                    loads = [
                        (W0[:, :], a["L0_gnn_weight"]), (b0[:, :], bc(a["L0_gnn_bias"])),
                        (W1[:, :], a["L1_gnn_W"]), (W1s[0:F, :], a["L1_gnn_W"][F:2 * F, :]), (W1s[F:2 * F, :], a["L1_gnn_W"][0:F, :]), (b1[:, :], bc(a["L1_gnn_b"])),
                        (Wlr[0:F, :], wl), (Wlr[F:2 * F, :], a["L2_gnn_W_r"]), (Wr0[:, :], a["L2_gnn_W_r"]),
                        (Wea[0:F, :], a["L2_gnn_W_e"]), (Wself[0:F, :], wl), (Wself[F:2 * F, :], a["L2_gnn_W_e"]),
                        (brow[0:1, 0, :], a["L2_gnn_b_l"].rearrange("(o f) -> o f", o=1)),
                        (brow[0:1, 1, :], a["L2_gnn_b_r"].rearrange("(o f) -> o f", o=1)),
                        (brow[F:F + 1, 0, :], a["L2_gnn_b_l"].rearrange("(o f) -> o f", o=1)),
                        (brow[F:F + 1, 1, :], a["L2_gnn_b_r"].rearrange("(o f) -> o f", o=1)),
                        (attb[:, :], bc(att)), (blb[:, :], bc(a["L2_gnn_b_l"])),
                        (b2[:, :], bc(a["L2_gnn_bias"])), (gamma[:, :], bc(a["L2_gnn_gamma"])), (beta[:, :], bc(a["L2_gnn_beta"])),
                    ]
                    for h in range(HEADS):
                        loads.append((Wst[(h % 2) * F:(h % 2 + 1) * F, h // 2, :], wl[:, h * F:(h + 1) * F]))
                    for k in range(3):
                        loads.append((W3[:, k, :], a[f"L3_gnn_W{k}"].rearrange("r d o -> (r d) o")))
                        loads.append((Ws3[:, k, :], a[f"L3_gnn_Ws{k}"]))
                        loads.append((b3[:, k, :], bc(a[f"L3_gnn_b{k}"])))
                    for to, of in loads:
                        act.dma_start(to, of).then_inc(w_in, 16)
                    act.wait_ge(w_in, 16 * len(loads))
                    act.sem_inc(w_n, 1)
                    act.wait_ge(sq_in, 1)
                    nc.scalar.activation(sq[:, :, :], tmp[:, :, :], ACT.Sqrt).then_inc(sq_out, 1)

                @block.gpsimd
                def _(pool):
                    nc.gpsimd.iota(row_i[:, :], pattern=[[1, P]], base=0, channel_multiplier=0)
                    nc.gpsimd.iota(col_i[:, :], pattern=[[0, 1]], base=0, channel_multiplier=1)
                    nc.gpsimd.iota(iota_i[:, :], pattern=[[1, 256]], base=0, channel_multiplier=0).then_inc(iotas, 1)

                @block.vector
                def _(dve):
                    v = nc.vector
                    for j in range(2):
                        v.memset(raw[:, j, :, :], NP - 1)
                    v.memset(raw[:, 2, :, :], 0)
                    v.memset(x_sb[:, FULL:T, :], 0.0)
                    v.memset(end_row[:, 0, :], float(NP))
                    v.memset(end_row[:, 1, :], 0.0)
                    v.memset(src_i[:, T:], 0)
                    v.memset(dst_i[:, T:], 0)
                    v.memset(eps[:, :], LN_EPS)
                    v.memset(ones1[:, :], 1.0)
                    v.memset(onesP[:, :], 1.0)
                    v.memset(zeros_w[:, :], 0.0).then_inc(filled, 1)
                    dve.wait_ge(iotas, 1)
                    v.tensor_copy(row_f[:, :], row_i[:, :])
                    v.tensor_copy(col_f[:, :], col_i[:, :])
                    v.tensor_copy(iota_b[:, :], iota_i[:, :])
                    v.drain()
                    v.tensor_scalar(ident[:, :], row_f[:, :], col_f[:, 0:1], None, ALU.is_equal).then_inc(ident_ok, 1)
                    v.tensor_scalar(m127[:, 0:1], col_f[:, :], float(P - 1), None, ALU.is_equal)
                    v.tensor_scalar(m127[:, 1:2], col_f[:, :], float(P - 1), -1.0, ALU.not_equal, ALU.mult)
                    dve.wait_ge(raw_in, 16 * n_raw)
                    v.tensor_copy(rows[:, 0:3, :, :].rearrange("r j b p -> r (j b p)"), raw[:, :, :, :].rearrange("r j b p -> r (j b p)")).then_inc(floats, 1)
                    dve.wait_ge(nxt_in, 16)
                    v.tensor_tensor(last[:, :, :], rows[:, 1, :, :], nxt[:, :, :], ALU.is_equal)
                    v.drain()
                    v.scalar_tensor_tensor(rows[:, 3, :, :], last[:, :, :], float(SKIP), rows[:, 1, :, :], ALU.mult, ALU.add).then_inc(put, 1)
                    dve.wait_ge(turned, 1)
                    v.tensor_copy(src_i[:, 0:T], bank[0][:, 0:T])
                    v.tensor_copy(dst_f[:, :], bank[1][:, 0:T])
                    v.tensor_copy(dst_i[:, 0:T], bank[1][:, 0:T])
                    v.tensor_scalar(rel[:, 0, :], bank[2][:, 0:T], 0.0, None, ALU.is_equal)
                    v.tensor_scalar(rel[:, 1, :], bank[2][:, 0:T], 0.0, None, ALU.not_equal)
                    v.tensor_copy(put_i[:, :], bank[3][:, 0:T])
                    v.tensor_scalar(is_last[:, :], bank[3][:, 0:T], float(SKIP), None, ALU.is_lt)
                    v.drain()
                    v.memset(prev_f[:, 0:1], -1.0)
                    v.tensor_scalar(prev_f[:, 1:T], dst_f[:, 0:T - 1], m127[:, 0:1], m127[:, 1:2], ALU.mult, ALU.add)
                    for j, idx in enumerate((src_i, dst_i)):
                        v.tensor_scalar(dig_i[:, 2 * j, :], idx[:, 0:T], 8, None, ALU.arith_shift_right)
                        v.tensor_scalar(dig_i[:, 2 * j + 1, :], idx[:, 0:T], 255, None, ALU.bitwise_and)
                    v.drain()
                    v.tensor_copy(dig[:, :, :], dig_i[:, :, :])
                    v.memset(real[:, 0:FULL], 1.0)
                    v.memset(real[:, FULL:T], 0.0)
                    v.drain()
                    if REM:
                        v.memset(real[0:REM, FULL:FULL + 1], 1.0)
                    v.drain()
                    v.sem_inc(cleared, 1)

                    def body(i, first):
                        for s in range(2):
                            if not first:
                                dve.wait_ge(counted, 2 * i + s - 1)
                            for t in range(HS):
                                for j in range(2):
                                    g = i * BODY + s * HS + t
                                    v.tensor_scalar(hi[:, s, j, t, :], iota_b[:, 0:HI], dig[:, 2 * j, bass.ds(g, 1)], None, ALU.is_equal)
                                    ins = v.tensor_scalar(lo[:, s, j, t, :], iota_b[:, :], dig[:, 2 * j + 1, bass.ds(g, 1)], None, ALU.is_equal)
                            ins.then_inc(oh, 1)
                    body(0, True)
                    with v.Fori(1, GI) as i:
                        body(i, False)
                    dve.wait_ge(summed, 1)
                    for j in range(2):
                        ins = v.tensor_copy(hist[:, j, :], bank[4 + j][0:R, :])
                    ins.then_inc(hist_ok, 1)
                    dve.wait_ge(hist_t, 1)
                    dve.wait_ge(types_out, 16)
                    for j in range(2):
                        for k in range(2):
                            for half in range(2):
                                d0 = deg[:, j, :].rearrange("p (k r h) -> p k r h", k=2, h=2)[:, k, :, half]
                                v.tensor_copy(d0, bank[j][:, (2 * k + half) * R:(2 * k + half + 1) * R])
                    v.drain()
                    v.tensor_copy(cnt[:, :], deg[:, 1, :])
                    v.tensor_scalar(tmp[:, 0, :], deg[:, 1, :], 1.0, None, ALU.max)
                    v.tensor_scalar(tmp[:, 1, :], deg[:, 0, :], 1.0, None, ALU.add)
                    v.tensor_scalar(tmp[:, 2, :], deg[:, 1, :], 1.0, None, ALU.add)
                    v.tensor_scalar(no_edge[:, :], deg[:, 1, :], 0.0, NEG, ALU.is_equal, ALU.mult)
                    v.drain()
                    v.sem_inc(sq_in, 1)
                    v.reciprocal(inv_cnt[:, :], tmp[:, 0, :])
                    dve.wait_ge(sq_out, 1)
                    v.reciprocal(norm[:, :], sq[:, 0, :])
                    v.reciprocal(rs_send[:, :], sq[:, 1, :])
                    v.tensor_tensor(upd_scale[:, :], sq[:, 2, :], tmp[:, 2, :], ALU.mult)
                    v.drain()
                    v.reciprocal(upd_scale[:, :], upd_scale[:, :])
                    dve.wait_ge(w_n, 2)
                    v.tensor_tensor(Wself[0:F, :], Wself[0:F, :], Wr0[:, :], ALU.add)
                    v.tensor_tensor(b_sum[:, :], brow[0:1, 0, :], brow[0:1, 1, :], ALU.add)
                    v.tensor_tensor(Wea[F:F + 1, :], brow[F:F + 1, 0, :], brow[F:F + 1, 1, :], ALU.add)
                    v.tensor_reduce(mu[:, :], blb[:, :].rearrange("p (h o) -> p o h", h=HEADS), AX.X, ALU.add)
                    v.drain()
                    v.scalar_tensor_tensor(b2[:, :], mu[:, :], 1.0 / HEADS, b2[:, :], ALU.mult, ALU.add)

                @block.tensor
                def _(pe):
                    pe.wait_ge(ident_ok, 1)
                    pe.wait_ge(floats, 1)
                    pe.wait_ge(put, 1)
                    for j in range(4):
                        for b in range(NBLK):
                            ins = nc.tensor.transpose(bank[j][:, b * R:(b + 1) * R], rows[:, j, b, :], ident[0:R, 0:R])
                    ins.then_inc(turned, 1)
                    pe.wait_ge(cleared, 1)
                    for j in range(2):
                        nc.tensor.matmul(bank[4 + j][0:R, :], zb[:, 0:R], zb[:, :], start=True, stop=False)

                    def body(i, first):
                        for s in range(2):
                            pe.wait_ge(oh, 2 * i + s + 1)
                            for t in range(HS):
                                for j in range(2):
                                    for k in range(2):
                                        ins = nc.tensor.matmul(bank[4 + j][0:R, k * 256:(k + 1) * 256], hi[:, s, j, t, k * R:(k + 1) * R],
                                                               lo[:, s, j, t, :], start=False, stop=False)
                            ins.then_inc(counted, 1)
                    with nc.tensor.Fori(0, GI) as i:
                        body(i, False)
                    for j in range(2):
                        ins = nc.tensor.matmul(bank[4 + j][0:R, :], zb[:, 0:R], zb[:, :], start=False, stop=True)
                    ins.then_inc(summed, 1)
                    pe.wait_ge(hist_ok, 1)
                    for j in range(2):
                        for k in range(2):
                            for half in range(2):
                                ins = nc.tensor.transpose(bank[j][:, (2 * k + half) * R:(2 * k + half + 1) * R],
                                                          hist[:, j, k * 256 + half * P:k * 256 + (half + 1) * P], ident[0:R, 0:R])
                    ins.then_inc(hist_t, 1)

        def edge_sums(tag, kind, W, sums):
            with nc.cleanup_on_exit(), ExitStack() as c, nc.Block() as block:
                tb = lambda name, shape, dt=f32: c.enter_context(nc.sbuf_tensor(tag + name, shape, dt))
                sm = lambda name: nc.alloc_semaphore(tag + name)
                two = lambda name: [sm(f"{name}{s}") for s in range(2)]
                drow = tb("drow", [P, 2, HS, P])
                same = tb("same", [P, 2, HS, P]); carry = tb("carry", [P, 2, HS, P])
                got = None
                if kind in ("typed", "gat"):
                    got = lent(rel_w, 2 * HS * F, lambda shape: tb("got", shape))
                msg = tb("msg", [P, 2, HS, W])
                tot = tb("tot", [P, 2, HS, W])
                src_st = tb("src_st", [P, 2, HS], i32); put_st = tb("put_st", [P, 2, HS], i32)
                ex = tb("ex", [P, 2, HS, HEADS]) if kind == "gat" else None
                zero = tb("zero", [P, 1848]) if kind == "wide" else None
                rows_in, side_in, gathered, src_ok, put_ok = two("rows_in"), two("side_in"), two("gathered"), two("src_ok"), two("put_ok")
                built, msg_ok, scat = two("built"), two("msg_ok"), two("scat")
                sums_ok, tot_ok, start0, go, exp_in, exp_ok = sm("sums_ok"), sm("tot_ok"), sm("start0"), sm("go"), two("exp_in"), two("exp_ok")
                zeroed = sm("zeroed"); z0 = sm("z0")
                uses_gather = kind != "gat"
                direct = kind in ("wide", "plain")
                gbuf = msg if direct else got
                PER = 16 * HS

                @block.sync
                def _(sp):
                    if kind == "wide":
                        sp.wait_ge(z0, 1)
                        per = 1848 // GATW
                        za = sums_a.rearrange("(g p r) f -> g p (r f)", p=P, r=per)
                        for g in range(za.shape[0]):
                            sp.dma_start(za[g], zero[:, 0:per * GATW]).then_inc(zeroed, 16)

                    def body(i, first, last):
                        for s in range(2):
                            at = i * BODY + s * HS
                            if not first:
                                sp.wait_ge(built[s], i)
                            sp.dma_start(drow[:, s, :, :].rearrange("p t q -> p (t q)"),
                                         dst_rows[bass.ds(at * P, HS * P)].rearrange("(o n) -> o n", o=1).to_broadcast((P, HS * P))).then_inc(rows_in[s], 16)
                            if kind == "wide":
                                if not first:
                                    sp.wait_ge(sums_ok, (i - 1) * BODY + (s + 1) * HS)
                                if not last or (i * BODY + s * HS + HS) <= FULL:
                                    sp.dma_start(msg[:, s, :, F:2 * F], tiles(a["edge_attr_64"][bass.ds(at * P, HS * P), :])).then_inc(side_in[s], 16)
                                else:
                                    n = FULL - at
                                    if n > 0:
                                        sp.dma_start(msg[:, s, 0:n, F:2 * F], tiles(a["edge_attr_64"][at * P:FULL * P, :])).then_inc(side_in[s], 16)
                                    if REM:
                                        sp.dma_start(msg[0:REM, s, n, F:2 * F], a["edge_attr_64"][FULL * P:N, :]).then_inc(side_in[s], 16)
                            if kind == "gat":
                                if not first:
                                    sp.wait_ge(msg_ok[s], i)
                                sp.dma_start(got[:, s, :, :], tiles(edge_h[bass.ds(at * P, HS * P), :])).then_inc(side_in[s], 16)
                    body(0, True, False)
                    with nc.sync.Fori(1, GI - 1) as i:
                        body(i, False, False)
                    body(GI - 1, False, True)
                    if kind == "wide":
                        sp.wait_ge(zeroed, 16 * (NP // P // (1848 // GATW)))

                def side_total(i, s, last):
                    if last and kind == "wide" and (i * BODY + s * HS + HS) > FULL:
                        n = FULL - (i * BODY + s * HS)
                        return 16 * i + 16 * ((1 if n > 0 else 0) + (1 if REM else 0))
                    return 16 * (i + 1)

                @block.gpsimd
                def _(pool):
                    def gather(i, s, first):
                        pool.wait_ge(src_ok[s], i + 1)
                        if not first:
                            if direct:
                                pool.wait_ge(sums_ok, (i - 1) * BODY + (s + 1) * HS)
                            else:
                                pool.wait_ge(msg_ok[s], i)
                        pool.sem_inc(go, 1)
                        for t in range(HS):
                            pool.indirect_dma_start(out=gbuf[:, s, t, 0:F], out_offset=None, in_=node_g,
                                                    in_offset=bass.IndirectOffsetOnAxis(ap=src_st[:, s, t:t + 1], axis=0)).then_inc(gathered[s], 16)

                    def scatter(i, s):
                        pool.wait_ge(put_ok[s], i + 1)
                        pool.wait_ge(tot_ok, i * BODY + (s + 1) * HS)
                        pool.sem_inc(go, 1)
                        for t in range(HS):
                            pool.indirect_dma_start(out=sums, out_offset=bass.IndirectOffsetOnAxis(ap=put_st[:, s, t:t + 1], axis=0),
                                                    in_=tot[:, s, t, :], in_offset=None, bounds_check=NP - 1, oob_is_err=False).then_inc(scat[s], 16)

                    def body(i, first, last):
                        if uses_gather:
                            gather(i, 1, first)
                        scatter(i, 0)
                        if uses_gather and not last:
                            gather(i + 1, 0, False)
                        scatter(i, 1)
                    if uses_gather:
                        gather(0, 0, True)
                    body(0, True, False)
                    with nc.gpsimd.Fori(1, GI - 1) as i:
                        body(i, False, False)
                    body(GI - 1, False, True)
                    for s in range(2):
                        pool.wait_ge(scat[s], PER * GI)

                @block.vector
                def _(dve):
                    v = nc.vector
                    if kind == "wide":
                        v.memset(zero[:, :], 0.0).then_inc(z0, 1)
                    v.memset(tot[:, 1, HS - 1, :], 0.0)
                    v.drain()
                    v.sem_inc(start0, 1)
                    if uses_gather:
                        for s in range(2):
                            v.tensor_copy(src_st[:, s, :], src_i[:, s * HS:(s + 1) * HS]).then_inc(src_ok[s], 1)

                    def body(i, first):
                        for s in range(2):
                            at = i * BODY + s * HS
                            dve.wait_ge(rows_in[s], 16 * (i + 1))
                            if not first:
                                dve.wait_ge(sums_ok, (i - 1) * BODY + (s + 1) * HS)
                            v.tensor_tensor(same[:, s, :, :], drow[:, s, :, :], dst_f[:, bass.ds(at, HS)].unsqueeze(2).to_broadcast((P, HS, P)), ALU.is_equal)
                            v.tensor_tensor(carry[:, s, :, :], drow[:, s, :, :], prev_f[:, bass.ds(at, HS)].unsqueeze(2).to_broadcast((P, HS, P)), ALU.is_equal).then_inc(built[s], 1)
                            if not first:
                                dve.wait_ge(scat[s], PER * i)
                                dve.wait_ge(start0, 1)
                            v.tensor_copy(put_st[:, s, :], put_i[:, bass.ds(at, HS)]).then_inc(put_ok[s], 1)
                            if kind == "typed":
                                dve.wait_ge(gathered[s], PER * (i + 1))
                                for r in range(2):
                                    ins = v.tensor_tensor(msg[:, s, :, r * F:(r + 1) * F], got[:, s, :, :],
                                                          rel[:, r, bass.ds(at, HS)].unsqueeze(2).to_broadcast((P, HS, F)), ALU.mult)
                                ins.then_inc(msg_ok[s], 1)
                            if kind == "gat":
                                v.tensor_tensor(ex[:, s, :, :], alpha[:, bass.ds(at, HS), :], amax[:, bass.ds(at, HS), :], ALU.subtract).then_inc(exp_in[s], 1)
                                v.tensor_tensor(msg[:, s, :, HF + HEADS:GATW], amax[:, bass.ds(at, HS), :],
                                                is_last[:, bass.ds(at, HS)].unsqueeze(2).to_broadcast((P, HS, HEADS)), ALU.mult)
                                dve.wait_ge(exp_ok[s], i + 1)
                                v.tensor_copy(msg[:, s, :, HF:HF + HEADS], ex[:, s, :, :])
                                dve.wait_ge(side_in[s], 16 * (i + 1))
                                for h in range(HEADS):
                                    ins = v.tensor_tensor(msg[:, s, :, h * F:(h + 1) * F], got[:, s, :, :],
                                                          ex[:, s, :, h:h + 1].to_broadcast((P, HS, F)), ALU.mult)
                                ins.then_inc(msg_ok[s], 1)
                            if uses_gather:
                                dve.wait_ge(gathered[s], PER * (i + 1))
                                dve.wait_ge(start0, 1)
                                v.tensor_copy(src_st[:, s, :], src_i[:, bass.ds(at + BODY, HS)]).then_inc(src_ok[s], 1)
                    body(0, True)
                    with v.Fori(1, GI) as i:
                        body(i, False)

                @block.tensor
                def _(pe):
                    pe.wait_ge(start0, 1)

                    def tile_sums(i, s, t, first):
                        k = i * BODY + s * HS + t
                        if not (first and s == 0):
                            pe.wait_ge(tot_ok, k - HS + 1)
                        nc.tensor.matmul(bank[t][:, 0:W], same[:, s, t, :], msg[:, s, t, :], start=True, stop=False)

                    def tile_carry(i, s, t, first):
                        k = i * BODY + s * HS + t
                        if not (first and s == 0 and t == 0):
                            pe.wait_ge(tot_ok, k)
                        prev = tot[:, s, t - 1, :] if t else tot[:, 1 - s, HS - 1, :]
                        nc.tensor.matmul(bank[t][:, 0:W], carry[:, s, t, :], prev, start=False, stop=True).then_inc(sums_ok, 1)

                    def body(i, first, last):
                        for s in range(2):
                            pe.wait_ge(built[s], i + 1)
                            if direct:
                                pe.wait_ge(gathered[s], PER * (i + 1))
                            if kind == "wide":
                                pe.wait_ge(side_in[s], side_total(i, s, last))
                            if not direct:
                                pe.wait_ge(msg_ok[s], i + 1)
                            tile_sums(i, s, 0, first)
                            for t in range(HS):
                                if t + 1 < HS:
                                    tile_sums(i, s, t + 1, first)
                                tile_carry(i, s, t, first)
                    body(0, True, False)
                    with nc.tensor.Fori(1, GI - 1) as i:
                        body(i, False, False)
                    body(GI - 1, False, True)

                @block.scalar
                def _(act):
                    act.wait_ge(start0, 1)

                    def body(i, first):
                        for s in range(2):
                            if kind == "gat":
                                act.wait_ge(exp_in[s], i + 1)
                                nc.scalar.activation(ex[:, s, :, :], ex[:, s, :, :], ACT.Exp).then_inc(exp_ok[s], 1)
                            if not first:
                                act.wait_ge(scat[s], PER * i)
                            for t in range(HS):
                                act.wait_ge(sums_ok, i * BODY + s * HS + t + 1)
                                nc.scalar.copy(tot[:, s, t, :], bank[t][:, 0:W]).then_inc(tot_ok, 1)
                    body(0, True)
                    with nc.scalar.Fori(1, GI) as i:
                        body(i, False)

        def nodes(tag, kind, layer=0):
            with nc.cleanup_on_exit(), ExitStack() as c, nc.Block() as block:
                tb = lambda name, shape, dt=f32: c.enter_context(nc.sbuf_tensor(tag + name, shape, dt))
                sm = lambda name: nc.alloc_semaphore(tag + name)
                two = lambda name: [sm(f"{name}{s}") for s in range(2)]
                adds = kind in ("conv", "sage", "bn")
                norms = kind in ("start", "conv", "sage", "bn")
                turn = {"conv": F, "sage": 2 * F, "rel": 2 * F}.get(kind, 0)
                inp = tb("inp", [P, 2, HS, turn or F])
                inp2 = tb("inp2", [P, 2, HS, F])
                inpT = tb("inpT", [P, 2, HS, P]); inp2T = tb("inp2T", [F, 2, HS, P])
                o = tb("o", [P, 2, HS, F])
                xc = tb("xc", [P, 2, HS, F]); sq = tb("sq", [P, 2, HS, F])
                st = tb("st", [P, 2, 4, HS])
                h = tb("h", [P, 2, HS, F]); g = tb("g", [P, 2, HS, F])
                loaded, tin, turned, tout = two("loaded"), two("tin"), two("turned"), two("tout")
                prod, xc_ok, sq_ok, var_ok, sd_ok, z_ok, h_ok, g_ok, stored = (two(n) for n in ("prod", "xc_ok", "sq_ok", "var_ok", "sd_ok", "z_ok", "h_ok", "g_ok", "stored"))
                used, o_free, go = two("used"), two("o_free"), sm("go")
                scaled = {"start": norm, "conv": rs_send}.get(kind)
                n_in = {"start": 0, "conv": 1, "sage": 3, "bn": 1, "rel": 2}[kind]
                n_out = 2 if kind == "conv" else 1
                final = kind == "rel" and layer == 2
                CH = [(0, 4), (4, HS)]

                @block.sync
                def _(sp):
                    def body(i, first):
                        for s in range(2):
                            at = bass.ds((i * BODY + s * HS) * P, HS * P)
                            if not first and n_in:
                                sp.wait_ge(used[s], i)
                            if kind == "conv":
                                sp.dma_start(inp[:, s, :, :], tiles(sums_w[at, 0:F])).then_inc(loaded[s], 16)
                            if kind == "sage":
                                sp.dma_start(inp[:, s, :, 0:F], tiles(node_h[at, :])).then_inc(loaded[s], 16)
                                sp.dma_start(inp[:, s, :, F:2 * F], tiles(sums_n[at, :])).then_inc(loaded[s], 16)
                                sp.dma_start(inp2[:, s, :, :], tiles(node_g[at, :])).then_inc(loaded[s], 16)
                            if kind == "bn":
                                sp.dma_start(inp2[:, s, :, :], tiles(gat_out[at, :])).then_inc(loaded[s], 16)
                            if kind == "rel":
                                sp.dma_start(inp[:, s, :, :], tiles(sums_w[at, :])).then_inc(loaded[s], 16)
                                sp.dma_start(inp2[:, s, :, :], tiles(node_g[at, :])).then_inc(loaded[s], 16)
                    if n_in:
                        body(0, True)
                        with nc.sync.Fori(1, GI) as i:
                            body(i, False)

                @block.gpsimd
                def _(pool):
                    pool.drain()
                    def body(i, first):
                        for s in range(2):
                            at = bass.ds((i * BODY + s * HS) * P, HS * P)
                            tl = bass.ds(i * BODY + s * HS, HS)
                            pool.wait_ge(h_ok[s], i + 1)
                            if scaled is not None:
                                pool.wait_ge(g_ok[s], i + 1)
                            pool.sem_inc(go, 1)
                            if kind == "conv":
                                pool.dma_start(tiles(node_h[at, :]), h[:, s, :, :]).then_inc(stored[s], 16)
                            if scaled is not None:
                                pool.dma_start(tiles(node_g[at, :]), g[:, s, :, :]).then_inc(stored[s], 16)
                            else:
                                pool.dma_start(tiles(node_g[at, :]), h[:, s, :, :]).then_inc(stored[s], 16)
                    if not final:
                        body(0, True)
                        with nc.gpsimd.Fori(1, GI) as i:
                            body(i, False)
                        for s in range(2):
                            pool.wait_ge(stored[s], 16 * n_out * GI)
                    else:
                        def tail(i, last):
                            for s in range(2):
                                at = i * BODY + s * HS
                                pool.wait_ge(h_ok[s], i + 1)
                                pool.sem_inc(go, 1)
                                if not last or at + HS <= FULL:
                                    pool.dma_start(tiles(out[bass.ds(at * P, HS * P), :]), h[:, s, :, :]).then_inc(stored[s], 16)
                                else:
                                    n = FULL - at
                                    if n > 0:
                                        pool.dma_start(tiles(out[at * P:FULL * P, :]), h[:, s, 0:n, :]).then_inc(stored[s], 16)
                                    if REM:
                                        pool.dma_start(out[FULL * P:N, :], h[0:REM, s, n, :]).then_inc(stored[s], 16)
                        with nc.gpsimd.Fori(0, GI - 1) as i:
                            tail(i, False)
                        tail(GI - 1, True)
                        for s in range(2):
                            at = (GI - 1) * BODY + s * HS
                            extra = 1 if at + HS <= FULL else (1 if FULL > at else 0) + (1 if REM else 0)
                            pool.wait_ge(stored[s], 16 * (GI - 1 + extra))

                @block.tensor
                def _(pe):
                    if not turn:
                        return
                    W = {"conv": W0[:, :], "sage": W1[:, :], "rel": W3[:, layer, :]}[kind]

                    def body(i, first):
                        for s in range(2):
                            pe.wait_ge(loaded[s], 16 * n_in * (i + 1))
                            if kind == "sage":
                                pe.wait_ge(tin[s], i + 1)
                            if not (first and s == 0):
                                pe.wait_ge(tout[1 - s], i + s)
                            pe.sem_inc(go, 1)
                            for b, (t0, t1) in enumerate(CH):
                                for t in range(t0, t1):
                                    ins = nc.tensor.transpose(bank[b][0:turn, (t - t0) * P:(t - t0 + 1) * P], inp[:, s, t, :], ident[:, :])
                            if kind == "rel":
                                for b, (t0, t1) in enumerate(CH):
                                    for t in range(t0, t1):
                                        ins = nc.tensor.transpose(bank[2 + b][0:F, (t - t0) * P:(t - t0 + 1) * P], inp2[:, s, t, :], ident[:, :])
                            ins.then_inc(turned[s], 1)
                            pe.wait_ge(tout[s], i + 1)
                            if not first:
                                pe.wait_ge(o_free[s], i)
                            for t in range(HS):
                                ins = nc.tensor.matmul(bank[4 + s][:, t * F:(t + 1) * F], inpT[0:turn, s, t, :], W, start=True, stop=kind != "rel")
                                if kind == "rel":
                                    ins = nc.tensor.matmul(bank[4 + s][:, t * F:(t + 1) * F], inp2T[:, s, t, :], Ws3[:, layer, :], start=False, stop=True)
                            ins.then_inc(prod[s], 1)
                    body(0, True)
                    with nc.tensor.Fori(1, GI) as i:
                        body(i, False)

                @block.scalar
                def _(act):
                    A = nc.scalar

                    def body(i, first):
                        if turn:
                            for s in range(2):
                                act.wait_ge(turned[s], i + 1)
                                if not first:
                                    act.wait_ge(prod[s], i)
                                for b, (t0, t1) in enumerate(CH):
                                    ins = A.copy(inpT[0:turn, s, t0:t1, :].rearrange("p t q -> p (t q)"), bank[b][0:turn, 0:(t1 - t0) * P])
                                    if kind == "rel":
                                        ins = A.copy(inp2T[:, s, t0:t1, :].rearrange("p t q -> p (t q)"), bank[2 + b][0:F, 0:(t1 - t0) * P])
                                ins.then_inc(tout[s], 1)
                        if norms:
                            for s in range(2):
                                act.wait_ge(xc_ok[s], i + 1)
                                A.activation(sq[:, s, :, :], xc[:, s, :, :], ACT.Square).then_inc(sq_ok[s], 1)
                            for s in range(2):
                                act.wait_ge(var_ok[s], i + 1)
                                A.activation(st[:, s, 2, :], st[:, s, 1, :], ACT.Sqrt, bias=eps[:, 0:1], scale=1.0 / F).then_inc(sd_ok[s], 1)
                        for s in range(2):
                            act.wait_ge(z_ok[s], i + 1)
                            if not first:
                                act.wait_ge(stored[s], 16 * n_out * i)
                            A.activation(h[:, s, :, :], xc[:, s, :, :], ACT.Copy if final else ACT.Relu).then_inc(h_ok[s], 1)
                    body(0, True)
                    with A.Fori(1, GI) as i:
                        body(i, False)

                @block.vector
                def _(dve):
                    v = nc.vector

                    def body(i, first):
                        tl = [bass.ds(i * BODY + s * HS, HS) for s in range(2)]
                        wide = lambda ap: ap.unsqueeze(2).to_broadcast((P, HS, F))
                        rowb = lambda ap: ap.unsqueeze(1).to_broadcast((P, HS, F))
                        if kind == "sage":
                            for s in range(2):
                                dve.wait_ge(loaded[s], 16 * n_in * (i + 1))
                                v.tensor_tensor(inp2[:, s, :, :], inp2[:, s, :, :], inp[:, s, :, F:2 * F], ALU.add)
                            v.drain()
                            for s in range(2):
                                v.tensor_tensor(inp[:, s, :, F:2 * F], inp2[:, s, :, :], wide(upd_scale[:, tl[s]]), ALU.mult).then_inc(tin[s], 1)
                        po = [bank[4 + s][:, 0:HS * F].rearrange("p (t f) -> p t f", t=HS) for s in range(2)]
                        if kind == "conv":
                            for s in range(2):
                                dve.wait_ge(prod[s], i + 1)
                                v.tensor_tensor(o[:, s, :, :], po[s], wide(norm[:, tl[s]]), ALU.mult).then_inc(o_free[s], 1)
                            v.drain()
                            for s in range(2):
                                v.tensor_tensor(o[:, s, :, :], o[:, s, :, :], rowb(b0[:, :]), ALU.add)
                            v.drain()
                            for s in range(2):
                                v.scalar_tensor_tensor(x_sb[:, tl[s], :], o[:, s, :, :], 0.0, x_sb[:, tl[s], :], ALU.max, ALU.add).then_inc(used[s], 1)
                            v.drain()
                        if kind == "sage":
                            for s in range(2):
                                dve.wait_ge(prod[s], i + 1)
                                v.tensor_tensor(o[:, s, :, :], po[s], rowb(b1[:, :]), ALU.add).then_inc(o_free[s], 1)
                            v.drain()
                            for s in range(2):
                                v.tensor_tensor(x_sb[:, tl[s], :], o[:, s, :, :], x_sb[:, tl[s], :], ALU.add).then_inc(used[s], 1)
                            v.drain()
                        if kind == "rel":
                            for s in range(2):
                                dve.wait_ge(prod[s], i + 1)
                                if not first:
                                    dve.wait_ge(h_ok[s], i)
                                v.tensor_tensor(o[:, s, :, :] if final else xc[:, s, :, :], po[s], rowb(b3[:, layer, :]), ALU.add).then_inc(o_free[s], 1)
                            v.drain()
                            for s in range(2):
                                if final:
                                    v.tensor_tensor(xc[:, s, :, :], o[:, s, :, :], x_sb[:, tl[s], :], ALU.add).then_inc(z_ok[s], 1)
                                else:
                                    v.sem_inc(z_ok[s], 1)
                                v.sem_inc(used[s], 1)
                            return
                        if kind == "bn":
                            for s in range(2):
                                dve.wait_ge(loaded[s], 16 * n_in * (i + 1))
                                v.tensor_tensor(o[:, s, :, :], inp2[:, s, :, :], rowb(mu[:, :]), ALU.subtract).then_inc(used[s], 1)
                            v.drain()
                            for s in range(2):
                                v.tensor_tensor(o[:, s, :, :], o[:, s, :, :], rowb(bn_a[:, :]), ALU.mult)
                            v.drain()
                            for s in range(2):
                                v.tensor_tensor(o[:, s, :, :], o[:, s, :, :], rowb(beta[:, :]), ALU.add)
                            v.drain()
                            for s in range(2):
                                v.scalar_tensor_tensor(x_sb[:, tl[s], :], o[:, s, :, :], 0.0, x_sb[:, tl[s], :], ALU.max, ALU.add)
                            v.drain()
                        for s in range(2):
                            v.tensor_reduce(st[:, s, 0, :], x_sb[:, tl[s], :], AX.X, ALU.add)
                        v.drain()
                        for s in range(2):
                            if not first:
                                dve.wait_ge(h_ok[s], i)
                            v.scalar_tensor_tensor(xc[:, s, :, :], wide(st[:, s, 0, :]), -1.0 / F, x_sb[:, tl[s], :], ALU.mult, ALU.add).then_inc(xc_ok[s], 1)
                        for s in range(2):
                            dve.wait_ge(sq_ok[s], i + 1)
                            v.tensor_reduce(st[:, s, 1, :], sq[:, s, :, :], AX.X, ALU.add).then_inc(var_ok[s], 1)
                        for s in range(2):
                            dve.wait_ge(sd_ok[s], i + 1)
                            v.reciprocal(st[:, s, 3, :], st[:, s, 2, :])
                        v.drain()
                        for s in range(2):
                            v.tensor_tensor(xc[:, s, :, :], xc[:, s, :, :], wide(st[:, s, 3, :]), ALU.mult).then_inc(z_ok[s], 1)
                        if scaled is not None:
                            for s in range(2):
                                dve.wait_ge(h_ok[s], i + 1)
                                if not first:
                                    dve.wait_ge(stored[s], 16 * n_out * i)
                                v.tensor_tensor(g[:, s, :, :], h[:, s, :, :], wide(scaled[:, tl[s]]), ALU.mult).then_inc(g_ok[s], 1)
                    body(0, True)
                    with v.Fori(1, GI) as i:
                        body(i, False)

        def edge_scores(tag):
            with nc.cleanup_on_exit(), ExitStack() as c, nc.Block() as block:
                tb = lambda name, shape, dt=f32: c.enter_context(nc.sbuf_tensor(tag + name, shape, dt))
                sm = lambda name: nc.alloc_semaphore(tag + name)
                two = lambda name: [sm(f"{name}{s}") for s in range(2)]
                PAIRS, ZB = BODY // 2, 4
                cat = tb("cat", [P, 2, HS, 2 * F]); ea = tb("ea", [P, 2, HS, F])
                catT = tb("catT", [P, 2, P]); eaT = tb("eaT", [F + 1, 2, P])
                y = tb("y", [P, ZB, 2 * HF]); act_z = tb("act_z", [P, 2 * HF]); prod = tb("prod", [P, 2 * HF])
                al = tb("al", [P, BODY, HEADS])
                src_st = tb("src_st", [P, 2, HS], i32); dst_st = tb("dst_st", [P, 2, HS], i32)
                gathered, idx_ok, ea_in, kept = two("gathered"), two("idx_ok"), two("ea_in"), two("kept")
                ones_ok, tr_ok, copied, z_ok, y_ok, z_used, go = (sm(n) for n in ("ones_ok", "tr_ok", "copied", "z_ok", "y_ok", "z_used", "go"))
                PER = 2 * 16 * HS

                def ea_total(i, s, last):
                    n = FULL - (GI - 1) * BODY - s * HS
                    if last and n < HS:
                        return 16 * (GI - 1) + 16 * ((1 if n > 0 else 0) + (1 if REM else 0))
                    return 16 * (i + 1)

                @block.sync
                def _(sp):
                    def body(i, first, last):
                        for s in range(2):
                            at = i * BODY + s * HS
                            if not first:
                                sp.wait_ge(tr_ok, (i - 1) * BODY + (s + 1) * HS)
                            if not last or at + HS <= FULL:
                                sp.dma_start(ea[:, s, :, :], tiles(a["edge_attr_64"][bass.ds(at * P, HS * P), :])).then_inc(ea_in[s], 16)
                            else:
                                n = FULL - at
                                if n > 0:
                                    sp.dma_start(ea[:, s, 0:n, :], tiles(a["edge_attr_64"][at * P:FULL * P, :])).then_inc(ea_in[s], 16)
                                if REM:
                                    sp.dma_start(ea[0:REM, s, n, :], a["edge_attr_64"][FULL * P:N, :]).then_inc(ea_in[s], 16)
                        for s in range(2):
                            sp.wait_ge(gathered[s], PER * (i + 1))
                            sp.dma_start(tiles(edge_h[bass.ds((i * BODY + s * HS) * P, HS * P), :]), cat[:, s, :, 0:F]).then_inc(kept[s], 16)
                    body(0, True, False)
                    with nc.sync.Fori(1, GI - 1) as i:
                        body(i, False, False)
                    body(GI - 1, False, True)
                    for s in range(2):
                        sp.wait_ge(kept[s], 16 * GI)

                @block.gpsimd
                def _(pool):
                    def gather(i, s, first):
                        pool.wait_ge(idx_ok[s], i + 1)
                        if not first:
                            pool.wait_ge(kept[s], 16 * i)
                            pool.wait_ge(tr_ok, (i - 1) * BODY + (s + 1) * HS)
                        pool.sem_inc(go, 1)
                        for t in range(HS):
                            pool.indirect_dma_start(out=cat[:, s, t, 0:F], out_offset=None, in_=node_g,
                                                    in_offset=bass.IndirectOffsetOnAxis(ap=src_st[:, s, t:t + 1], axis=0)).then_inc(gathered[s], 16)
                            pool.indirect_dma_start(out=cat[:, s, t, F:2 * F], out_offset=None, in_=node_g,
                                                    in_offset=bass.IndirectOffsetOnAxis(ap=dst_st[:, s, t:t + 1], axis=0)).then_inc(gathered[s], 16)
                    for s in range(2):
                        gather(0, s, True)
                    with nc.gpsimd.Fori(1, GI) as i:
                        for s in range(2):
                            gather(i, s, False)

                @block.tensor
                def _(pe):
                    pe.wait_ge(ones_ok, 1)

                    def turn(i, k, first, last):
                        s, t = k // HS, k % HS
                        if t == 0:
                            pe.wait_ge(gathered[s], PER * (i + 1))
                            pe.wait_ge(ea_in[s], ea_total(i, s, last))
                        if not (first and k < 2):
                            pe.wait_ge(copied, i * BODY + k - 1)
                        nc.tensor.transpose(bank[k % 2][:, 0:P], cat[:, s, t, :], ident[:, :])
                        nc.tensor.transpose(bank[k % 2][0:F, P:2 * P], ea[:, s, t, :], ident[:, :]).then_inc(tr_ok, 1)

                    def score(i, k, first):
                        q = k // 2
                        if k % 2 == 0 and not (first and q < ZB):
                            before = q - ZB + 1 if q >= ZB else max(j for j in range(PAIRS) if j % ZB == q % ZB) + 1 - PAIRS
                            pe.wait_ge(z_used, i * PAIRS + before)
                        pe.wait_ge(copied, i * BODY + k + 1)
                        zk = bank[2 + q % ZB][:, (k % 2) * HF:(k % 2 + 1) * HF]
                        nc.tensor.matmul(zk, catT[:, k % 2, :], Wlr[:, :], start=True, stop=False)
                        nc.tensor.matmul(zk, eaT[:, k % 2, :], Wea[:, :], start=False, stop=True).then_inc(z_ok, 1)

                    def body(i, first, last):
                        turn(i, 0, first, last)
                        for k in range(BODY):
                            if k + 1 < BODY:
                                turn(i, k + 1, first, last)
                            score(i, k, first)
                    body(0, True, False)
                    with nc.tensor.Fori(1, GI - 1) as i:
                        body(i, False, False)
                    body(GI - 1, False, True)

                @block.scalar
                def _(act):
                    A = nc.scalar

                    def slopes(i, q, first):
                        act.wait_ge(z_ok, i * BODY + 2 * q + 2)
                        if not (first and q < ZB):
                            before = q - ZB + 1 if q >= ZB else max(j for j in range(PAIRS) if j % ZB == q % ZB) + 1 - PAIRS
                            act.wait_ge(z_used, i * PAIRS + before)
                        A.mul(y[:, q % ZB, :], bank[2 + q % ZB][:, :], SLOPE).then_inc(y_ok, 1)

                    def body(i, first):
                        for k in range(BODY):
                            act.wait_ge(tr_ok, i * BODY + k + 1)
                            if not (first and k < 2):
                                act.wait_ge(z_ok, i * BODY + k - 1)
                            A.copy(catT[:, k % 2, :], bank[k % 2][:, 0:P])
                            A.copy(eaT[0:F, k % 2, :], bank[k % 2][0:F, P:2 * P]).then_inc(copied, 1)
                            if k % 2 == 0 and k:
                                slopes(i, k // 2 - 1, first)
                        slopes(i, PAIRS - 1, first)
                    body(0, True)
                    with A.Fori(1, GI) as i:
                        body(i, False)

                @block.vector
                def _(dve):
                    v = nc.vector
                    v.memset(eaT[F:F + 1, :, :], 1.0).then_inc(ones_ok, 1)
                    for s in range(2):
                        v.tensor_copy(src_st[:, s, :], src_i[:, s * HS:(s + 1) * HS])
                        v.tensor_copy(dst_st[:, s, :], dst_i[:, s * HS:(s + 1) * HS]).then_inc(idx_ok[s], 1)

                    def body(i, first):
                        for q in range(PAIRS):
                            dve.wait_ge(y_ok, i * PAIRS + q + 1)
                            v.tensor_tensor(act_z[:, :], bank[2 + q % ZB][:, :], y[:, q % ZB, :], ALU.max).then_inc(z_used, 1)
                            v.drain()
                            v.tensor_tensor(prod[:, :].rearrange("p (t c) -> p t c", t=2), act_z[:, :].rearrange("p (t c) -> p t c", t=2),
                                            attb[:, :].unsqueeze(1).to_broadcast((P, 2, HF)), ALU.mult)
                            v.drain()
                            v.tensor_reduce(al[:, 2 * q:2 * q + 2, :], prod[:, :].rearrange("p (t h f) -> p t h f", t=2, h=HEADS), AX.X, ALU.add)
                            if q in (3, PAIRS - 1):
                                s = 0 if q == 3 else 1
                                at = i * BODY + s * HS + BODY
                                v.drain()
                                dve.wait_ge(gathered[s], PER * (i + 1))
                                v.tensor_copy(src_st[:, s, :], src_i[:, bass.ds(at, HS)])
                                v.tensor_copy(dst_st[:, s, :], dst_i[:, bass.ds(at, HS)]).then_inc(idx_ok[s], 1)
                        v.drain()
                        v.tensor_copy(alpha[:, bass.ds(i * BODY, BODY), :], al[:, :, :])
                        v.drain()
                    body(0, True)
                    with v.Fori(1, GI) as i:
                        body(i, False)

        def segment_max(tag, windows):
            with nc.cleanup_on_exit(), ExitStack() as c, nc.Block() as block:
                tb = lambda name, shape, dt=f32: c.enter_context(nc.sbuf_tensor(tag + name, shape, dt))
                sm = lambda name: nc.alloc_semaphore(tag + name)
                W = NBLK * P
                key = tb("key", [R, NBLK, P]); pen = tb("pen", [R, 2, NBLK, P]); penf, penb = pen[:, 0], pen[:, 1]
                mf = tb("mf", [R, HEADS, W]); mb = tb("mb", [R, HEADS, W]); m = tb("m", [R, HEADS, NBLK, P])
                ekey = tb("ekey", [HEADS, 2 * T]); e = tb("e", [HEADS, 2 * T]); ef = tb("ef", [HEADS, 2 * T]); eb = tb("eb", [HEADS, 2 * T])
                epf, epb = (mb[0:HEADS, :, :].rearrange("r h w -> r (h w)")[:, k * 2 * T:(k + 1) * 2 * T] for k in range(2))
                back = tb("back", [R, HEADS, NBLK, 2]); off = pen
                nxt = tb("nxt", [R, NBLK, P]) if windows else None
                exps, lasts = mf, mb
                cand = mf[:, 0:2, :].rearrange("r s (b p) -> r s b p", p=P)
                nxt_in, x_ok, lasts_ok, exp_ok, x_out = (sm(n) for n in ("nxt_in", "x_ok", "lasts_ok", "exp_ok", "x_out"))
                key_in, turned, ends_ok, ends_out, e_in, em_ok, em_out, back_in, m_ok, backT = (
                    sm(n) for n in ("key_in", "turned", "ends_ok", "ends_out", "e_in", "em_ok", "em_out", "back_in", "m_ok", "backT"))

                @block.sync
                def _(sp):
                    sp.dma_start(key[:, :, :], dst_rows[0:NP].rearrange("(b r p) -> r b p", r=R, p=P)).then_inc(key_in, 16)
                    sp.wait_ge(key_in, 16)
                    with nc.allow_non_contiguous_dma(reason="two values a tile"):
                        for side in range(2):
                            col = side * (P - 1)
                            sp.dma_start(ends_k[:, side].rearrange("(b r) -> r b", r=R), key[:, :, col]).then_inc(ends_out, 16)
                        sp.wait_ge(ends_ok, 1)
                        for h in range(HEADS):
                            for side in range(2):
                                col = side * (P - 1)
                                sp.dma_start(ends_d[h, :, side].rearrange("(b r) -> r b", r=R), m[:, h, :, col]).then_inc(ends_out, 16)
                        sp.wait_ge(ends_out, 16 * (2 + 2 * HEADS))
                        sp.dma_start(e[:, :], ends_d.rearrange("h t l -> h (t l)")).then_inc(e_in, 16)
                        sp.dma_start(ekey[:, :], ends_k.rearrange("(o t) l -> o (t l)", o=1).to_broadcast((HEADS, 2 * T))).then_inc(e_in, 16)
                        sp.wait_ge(em_ok, 1)
                        sp.dma_start(ends_m.rearrange("h t l -> h (t l)"), e[:, :]).then_inc(em_out, 16)
                        sp.wait_ge(em_out, 16)
                        for h in range(HEADS):
                            sp.dma_start(back[:, h, :, :], ends_m[h].rearrange("(b r) l -> r b l", r=R)).then_inc(back_in, 16)
                    if windows:
                        sp.dma_start(nxt[:, :, :], dst_rows[1:NP + 1].rearrange("(b r p) -> r b p", r=R, p=P)).then_inc(nxt_in, 16)
                        for lo in [0] + [FRONT + NP + k * P for k in range(WT)]:
                            sp.dma_start(exp_all[:, lo:lo + P], zeros_w[0:2 * HEADS, 0:P]).then_inc(x_out, 16)
                        rows_of = lambda c: exp_all[c, FRONT:FRONT + NP].rearrange("(b r p) -> r b p", r=R, p=P)
                        sp.wait_ge(lasts_ok, 1)
                        for h in range(HEADS):
                            sp.dma_start(rows_of(HEADS + h), lasts[:, h, :].rearrange("r (b p) -> r b p", p=P)).then_inc(x_out, 16)
                        sp.wait_ge(exp_ok, 1)
                        for h in range(HEADS):
                            sp.dma_start(rows_of(h), exps[:, h, :].rearrange("r (b p) -> r b p", p=P)).then_inc(x_out, 16)
                        sp.wait_ge(x_out, 16 * (1 + WT + 2 * HEADS))

                if windows:
                    @block.scalar
                    def _(act):
                        act.wait_ge(x_ok, 1)
                        nc.scalar.activation(exps[:, :, :], exps[:, :, :], ACT.Exp).then_inc(exp_ok, 1)

                @block.tensor
                def _(pe):
                    for h in range(HEADS):
                        for b in range(NBLK):
                            ins = nc.tensor.transpose(bank[h][0:R, b * P:(b + 1) * P], alpha[:, b * R:(b + 1) * R, h], ident[:, :])
                    ins.then_inc(turned, 1)
                    if windows:
                        return
                    pe.wait_ge(m_ok, 1)
                    for h in range(HEADS):
                        for b in range(NBLK):
                            ins = nc.tensor.transpose(bank[4 + h][:, b * R:(b + 1) * R], m[:, h, b, :], ident[0:R, 0:R])
                    ins.then_inc(backT, 1)

                @block.vector
                def _(dve):
                    v = nc.vector
                    dve.wait_ge(key_in, 16)
                    v.memset(penf[:, :, 0:1], NEG)
                    v.memset(penb[:, :, P - 1:P], NEG)
                    v.tensor_tensor(penf[:, :, 1:P], key[:, :, 1:P], key[:, :, 0:P - 1], ALU.not_equal)
                    v.tensor_tensor(penb[:, :, 0:P - 1], key[:, :, 0:P - 1], key[:, :, 1:P], ALU.not_equal)
                    v.drain()
                    v.tensor_scalar(penf[:, :, 1:P], penf[:, :, 1:P], NEG, None, ALU.mult)
                    v.tensor_scalar(penb[:, :, 0:P - 1], penb[:, :, 0:P - 1], NEG, None, ALU.mult)
                    dve.wait_ge(turned, 1)
                    v.drain()
                    pf, pb = penf[:, :, :].rearrange("r b p -> r (b p)"), penb[:, :, :].rearrange("r b p -> r (b p)")
                    for h in range(HEADS):
                        v.tensor_tensor_scan(mf[:, h, :], pf, bank[h][0:R, :], NEG, ALU.add, ALU.max)
                        v.tensor_tensor_scan(mb[:, h, W - 1::-1], pb[:, W - 1::-1], bank[h][0:R, W - 1::-1], NEG, ALU.add, ALU.max)
                    v.drain()
                    v.tensor_tensor(m[:, :, :, :].rearrange("r h b p -> r (h b p)"), mf[:, :, :].rearrange("r h w -> r (h w)"),
                                    mb[:, :, :].rearrange("r h w -> r (h w)"), ALU.max).then_inc(ends_ok, 1)
                    for side in range(2):
                        col = side * (P - 1)
                        v.tensor_tensor(off[:, side, :, :], key[:, :, :], key[:, :, col:col + 1].to_broadcast((R, NBLK, P)), ALU.not_equal)
                    dve.wait_ge(e_in, 32)
                    L = 2 * T
                    v.drain()
                    v.memset(epf[:, 0:1], NEG)
                    v.memset(epb[:, L - 1:L], NEG)
                    v.tensor_tensor(epf[:, 1:L], ekey[:, 1:L], ekey[:, 0:L - 1], ALU.not_equal)
                    v.tensor_tensor(epb[:, 0:L - 1], ekey[:, 0:L - 1], ekey[:, 1:L], ALU.not_equal)
                    v.drain()
                    v.tensor_scalar(epf[:, 1:L], epf[:, 1:L], NEG, None, ALU.mult)
                    v.tensor_scalar(epb[:, 0:L - 1], epb[:, 0:L - 1], NEG, None, ALU.mult)
                    v.drain()
                    v.tensor_tensor_scan(ef[:, :], epf[:, :], e[:, :], NEG, ALU.add, ALU.max)
                    v.tensor_tensor_scan(eb[:, L - 1::-1], epb[:, L - 1::-1], e[:, L - 1::-1], NEG, ALU.add, ALU.max)
                    v.drain()
                    v.tensor_tensor(e[:, :], ef[:, :], eb[:, :], ALU.max).then_inc(em_ok, 1)
                    dve.wait_ge(back_in, 16 * HEADS)
                    for h in range(HEADS):
                        for side in range(2):
                            v.drain()
                            v.scalar_tensor_tensor(cand[:, side, :, :], off[:, side, :, :], NEG, back[:, h, :, side:side + 1].to_broadcast((R, NBLK, P)), ALU.mult, ALU.add)
                            v.drain()
                            ins = v.tensor_tensor(m[:, h, :, :], m[:, h, :, :], cand[:, side, :, :], ALU.max)
                    ins.then_inc(m_ok, 1)
                    if windows:
                        dve.wait_ge(nxt_in, 16)
                        v.drain()
                        v.tensor_tensor(nxt[:, :, :], key[:, :, :], nxt[:, :, :], ALU.not_equal)
                        for h in range(HEADS):
                            v.tensor_tensor(exps[:, h, :], bank[h][0:R, :], m[:, h, :, :].rearrange("r b p -> r (b p)"), ALU.subtract)
                        v.drain()
                        v.sem_inc(x_ok, 1)
                        for h in range(HEADS):
                            v.tensor_tensor(lasts[:, h, :].rearrange("r (b p) -> r b p", p=P), m[:, h, :, :], nxt[:, :, :], ALU.mult)
                        v.drain()
                        v.sem_inc(lasts_ok, 1)
                        return
                    dve.wait_ge(backT, 1)
                    for h in range(HEADS):
                        v.tensor_copy(amax[:, :, h], bank[4 + h][:, 0:T])

        def attend(tag):
            with nc.cleanup_on_exit(), ExitStack() as c, nc.Block() as block:
                tb = lambda name, shape, dt=f32: c.enter_context(nc.sbuf_tensor(tag + name, shape, dt))
                sm = lambda name: nc.alloc_semaphore(tag + name)
                two = lambda name: [sm(f"{name}{s}") for s in range(2)]
                cat = tb("cat", [P, 2, HS, 2 * F]); sums = tb("sums", [P, 2, HS, GATW])
                catT = tb("catT", [P, HS, P]); aggT = tb("aggT", [P, HS, 2, P])
                y = tb("y", [P, HS * HF]); z = tb("z", [P, HS * HF])
                own = tb("own", [P, HS, HEADS]); me = tb("me", [P, HS, HEADS]); mm = tb("mm", [P, HS, HEADS])
                d = tb("d", [P, 2, HS, HEADS]); den = tb("den", [P, HS, HEADS]); cc = tb("cc", [P, 2, HS, HEADS])
                o = tb("o", [P, 2, HS, F])
                loaded, scaled, turned, copied, z_ok, y_ok, z_used, d_ok, e_ok, agg_ok, aT, aT_copied, prod, o_ok, stored, stat, used, first_z, stat_end, go = (
                    sm(n) for n in ("loaded", "scaled", "turned", "copied", "z_ok", "y_ok", "z_used", "d_ok", "e_ok", "agg_ok", "aT", "aT_copied", "prod", "o_ok",
                                    "stored", "stat", "used", "first_z", "stat_end", "go"))
                loads, st_s = two("loads"), two("st_s")
                GROUPS = [(0, 2), (2, 4), (4, 6), (6, HS)]
                CH = [(0, 4), (4, HS)]
                AC = [(0, 4), (4, 8), (8, 12), (12, 14)]

                @block.sync
                def _(sp):
                    def body(i, first):
                        for s in range(2):
                            at = bass.ds((i * BODY + s * HS) * P, HS * P)
                            if not first:
                                sp.wait_ge(used, 2 * i + s - 1)
                            sp.dma_start(cat[:, s, :, 0:F], tiles(node_g[at, :])).then_inc(loads[s], 16)
                            sp.dma_start(cat[:, s, :, F:2 * F], tiles(sums_w[at, F:2 * F])).then_inc(loads[s], 16)
                            sp.dma_start(sums[:, s, :, :], tiles(sums_a[at, :])).then_inc(loads[s], 16)
                    body(0, True)
                    with nc.sync.Fori(1, GI) as i:
                        body(i, False)

                @block.gpsimd
                def _(pool):
                    with nc.gpsimd.Fori(0, GI) as i:
                        for s in range(2):
                            pool.wait_ge(o_ok, 2 * i + s + 1)
                            pool.sem_inc(go, 1)
                            pool.dma_start(tiles(gat_out[bass.ds((i * BODY + s * HS) * P, HS * P), :]), o[:, s, :, :]).then_inc(st_s[s], 16)
                    for s in range(2):
                        pool.wait_ge(st_s[s], 16 * GI)

                @block.tensor
                def _(pe):
                    nc.tensor.matmul(bank[7][:, 0:HS * F], zeros_w[:, 0:P], zeros_w[:, 0:HS * F], start=True, stop=False)

                    def body(i, first):
                        for s in range(2):
                            n = 2 * i + s
                            pe.wait_ge(scaled, n + 1)
                            if not (first and s == 0):
                                pe.wait_ge(aT_copied, 4 * n)
                            pe.sem_inc(go, 1)
                            for b, (t0, t1) in enumerate(CH):
                                for t in range(t0, t1):
                                    ins = nc.tensor.transpose(bank[b][:, (t - t0) * P:(t - t0 + 1) * P], cat[:, s, t, :], ident[:, :])
                            ins.then_inc(turned, 1)
                            pe.wait_ge(copied, n + 1)
                            for j, (t0, t1) in enumerate(GROUPS):
                                if not (first and s == 0):
                                    pe.wait_ge(z_used, n)
                                for t in range(t0, t1):
                                    zt = bank[2 + j][:, (t - t0) * HF:(t - t0 + 1) * HF]
                                    nc.tensor.matmul(zt, catT[:, t, :], Wself[:, :], start=True, stop=False)
                                    ins = nc.tensor.matmul(zt, ones1[:, :], b_sum[:, :], start=False, stop=True)
                                ins.then_inc(z_ok, 1)
                            pe.wait_ge(agg_ok, n + 1)
                            for j, (k0, k1) in enumerate(AC):
                                if j >= 2:
                                    pe.wait_ge(aT_copied, 4 * n + j - 1)
                                    pe.sem_inc(go, 1)
                                for k in range(k0, k1):
                                    ins = nc.tensor.transpose(bank[j % 2][:, (k - k0) * P:(k - k0 + 1) * P], sums[:, s, k // 2, (k % 2) * P:(k % 2 + 1) * P], ident[:, :])
                                ins.then_inc(aT, 1)
                            pe.wait_ge(aT_copied, 4 * n + 4)
                            for t in range(HS):
                                for q in range(2):
                                    ins = nc.tensor.matmul(bank[6][:, t * F:(t + 1) * F], aggT[:, t, q, :], Wst[:, q, :], start=(q == 0), stop=(q == 1))
                            ins.then_inc(prod, 1)
                            pe.wait_ge(o_ok, n + 1)
                            nc.tensor.matmul(bank[7][:, 0:HS * F], onesP[:, :], o[:, s, :, :].rearrange("p t f -> p (t f)"), start=False, stop=False).then_inc(stat, 1)
                    body(0, True)
                    with nc.tensor.Fori(1, GI) as i:
                        body(i, False)
                    nc.tensor.matmul(bank[7][:, 0:HS * F], zeros_w[:, 0:P], zeros_w[:, 0:HS * F], start=False, stop=True).then_inc(stat_end, 1)

                @block.scalar
                def _(act):
                    A = nc.scalar

                    def body(i, first):
                        for s in range(2):
                            n = 2 * i + s
                            act.wait_ge(turned, n + 1)
                            for b, (t0, t1) in enumerate(CH):
                                ins = A.copy(catT[:, t0:t1, :].rearrange("p t q -> p (t q)"), bank[b][:, 0:(t1 - t0) * P])
                            ins.then_inc(copied, 1)
                            for j, (t0, t1) in enumerate(GROUPS):
                                act.wait_ge(z_ok, 4 * n + j + 1)
                                if not (first and s == 0):
                                    act.wait_ge(z_used, n)
                                A.mul(y[:, t0 * HF:t1 * HF], bank[2 + j][:, 0:(t1 - t0) * HF], SLOPE).then_inc(y_ok, 1)
                            act.wait_ge(d_ok, n + 1)
                            A.activation(d[:, :, :, :], d[:, :, :, :], ACT.Exp).then_inc(e_ok, 1)
                            for j, (k0, k1) in enumerate(AC):
                                act.wait_ge(aT, 4 * n + j + 1)
                                A.copy(aggT[:, :, :, :].rearrange("p t q c -> p (t q c)")[:, k0 * P:k1 * P], bank[j % 2][:, 0:(k1 - k0) * P]).then_inc(aT_copied, 1)
                    body(0, True)
                    with A.Fori(1, GI) as i:
                        body(i, False)

                @block.vector
                def _(dve):
                    v = nc.vector

                    def body(i, first):
                        for s in range(2):
                            n = 2 * i + s
                            at = bass.ds(i * BODY + s * HS, HS)
                            sm_ = sums[:, s, :, :]
                            heads = lambda ap: ap.unsqueeze(2).to_broadcast((P, HS, HEADS))
                            dve.wait_ge(loads[s], 48 * (i + 1))
                            v.tensor_tensor(cat[:, s, :, F:2 * F], cat[:, s, :, F:2 * F], inv_cnt[:, at].unsqueeze(2).to_broadcast((P, HS, F)), ALU.mult).then_inc(scaled, 1)
                            v.tensor_tensor(me[:, :, :], sm_[:, :, HF + HEADS:GATW], heads(no_edge[:, at]), ALU.add)
                            for j, (t0, t1) in enumerate(GROUPS):
                                dve.wait_ge(y_ok, 4 * n + j + 1)
                                ins = v.tensor_tensor(z[:, t0 * HF:t1 * HF], bank[2 + j][:, 0:(t1 - t0) * HF], y[:, t0 * HF:t1 * HF], ALU.max)
                            ins.then_inc(z_used, 1)
                            v.drain()
                            zz = z[:, :].rearrange("p (t c) -> p t c", t=HS)
                            v.tensor_tensor(zz, zz, attb[:, :].unsqueeze(1).to_broadcast((P, HS, HF)), ALU.mult)
                            v.drain()
                            v.tensor_reduce(own[:, :, :], z[:, :].rearrange("p (t h f) -> p t h f", t=HS, h=HEADS), AX.X, ALU.add)
                            v.drain()
                            v.tensor_tensor(mm[:, :, :], me[:, :, :], own[:, :, :], ALU.max)
                            v.drain()
                            v.tensor_tensor(d[:, 0, :, :], me[:, :, :], mm[:, :, :], ALU.subtract)
                            v.tensor_tensor(d[:, 1, :, :], own[:, :, :], mm[:, :, :], ALU.subtract).then_inc(d_ok, 1)
                            dve.wait_ge(e_ok, n + 1)
                            v.tensor_tensor(den[:, :, :], sm_[:, :, HF:HF + HEADS], d[:, 0, :, :], ALU.mult)
                            v.drain()
                            v.tensor_tensor(den[:, :, :], den[:, :, :], d[:, 1, :, :], ALU.add)
                            v.drain()
                            v.tensor_scalar(den[:, :, :], den[:, :, :], SM_EPS, None, ALU.add)
                            v.drain()
                            v.reciprocal(den[:, :, :], den[:, :, :])
                            v.drain()
                            for q in range(2):
                                v.tensor_tensor(cc[:, q, :, :], d[:, q, :, :], den[:, :, :], ALU.mult)
                            v.drain()
                            num = sm_[:, :, 0:HF].rearrange("p t (h f) -> p t h f", h=HEADS)
                            z4 = z[:, :].rearrange("p (t h f) -> p t h f", t=HS, h=HEADS)
                            for h in range(HEADS):
                                v.tensor_tensor(num[:, :, h, :], num[:, :, h, :], cc[:, 0, :, h:h + 1].to_broadcast((P, HS, F)), ALU.mult)
                                v.tensor_tensor(z4[:, :, h, :], cat[:, s, :, 0:F], cc[:, 1, :, h:h + 1].to_broadcast((P, HS, F)), ALU.mult)
                            v.drain()
                            v.tensor_tensor(sm_[:, :, 0:HF], sm_[:, :, 0:HF], zz, ALU.add).then_inc(agg_ok, 1)
                            dve.wait_ge(prod, n + 1)
                            v.sem_inc(used, 1)
                            if not first:
                                dve.wait_ge(st_s[s], 16 * i)
                                dve.wait_ge(stat, n - 1)
                            v.tensor_scalar(o[:, s, :, :].rearrange("p t f -> p (t f)"), bank[6][:, 0:HS * F], 1.0 / HEADS, None, ALU.mult)
                            v.drain()
                            v.tensor_tensor(o[:, s, :, :], o[:, s, :, :], b2[:, :].unsqueeze(1).to_broadcast((P, HS, F)), ALU.add)
                            v.drain()
                            v.tensor_tensor(o[:, s, :, :], o[:, s, :, :], real[:, at].unsqueeze(2).to_broadcast((P, HS, F)), ALU.mult).then_inc(o_ok, 1)
                    body(0, True)
                    with v.Fori(1, GI) as i:
                        body(i, False)
                    dve.wait_ge(stat_end, 1)
                    v.tensor_reduce(mu[:, :], bank[7][:, 0:HS * F].rearrange("p (t f) -> p f t", t=HS), AX.X, ALU.add)
                    v.drain()
                    v.tensor_scalar(mu[:, :], mu[:, :], 1.0 / N, None, ALU.mult)

        def variance(tag):
            with nc.cleanup_on_exit(), ExitStack() as c, nc.Block() as block:
                tb = lambda name, shape, dt=f32: c.enter_context(nc.sbuf_tensor(tag + name, shape, dt))
                sm = lambda name: nc.alloc_semaphore(tag + name)
                o = tb("o", [P, 2, HS, F]); dev = tb("dev", [P, 2, HS, F]); sq = tb("sq", [P, 2, HS, F]); var = tb("var", [P, 2, F])
                o_in = [sm(f"o_in{s}") for s in range(2)]
                dev_ok, sq_ok, summed, done, v_ok, sd_ok = (sm(n) for n in ("dev_ok", "sq_ok", "summed", "done", "v_ok", "sd_ok"))

                @block.sync
                def _(sp):
                    def body(i, first):
                        for s in range(2):
                            if not first:
                                sp.wait_ge(dev_ok, 2 * i + s - 1)
                            sp.dma_start(o[:, s, :, :], tiles(gat_out[bass.ds((i * BODY + s * HS) * P, HS * P), :])).then_inc(o_in[s], 16)
                    body(0, True)
                    with nc.sync.Fori(1, GI) as i:
                        body(i, False)

                @block.vector
                def _(dve):
                    v = nc.vector

                    def body(i, first):
                        for s in range(2):
                            dve.wait_ge(o_in[s], 16 * (i + 1))
                            if not first:
                                dve.wait_ge(sq_ok, 2 * i + s - 1)
                            v.tensor_tensor(dev[:, s, :, :], o[:, s, :, :], mu[:, :].unsqueeze(1).to_broadcast((P, HS, F)), ALU.subtract)
                            v.drain()
                            v.tensor_tensor(dev[:, s, :, :], dev[:, s, :, :], real[:, bass.ds(i * BODY + s * HS, HS)].unsqueeze(2).to_broadcast((P, HS, F)), ALU.mult).then_inc(dev_ok, 1)
                    body(0, True)
                    with v.Fori(1, GI) as i:
                        body(i, False)
                    dve.wait_ge(done, 1)
                    v.tensor_reduce(var[:, 0, :], bank[7][:, 0:HS * F].rearrange("p (t f) -> p f t", t=HS), AX.X, ALU.add).then_inc(v_ok, 1)
                    dve.wait_ge(sd_ok, 1)
                    v.reciprocal(var[:, 0, :], var[:, 1, :])
                    v.drain()
                    v.tensor_tensor(bn_a[:, :], gamma[:, :], var[:, 0, :], ALU.mult)

                @block.scalar
                def _(act):
                    def body(i, first):
                        for s in range(2):
                            act.wait_ge(dev_ok, 2 * i + s + 1)
                            if not first:
                                act.wait_ge(summed, 2 * i + s - 1)
                            nc.scalar.activation(sq[:, s, :, :], dev[:, s, :, :], ACT.Square).then_inc(sq_ok, 1)
                    body(0, True)
                    with nc.scalar.Fori(1, GI) as i:
                        body(i, False)
                    act.wait_ge(v_ok, 1)
                    nc.scalar.activation(var[:, 1, :], var[:, 0, :], ACT.Sqrt, bias=eps[:, 0:1], scale=1.0 / N).then_inc(sd_ok, 1)

                @block.tensor
                def _(pe):
                    nc.tensor.matmul(bank[7][:, 0:HS * F], zeros_w[:, 0:P], zeros_w[:, 0:HS * F], start=True, stop=False)
                    with nc.tensor.Fori(0, GI) as i:
                        for s in range(2):
                            pe.wait_ge(sq_ok, 2 * i + s + 1)
                            nc.tensor.matmul(bank[7][:, 0:HS * F], onesP[:, :], sq[:, s, :, :].rearrange("p t f -> p (t f)"), start=False, stop=False).then_inc(summed, 1)
                    nc.tensor.matmul(bank[7][:, 0:HS * F], zeros_w[:, 0:P], zeros_w[:, 0:HS * F], start=False, stop=True).then_inc(done, 1)

        def plan():
            with nc.cleanup_on_exit(), ExitStack() as c, nc.Block() as block:
                tb = lambda name, shape, dt=f32: c.enter_context(nc.sbuf_tensor("pl_" + name, shape, dt))
                sm = lambda name: nc.alloc_semaphore("pl_" + name)
                GS = min(14, NS)
                NG = NS // GS
                key = tb("key", [R, NBLK * P]); nxt = tb("nxt", [R, NBLK * P]); down = tb("down", [P, 1])
                tot = tb("tot", [P, T]); one = tb("one", [P, T]); cum = tb("cum", [P, T]); first = tb("first", [P, T])
                tile_i = tb("tile_i", [P, 2, T], i32); tile_at = tb("tile_at", [P, 2, T])
                bad = tb("bad", [P, NS]); early = tb("early", [P, NS]); late = tb("late", [P, NS]); mx = tb("mx", [P, 4])
                winr = tb("winr", [GS * WT, 2, NG, P]); winT = tb("winT", [P, 2, NS, WT])
                invr = tb("invr", [R, NBLK * P])
                keys_in, iotas, ones_ok, tot_ok, down_ok, down_sum, starts_ok, copied, wins_in, winT_ok, inv_ok, inv_sb, inv_out = (
                    sm(n) for n in ("keys_in", "iotas", "ones_ok", "tot_ok", "down_ok", "down_sum", "starts_ok", "copied", "wins_in", "winT_ok", "inv_ok", "inv_sb", "inv_out"))

                @block.sync
                def _(sp):
                    blk = lambda lo: dst_rows[lo:lo + NP].rearrange("(b r p) -> r b p", r=R, p=P)
                    for to, lo in ((key, 0), (nxt, 1)):
                        sp.dma_start(to[:, :].rearrange("r (b p) -> r b p", p=P), blk(lo)).then_inc(keys_in, 16)
                    sp.wait_ge(starts_ok, 1)
                    with nc.sync.Fori(0, NS) as n:
                        begin = nc.sync.value_load(starts[0:1, bass.ds(n, 1)], min_val=0, max_val=FRONT + NP)
                        for to, of in ((dst_win, dst_all), (type_win, type_all)):
                            sp.dma_start(to[bass.ds(n * WR, WR)].rearrange("(q p) -> q p", p=P), of[bass.ds(begin, WR)].rearrange("(q p) -> q p", p=P)).then_inc(copied, 16)
                    sp.wait_ge(copied, 32 * NS)
                    for j, of in enumerate((dst_win, type_win)):
                        sp.dma_start(winr[:, j, :, :], of.rearrange("(g n p) -> n g p", g=NG, p=P)).then_inc(wins_in, 16)
                    sp.wait_ge(inv_sb, 1)
                    sp.dma_start(inv_row.rearrange("(b r p) -> r b p", r=R, p=P), invr[:, :].rearrange("r (b p) -> r b p", p=P)).then_inc(inv_out, 16)
                    sp.wait_ge(inv_out, 16)

                @block.gpsimd
                def _(pool):
                    nc.gpsimd.iota(tile_i[:, 0, :], pattern=[[P, T]], base=0, channel_multiplier=0)
                    nc.gpsimd.iota(tile_i[:, 1, :].rearrange("p (n t) -> p n t", t=HS), pattern=[[0, NS], [P, HS]], base=0, channel_multiplier=0).then_inc(iotas, 1)

                @block.tensor
                def _(pe):
                    nc.tensor.matmul(bank[0][:, 0:T], onesP[:, :], cnt[:, :], start=True, stop=True).then_inc(tot_ok, 1)
                    for b in range(NBLK):
                        ins = nc.tensor.transpose(bank[4][0:R, b * P:(b + 1) * P], inv_cnt[:, b * R:(b + 1) * R], ident[:, :])
                    ins.then_inc(inv_ok, 1)
                    pe.wait_ge(down_ok, 1)
                    nc.tensor.matmul(bank[1][:, 0:1], onesP[0:R, :], down[0:R, :], start=True, stop=True).then_inc(down_sum, 1)
                    pe.wait_ge(wins_in, 32)
                    for j in range(2):
                        for g in range(NG):
                            ins = nc.tensor.transpose(bank[2 + j][:, g * GS * WT:(g + 1) * GS * WT], winr[:, j, g, :], ident[0:GS * WT, 0:GS * WT])
                    ins.then_inc(winT_ok, 1)

                @block.vector
                def _(dve):
                    v = nc.vector
                    slots = lambda ap: ap.rearrange("p (n t) -> p n t", t=HS)
                    v.memset(one[:, :], 1.0)
                    dve.wait_ge(keys_in, 32)
                    v.tensor_tensor(nxt[:, :], key[:, :], nxt[:, :], ALU.is_gt)
                    dve.wait_ge(iotas, 1)
                    v.tensor_copy(tile_at[:, :, :], tile_i[:, :, :])
                    v.drain()
                    v.tensor_reduce(down[0:R, :], nxt[:, :], AX.X, ALU.add).then_inc(down_ok, 1)
                    dve.wait_ge(tot_ok, 1)
                    v.tensor_copy(tot[:, :], bank[0][:, 0:T])
                    v.drain()
                    v.tensor_tensor_scan(cum[:, :], one[:, :], tot[:, :], 0.0, ALU.mult, ALU.add)
                    v.drain()
                    v.tensor_tensor(first[:, :], cum[:, :], tot[:, :], ALU.subtract)
                    v.drain()
                    begin = slots(first[:, :])[:, :, 0]
                    beginb = begin.unsqueeze(2).to_broadcast((P, NS, HS))
                    v.tensor_tensor(slots(tot[:, :]), slots(first[:, :]), beginb, ALU.subtract)
                    v.tensor_tensor(slots(cum[:, :]), slots(cum[:, :]), beginb, ALU.subtract)
                    v.drain()
                    v.tensor_tensor(tot[:, :], tot[:, :], tile_at[:, 1, :], ALU.subtract)
                    v.tensor_tensor(cum[:, :], cum[:, :], tile_at[:, 1, :], ALU.subtract)
                    v.drain()
                    v.tensor_scalar(tot[:, :], tot[:, :], -1.0, None, ALU.mult)
                    v.drain()
                    v.tensor_reduce(early[:, :], slots(tot[:, :]), AX.X, ALU.max)
                    v.tensor_reduce(late[:, :], slots(cum[:, :]), AX.X, ALU.max)
                    v.drain()
                    v.tensor_tensor(late[:, :], late[:, :], early[:, :], ALU.add)
                    v.tensor_tensor(tot[:, 0:NS], begin, early[:, :], ALU.subtract)
                    v.tensor_tensor(bad[:, 0:NS], begin, slots(tile_at[:, 0, :])[:, :, 0], ALU.subtract)
                    v.drain()
                    v.tensor_scalar(starts[:, :], tot[0:1, 0:NS], float(FRONT), 0.0, ALU.add, ALU.max).then_inc(starts_ok, 1)
                    v.tensor_scalar(late[:, :], late[:, :], float(BAND * P), None, ALU.is_gt)
                    v.tensor_scalar(early[:, :], early[:, :], float(FRONT), None, ALU.is_gt)
                    v.tensor_scalar(bad[:, 0:NS], bad[:, 0:NS], float((LAG + 1) * HS * P - WR), None, ALU.is_gt)
                    v.drain()
                    for j, cond in enumerate((early, late, bad)):
                        v.tensor_reduce(mx[:, j:j + 1], cond[:, 0:NS], AX.X, ALU.add)
                    dve.wait_ge(down_sum, 1)
                    v.tensor_copy(mx[:, 3:4], bank[1][:, 0:1])
                    v.drain()
                    v.tensor_reduce(down[:, :], mx[:, :], AX.X, ALU.add)
                    v.drain()
                    v.tensor_scalar(fast[:, :], down[0:1, :], 0.0, None, ALU.is_equal)
                    dve.wait_ge(inv_ok, 1)
                    v.tensor_copy(invr[:, :], bank[4][0:R, 0:NBLK * P]).then_inc(inv_sb, 1)
                    dve.wait_ge(winT_ok, 1)
                    v.tensor_copy(winT[:, 0, :, :].rearrange("p n q -> p (n q)"), bank[2][:, 0:NS * WT])
                    v.tensor_scalar(rel_w[:, 0, :], bank[3][:, 0:NS * WT], 0.0, None, ALU.is_equal)
                    v.tensor_scalar(rel_w[:, 1, :], bank[3][:, 0:NS * WT], 0.0, None, ALU.not_equal)
                    ids = edge_id[:, 0:NS * HS * BAND].rearrange("p (n t q) -> p n t q", t=HS, q=BAND)
                    at = slots(tile_at[:, 0, :])
                    v.drain()
                    for q in range(BAND):
                        v.tensor_tensor(ids[:, :, :, q], winT[:, 0, :, q:q + HS], at, ALU.subtract)

        def clear_sums():
            with nc.cleanup_on_exit(), ExitStack() as c, nc.Block() as block:
                zero = c.enter_context(nc.sbuf_tensor("cl_zero", [P, 28 * F], f32))
                ready, zeroed = nc.alloc_semaphore("cl_ready"), nc.alloc_semaphore("cl_zeroed")

                @block.vector
                def _(dve):
                    nc.vector.memset(zero[:, :], 0.0).then_inc(ready, 1)

                @block.sync
                def _(sp):
                    sp.wait_ge(ready, 1)
                    wide = sums_w.rearrange("(g p r) f -> g p (r f)", p=P, r=14)
                    narrow = sums_n.rearrange("(g p r) f -> g p (r f)", p=P, r=28)
                    for g in range(wide.shape[0]):
                        sp.dma_start(wide[g], zero[:, 0:14 * 2 * F]).then_inc(zeroed, 16)
                    for g in range(narrow.shape[0]):
                        sp.dma_start(narrow[g], zero[:, 0:28 * F]).then_inc(zeroed, 16)
                    sp.wait_ge(zeroed, 16 * (wide.shape[0] + narrow.shape[0]))

        def normalise(dve, j, s, tl, xn, bs, ln, var_ok, sd_ok, ln_ok, conv):
            v = nc.vector
            """The layer norm's scale and shift of each row, from halves' means and squares."""
            L = lambda r: ln[:, s, r, :]
            for t in range(HS):
                v.bn_stats(bs[:, s, t, :], xn[:, s, t, :])
            v.drain()
            v.tensor_tensor(L(0), bs[:, s, :, 1], bs[:, s, :, 4], ALU.add)
            v.tensor_tensor(L(1), bs[:, s, :, 1], bs[:, s, :, 4], ALU.subtract)
            v.tensor_tensor(L(2), bs[:, s, :, 2], bs[:, s, :, 5], ALU.add)
            v.drain()
            v.tensor_tensor(L(1), L(1), L(1), ALU.mult)
            v.drain()
            v.scalar_tensor_tensor(L(3), L(1), F / 4.0, L(2), ALU.mult, ALU.add).then_inc(var_ok[s], 1)
            dve.wait_ge(sd_ok[s], j + 1)
            v.reciprocal(L(5), L(4))
            v.drain()
            ins = v.scalar_tensor_tensor(L(6), L(0), -0.5, L(5), ALU.mult, ALU.mult)
            if conv:
                v.drain()
                v.tensor_tensor(L(0), L(5), rs_send[:, tl], ALU.mult)
                ins = v.tensor_tensor(L(1), L(6), rs_send[:, tl], ALU.mult)
            ins.then_inc(ln_ok[s], 1)

        def layer(tag, kind, table_in, table_out, k=0):
            with nc.cleanup_on_exit(), ExitStack() as c, nc.Block() as block:
                tb = lambda name, shape, dt=f32: c.enter_context(nc.sbuf_tensor(tag + name, shape, dt))
                sm = lambda name: nc.alloc_semaphore(tag + name)
                two = lambda name: [sm(f"{name}{s}") for s in range(2)]
                typed, conv, sage = kind == "typed", kind == "conv", kind == "sage"
                final = typed and k == 2
                norms = not typed
                M = F if sage else 2 * F
                got = tb("got", [P, 2, HS, F]); src_st = tb("src_st", [P, 2, HS], i32)
                win = tb("win", [P, 2, WT, F]) if typed else None
                msg = tb("msg", [P, 2, WT, M])
                S = tb("S", [P, 2, BAND * HS, P])
                own = None if conv else tb("own", [P, 2, HS, 2 * F if sage else F])
                inv_r = tb("inv_r", [P, 2, HS * P]) if conv else None
                aT = tb("aT", [P, 2, HS * P])
                loopT = aT
                hT = tb("hT", [F, 2, HS * P]) if typed else None
                o = tb("o", [P, 2, HS, F])
                xn = lent(alpha, 2 * HS * F, lambda shape: tb("xn", shape)); h = lent(amax, 2 * HS * F, lambda shape: tb("h", shape))
                g = tb("g", [P, 2, HS, F]) if conv else None
                bs = tb("bs", [P, 2, HS, 6]); ln = tb("ln", [P, 2, 8, HS])
                gathered, src_ok, kept, win_in, S_ok, msg_ok = two("gathered"), two("src_ok"), two("kept"), two("win_in"), two("S_ok"), two("msg_ok")
                agg_ok, aT_ok, loop_ok, loop_out, prod, o_free = two("agg_ok"), two("aT_ok"), two("loop_ok"), two("loop_out"), two("prod"), two("o_free")
                x_ok, x_kept, var_ok, sd_ok, ln_ok, h_ok, stored, go = two("x_ok"), two("x_kept"), two("var_ok"), two("sd_ok"), two("ln_ok"), two("h_ok"), two("stored"), sm("go")
                n_win = {"conv": 3, "sage": 3, "typed": 2}[kind]
                n_out = 2 if conv else 1
                PER = 16 * HS
                CH = [(0, 4), (4, HS)]

                @block.gpsimd
                def _(pool):
                    def gather(i, s, first):
                        if not first:
                            pool.wait_ge(kept[s], 16 * i)
                        pool.sem_inc(go, 1)
                        nc.gpsimd.tensor_copy(src_st[:, s, :], src_i[:, bass.ds(i * BODY + s * HS, HS)]).then_inc(src_ok[s], 1)
                        pool.wait_ge(src_ok[s], i + 1)
                        pool.sem_inc(go, 1)
                        for t in range(HS):
                            pool.indirect_dma_start(out=got[:, s, t, :], out_offset=None, in_=table_in,
                                                    in_offset=bass.IndirectOffsetOnAxis(ap=src_st[:, s, t:t + 1], axis=0)).then_inc(gathered[s], 16)
                    for s in range(2):
                        gather(0, s, True)
                    with nc.gpsimd.Fori(1, GI) as i:
                        for s in range(2):
                            gather(i, s, False)

                @block.sync
                def _(sp):
                    def keep(i, s):
                        sp.wait_ge(gathered[s], PER * (i + 1))
                        sp.sem_inc(go, 1)
                        sp.dma_start(tiles(edge_h[bass.ds((i * BODY + s * HS) * P, HS * P), :]), got[:, s, :, :]).then_inc(kept[s], 16)

                    def windows(j, s, first):
                        n = 2 * j + s
                        sp.sem_inc(go, 1)
                        begin = nc.sync.value_load(starts[0:1, bass.ds(n, 1)], min_val=0, max_val=FRONT + NP)
                        at = bass.ds((j * BODY + s * HS) * P, HS * P)
                        if not first:
                            sp.wait_ge(agg_ok[s], j)
                            if typed:
                                sp.wait_ge(msg_ok[s], j)
                            if conv:
                                sp.wait_ge(loop_ok[s], j)
                        to = win[:, s, :, :] if typed else msg[:, s, :, 0:F]
                        sp.dma_start(to, tiles(edge_all[bass.ds(begin, WR), :])).then_inc(win_in[s], 16)
                        if conv:
                            sp.dma_start(msg[:, s, :, F:2 * F], tiles(attr_all[bass.ds(begin, WR), :])).then_inc(win_in[s], 16)
                            sp.dma_start(inv_r[F:2 * F, s, :], inv_row[at].rearrange("(o n) -> o n", o=1).to_broadcast((F, HS * P))).then_inc(win_in[s], 16)
                        if typed:
                            sp.dma_start(own[:, s, :, :], tiles(table_in[at, :])).then_inc(win_in[s], 16)
                        if sage:
                            sp.dma_start(own[:, s, :, 0:F], tiles(table_in[at, :])).then_inc(win_in[s], 16)
                            sp.dma_start(own[:, s, :, F:2 * F], tiles(node_h[at, :])).then_inc(win_in[s], 16)

                    for s in range(2):
                        keep(0, s)

                    def body(i, first):
                        for s in range(2):
                            keep(i, s)
                            sp.wait_ge(kept[s], 16 * (i + 1))
                            sp.sem_inc(go, 1)
                            sp.wait_ge(kept[1 - s], 16 * (i + s))
                            windows(i - 1, s, first)
                    body(1, True)
                    with nc.sync.Fori(2, GI) as i:
                        body(i, False)
                    for s in range(2):
                        sp.wait_ge(kept[1], 16 * GI)
                        windows(GI - 1, s, False)

                @block.tensor
                def _(pe):
                    def sums(j, s, first):
                        pe.wait_ge(S_ok[s], j + 1)
                        if typed:
                            pe.wait_ge(msg_ok[s], j + 1)
                        pe.wait_ge(win_in[s], 16 * n_win * (j + 1))
                        if not first:
                            pe.wait_ge(aT_ok[s], j)
                            if conv:
                                pe.wait_ge(loop_ok[s], j)
                        if typed and not (first and s == 0):
                            pe.wait_ge(aT_ok[1 - s], j + s)
                        pe.sem_inc(go, 1)
                        for b, (t0, t1) in enumerate(CH):
                            for t in range(t0, t1):
                                col = slice((t - t0) * P, (t - t0 + 1) * P)
                                to = bank[2 * s + b][0:M, col]
                                qs = range(BAND)
                                if sage:
                                    nc.tensor.matmul(bank[2 * s + b][F:2 * F, col], own[:, s, t, F:2 * F], ident[:, :], start=True, stop=True)
                                    nc.tensor.matmul(to, own[:, s, t, 0:F], ident[:, :], start=True, stop=False)
                                for q in qs:
                                    ins = nc.tensor.matmul(to, msg[:, s, t + q, :], S[:, s, BAND * t + q, :], start=(q == 0 and not sage), stop=(q == BAND - 1))
                                if typed:
                                    ins = nc.tensor.transpose(bank[4 + b][0:F, col], own[:, s, t, :], ident[:, :])
                        ins.then_inc(agg_ok[s], 1)

                    def products(j, s, first):
                        pe.wait_ge(aT_ok[s], j + 1)
                        if not first:
                            pe.wait_ge(o_free[s], j)
                        pe.sem_inc(go, 1)
                        for t in range(HS):
                            po = bank[6 + s][:, t * F:(t + 1) * F]
                            a_t = lambda lo, hi: aT[lo:hi, s, t * P:(t + 1) * P]
                            if conv:
                                ins = nc.tensor.matmul(po, a_t(0, F), W0[:, :], start=True, stop=True)
                            if sage:
                                nc.tensor.matmul(po, a_t(F, 2 * F), W1s[F:2 * F, :], start=True, stop=True)
                                ins = nc.tensor.matmul(bank[4 + s][:, t * F:(t + 1) * F], a_t(0, F), W1s[0:F, :], start=True, stop=True)
                            if typed:
                                nc.tensor.matmul(po, a_t(0, 2 * F), W3[:, k, :], start=True, stop=False)
                                ins = nc.tensor.matmul(po, hT[:, s, t * P:(t + 1) * P], Ws3[:, k, :], start=False, stop=True)
                        ins.then_inc(prod[s], 1)

                    sums(0, 0, True)

                    def body(j, first, last):
                        sums(j, 1, first)
                        products(j, 0, first)
                        if not last:
                            sums(j + 1, 0, False)
                        products(j, 1, first)
                    body(0, True, False)
                    with nc.tensor.Fori(1, GI - 1) as j:
                        body(j, False, False)
                    body(GI - 1, False, True)

                @block.scalar
                def _(act):
                    A = nc.scalar

                    def evacuate(j, s, first):
                        act.wait_ge(agg_ok[s], j + 1)
                        if not first:
                            act.wait_ge(prod[s], j)
                        rows = F if conv else 2 * F
                        for b, (t0, t1) in enumerate(CH):
                            ins = A.copy(aT[0:rows, s, t0 * P:t1 * P], bank[2 * s + b][0:rows, 0:(t1 - t0) * P])
                            if typed:
                                ins = A.copy(hT[:, s, t0 * P:t1 * P], bank[4 + b][0:F, 0:(t1 - t0) * P])
                        ins.then_inc(aT_ok[s], 1)

                    def rows_out(j, s, first):
                        n = 2 * j + s
                        at = bass.ds((j * BODY + s * HS) * P, HS * P)
                        if norms:
                            act.wait_ge(x_ok[s], j + 1)
                            A.copy(x_sb[:, bass.ds(j * BODY + s * HS, HS), :], xn[:, s, :, :]).then_inc(x_kept[s], 1)
                            act.wait_ge(var_ok[s], j + 1)
                            A.activation(ln[:, s, 4, :], ln[:, s, 3, :], ACT.Sqrt, bias=eps[:, 0:1], scale=1.0 / F).then_inc(sd_ok[s], 1)
                        act.wait_ge(o_free[s] if typed and not final else ln_ok[s], j + 1)
                        if not first:
                            act.wait_ge(stored[s], 16 * n_out * j)
                            A.sem_inc(go, 1)
                        if norms:
                            for t in range(HS):
                                ins = A.activation(h[:, s, t, :], xn[:, s, t, :], ACT.Relu, bias=ln[:, s, 6, t:t + 1], scale=ln[:, s, 5, t:t + 1])
                                if conv:
                                    ins = A.activation(g[:, s, t, :], xn[:, s, t, :], ACT.Relu, bias=ln[:, s, 1, t:t + 1], scale=ln[:, s, 0, t:t + 1])
                        elif final:
                            ins = A.copy(h[:, s, :, :], o[:, s, :, :])
                        else:
                            ins = A.activation(h[:, s, :, :], o[:, s, :, :], ACT.Relu)
                        ins.then_inc(h_ok[s], 1)
                        act.wait_ge(h_ok[s], j + 1)
                        if not final:
                            if conv:
                                act.dma_start(tiles(node_h[at, :]), h[:, s, :, :]).then_inc(stored[s], 16)
                                act.dma_start(tiles(table_out[at, :]), g[:, s, :, :]).then_inc(stored[s], 16)
                            else:
                                act.dma_start(tiles(table_out[at, :]), h[:, s, :, :]).then_inc(stored[s], 16)
                        elif isinstance(j, int) and j == GI - 1 and j * BODY + s * HS + HS > FULL:
                            to = FULL - (j * BODY + s * HS)
                            if to > 0:
                                act.dma_start(tiles(out[(FULL - to) * P:FULL * P, :]), h[:, s, 0:to, :]).then_inc(stored[s], 16)
                            if REM:
                                act.dma_start(out[FULL * P:N, :], h[0:REM, s, to, :]).then_inc(stored[s], 16)
                        else:
                            act.dma_start(tiles(out[at, :]), h[:, s, :, :]).then_inc(stored[s], 16)
                        if conv:
                            act.wait_ge(loop_ok[s], j + 1)
                            act.dma_start(loop_rows[:, at], loopT[F:2 * F, s, :]).then_inc(loop_out[s], 16)

                    evacuate(0, 0, True)

                    def body(j, first, last):
                        evacuate(j, 1, first)
                        rows_out(j, 0, first)
                        if not last:
                            evacuate(j + 1, 0, False)
                        rows_out(j, 1, first)
                    body(0, True, False)
                    with A.Fori(1, GI - 1) as j:
                        body(j, False, False)
                    body(GI - 1, False, True)
                    for s in range(2):
                        n = FULL - ((GI - 1) * BODY + s * HS)
                        last = 1 if n >= HS else (1 if n > 0 else 0) + (1 if REM else 0)
                        act.wait_ge(stored[s], 16 * (GI - 1 + last) if final else 16 * n_out * GI)
                        if conv:
                            act.wait_ge(loop_out[s], 16 * GI)

                @block.vector
                def _(dve):
                    v = nc.vector
                    def matrices(j, s, first):
                        n = 2 * j + s
                        if not first:
                            dve.wait_ge(agg_ok[s], j)
                        v.tensor_tensor(S[:, s, :, :], node_id[:, :].unsqueeze(1).to_broadcast((P, BAND * HS, P)),
                                        edge_id[:, bass.ds(n * BAND * HS, BAND * HS)].unsqueeze(2).to_broadcast((P, BAND * HS, P)), ALU.is_equal).then_inc(S_ok[s], 1)
                        if typed:
                            dve.wait_ge(win_in[s], 16 * n_win * (j + 1))
                            for r in range(2):
                                ins = v.tensor_tensor(msg[:, s, :, r * F:(r + 1) * F], win[:, s, :, :],
                                                      rel_w[:, r, bass.ds(n * WT, WT)].unsqueeze(2).to_broadcast((P, WT, F)), ALU.mult)
                            ins.then_inc(msg_ok[s], 1)

                    def update(j, s, first):
                        tl = bass.ds(j * BODY + s * HS, HS)
                        wide = lambda ap: ap.unsqueeze(2).to_broadcast((P, HS, F))
                        rowb = lambda ap: ap.unsqueeze(1).to_broadcast((P, HS, F))
                        po = bank[6 + s][:, 0:HS * F].rearrange("p (t f) -> p t f", t=HS)
                        if conv:
                            dve.wait_ge(agg_ok[s], j + 1)
                            if not first:
                                dve.wait_ge(loop_out[s], 16 * j)
                            for b, (t0, t1) in enumerate(CH):
                                ins = v.tensor_tensor(loopT[F:2 * F, s, t0 * P:t1 * P], bank[2 * s + b][F:2 * F, 0:(t1 - t0) * P],
                                                      inv_r[F:2 * F, s, t0 * P:t1 * P], ALU.mult)
                            ins.then_inc(loop_ok[s], 1)
                        dve.wait_ge(prod[s], j + 1)
                        if not first and norms:
                            dve.wait_ge(x_kept[s], j)
                            dve.wait_ge(h_ok[s], j)
                        if not first and typed:
                            dve.wait_ge(h_ok[s], j)
                        if typed:
                            if final:
                                v.tensor_tensor(xn[:, s, :, :], po, rowb(b3[:, k, :]), ALU.add).then_inc(o_free[s], 1)
                                v.drain()
                                v.tensor_tensor(o[:, s, :, :], xn[:, s, :, :], x_sb[:, tl, :], ALU.add).then_inc(ln_ok[s], 1)
                            else:
                                v.tensor_tensor(o[:, s, :, :], po, rowb(b3[:, k, :]), ALU.add).then_inc(o_free[s], 1)
                            return
                        if conv:
                            v.tensor_tensor(o[:, s, :, :], po, wide(norm[:, tl]), ALU.mult).then_inc(o_free[s], 1)
                            v.drain()
                            v.tensor_tensor(o[:, s, :, :], o[:, s, :, :], rowb(b0[:, :]), ALU.add)
                            v.drain()
                            v.scalar_tensor_tensor(xn[:, s, :, :], o[:, s, :, :], 0.0, x_sb[:, tl, :], ALU.max, ALU.add).then_inc(x_ok[s], 1)
                        if sage:
                            pu = bank[4 + s][:, 0:HS * F].rearrange("p (t f) -> p t f", t=HS)
                            v.tensor_tensor(o[:, s, :, :], pu, wide(upd_scale[:, tl]), ALU.mult)
                            v.drain()
                            v.tensor_tensor(o[:, s, :, :], o[:, s, :, :], po, ALU.add).then_inc(o_free[s], 1)
                            v.drain()
                            v.tensor_tensor(o[:, s, :, :], o[:, s, :, :], rowb(b1[:, :]), ALU.add)
                            v.drain()
                            v.tensor_tensor(xn[:, s, :, :], o[:, s, :, :], x_sb[:, tl, :], ALU.add).then_inc(x_ok[s], 1)
                        v.drain()
                        normalise(dve, j, s, tl, xn, bs, ln, var_ok, sd_ok, ln_ok, conv)

                    matrices(0, 0, True)

                    def body(j, first, last):
                        matrices(j, 1, first)
                        update(j, 0, first)
                        if not last:
                            matrices(j + 1, 0, False)
                        update(j, 1, first)
                    body(0, True, False)
                    with v.Fori(1, GI - 1) as j:
                        body(j, False, False)
                    body(GI - 1, False, True)

        def attention_weights():
            with nc.cleanup_on_exit(), ExitStack() as c, nc.Block() as block:
                tb = lambda name, shape, dt=f32: c.enter_context(nc.sbuf_tensor("aw_" + name, shape, dt))
                brb = tb("brb", [P, HF]); part = tb("part", [P, 3, HF]); halves = tb("halves", [P, 2, 2]); blc = tb("blc", [F, HEADS + 1])
                zeroed, loaded = nc.alloc_semaphore("aw_zeroed"), nc.alloc_semaphore("aw_loaded")
                n_loads = 11

                @block.sync
                def _(sp):
                    sp.wait_ge(zeroed, 1)
                    column = lambda v: v.rearrange("(f o) -> f o", o=1)
                    with nc.allow_non_contiguous_dma(reason="a few columns of weights"):
                        for h in range(HEADS):
                            sp.dma_start(attc[(h % 2) * F:(h % 2 + 1) * F, h // 2, h:h + 1], column(a["L2_gnn_att"][h])).then_inc(loaded, 16)
                        for j, name in enumerate(("L2_gnn_b_l", "L2_gnn_b_r")):
                            sp.dma_start(halves[:, j, :], a[name].rearrange("(q p) -> p q", p=P)).then_inc(loaded, 16)
                        sp.dma_start(blc[:, 0:HEADS], a["L2_gnn_b_l"].rearrange("(h f) -> f h", f=F)).then_inc(loaded, 16)
                        sp.dma_start(blc[:, HEADS:], column(a["L2_gnn_bias"])).then_inc(loaded, 16)
                        sp.dma_start(bn_col[:, 0:1], column(a["L2_gnn_gamma"])).then_inc(loaded, 16)
                        sp.dma_start(bn_col[:, 1:2], column(a["L2_gnn_beta"])).then_inc(loaded, 16)
                    sp.dma_start(brb[:, :], a["L2_gnn_b_r"].rearrange("(o f) -> o f", o=1).to_broadcast((P, HF))).then_inc(loaded, 16)

                @block.vector
                def _(dve):
                    v = nc.vector
                    heads = lambda ap: ap.rearrange("p (h f) -> p h f", h=HEADS)
                    v.memset(attc[:, :, :], 0.0).then_inc(zeroed, 1)
                    dve.wait_ge(loaded, 16 * n_loads)
                    v.tensor_scalar(attc[:, :, :], attc[:, :, :], (1.0 - SLOPE) / 2, None, ALU.mult)
                    v.tensor_tensor(b_col[:, :], halves[:, 0, :], halves[:, 1, :], ALU.add)
                    v.tensor_tensor(brb[:, :], brb[:, :], blb[:, :], ALU.add)
                    v.tensor_reduce(o_col[:, :], blc[:, 0:HEADS], AX.X, ALU.add)
                    v.drain()
                    v.scalar_tensor_tensor(o_col[:, :], o_col[:, :], 1.0 / HEADS, blc[:, HEADS:], ALU.mult, ALU.add)
                    for j, w in enumerate((brb, Wlr, Wself)):
                        v.scalar_tensor_tensor(part[:, j, :], w[:, :], (1.0 + SLOPE) / 2, attb[:, :], ALU.mult, ALU.mult)
                    v.drain()
                    for j, to in enumerate((a_const, Vlr, Vself)):
                        v.tensor_reduce(to[:, :], heads(part[:, j, :]), AX.X, ALU.add)
                    v.drain()
                    v.scalar_tensor_tensor(part[0:F, 0, :], Wea[0:F, :], (1.0 + SLOPE) / 2, attb[0:F, :], ALU.mult, ALU.mult)
                    v.drain()
                    v.tensor_reduce(Vea[:, :], heads(part[0:F, 0, :]), AX.X, ALU.add)

        def attention(tag):
            with nc.cleanup_on_exit(), ExitStack() as c, nc.Block() as block:
                tb = lambda name, shape, dt=f32: c.enter_context(nc.sbuf_tensor(tag + name, shape, dt))
                sm = lambda name: nc.alloc_semaphore(tag + name)
                two = lambda name: [sm(f"{name}{s}") for s in range(2)]
                E8 = 2 * HEADS
                win = lent(alpha, 2 * WT * F, lambda shape: tb("win", shape))
                own = lent(amax, 2 * HS * F, lambda shape: tb("own", shape))
                shared = tb("shared", [P, 2, WR])
                oT = shared[0:F, :, 0:HS * P]; exw = shared[F:F + E8, :, :]
                exs = tb("exs", [P, WT, E8])
                msg = tb("msg", [P, WT, HEADS, F])
                S = tb("S", [P, BAND * HS, P])
                catT = tb("catT", [P, 2, HS * P]); az = tb("az", [P, 2, HS * P])
                mine = tb("mine", [P, HS, HEADS, F])
                idle = lent(per_tile, 4 * HS * HF // 2, lambda shape: tb("idle", shape))
                agg, aggT = (idle[:, k].rearrange("p t f -> p (t f)") for k in range(2))
                agg = agg.rearrange("p (t h f) -> p t h f", t=HS, h=HEADS); aggT = aggT.rearrange("p (q n) -> p q n", q=2)
                score = tb("score", [P, HS, HEADS]); me = tb("me", [P, HS, HEADS]); den = tb("den", [P, 2, HS, HEADS]); mm = tb("mm", [P, HS, HEADS])
                d = tb("d", [P, 2, HS, HEADS]); cc = tb("cc", [P, 2, HS, HEADS])
                stats = tb("stats", [F, 2 * NS, 6]); mv = tb("mv", [F, 4])
                loads, stored = two("loads"), two("stored")
                (madeA, readA, madeC, readC, ex_made, exs_ok, msg_ok, S_ok, own_made, sums_ok, small_read, d_ok, e_ok, c_ok, mine_ok, agg_ok,
                 aT_made, aT_read, stat_ok, var_ok, sd_ok, go) = (sm(n) for n in (
                     "madeA", "readA", "madeC", "readC", "ex_made", "exs_ok", "msg_ok", "S_ok", "own_made", "sums_ok", "small_read", "d_ok", "e_ok", "c_ok",
                     "mine_ok", "agg_ok", "aT_made", "aT_read", "stat_ok", "var_ok", "sd_ok", "go"))
                CH = [(0, 4), (4, HS)]
                turned_ex = bank[7][:, 0:WT * E8].rearrange("p (t c) -> p t c", c=E8)
                own_ps = bank[7][:, 64:64 + HS * HEADS].rearrange("p (t h) -> p t h", h=HEADS)
                small_ps = bank[7][:, 128:128 + HS * E8].rearrange("p (t c) -> p t c", c=E8)
                assert N > (NS - 1) * HS * P

                @block.sync
                def _(sp):
                    def load(j, s, first):
                        n = 2 * j + s
                        if not first:
                            sp.wait_ge(mine_ok, n - 1)
                            sp.sem_inc(go, 1)
                            sp.wait_ge(own_made, n - 1)
                            sp.sem_inc(go, 1)
                        begin = nc.sync.value_load(starts[0:1, bass.ds(n, 1)], min_val=0, max_val=FRONT + NP)
                        at = bass.ds((j * BODY + s * HS) * P, HS * P)
                        sp.dma_start(own[:, s, :, :], tiles(node_g[at, :])).then_inc(loads[s], 16)
                        sp.dma_start(catT[F:2 * F, s, :], loop_rows[:, at]).then_inc(loads[s], 16)
                        sp.dma_start(exw[:, s, :], exp_all[:, bass.ds(begin, WR)]).then_inc(loads[s], 16)
                        sp.dma_start(win[:, s, :, :], tiles(edge_all[bass.ds(begin, WR), :])).then_inc(loads[s], 16)
                    for s in range(2):
                        load(0, s, True)
                    with nc.sync.Fori(1, GI) as j:
                        for s in range(2):
                            load(j, s, False)

                @block.gpsimd
                def _(pool):
                    g = nc.gpsimd

                    def messages(j, s, first):
                        n = 2 * j + s
                        pool.wait_ge(exs_ok, n + 1)
                        pool.wait_ge(loads[s], 64 * (j + 1))
                        if not first:
                            pool.wait_ge(sums_ok, 2 * n)
                        for h in range(HEADS):
                            ins = g.tensor_tensor(msg[:, :, h, :], win[:, s, :, :], exs[:, :, h:h + 1].to_broadcast((P, WT, F)), ALU.mult)
                        ins.then_inc(msg_ok, 1)

                    def own_edges(j, s):
                        pool.wait_ge(c_ok, 2 * j + s + 1)
                        for h in range(HEADS):
                            ins = g.tensor_tensor(mine[:, :, h, :], own[:, s, :, :], cc[:, 1, :, h:h + 1].to_broadcast((P, HS, F)), ALU.mult)
                        ins.then_inc(mine_ok, 1)
                    messages(0, 0, True)
                    own_edges(0, 0)
                    messages(0, 1, False)
                    own_edges(0, 1)
                    with g.Fori(1, GI) as j:
                        for s in range(2):
                            messages(j, s, False)
                            own_edges(j, s)

                @block.tensor
                def _(pe):
                    def own_rows(j, s, first):
                        n = 2 * j + s
                        pe.wait_ge(loads[s], 64 * (j + 1))
                        if not first:
                            pe.wait_ge(small_read, n)
                        pe.sem_inc(go, 1)
                        for q in range(WT):
                            ins = nc.tensor.transpose(turned_ex[:, q, :], exw[:, s, q * P:(q + 1) * P], ident[F:F + E8, F:F + E8])
                        ins.then_inc(ex_made, 1)
                        for b, (t0, t1) in enumerate(CH):
                            if not first:
                                if isinstance(j, int) and n == 1:
                                    pe.wait_ge(readA, 4 + b)
                                else:
                                    pe.wait_ge(readC, 2 * n - 3 + b)
                            pe.sem_inc(go, 1)
                            for t in range(t0, t1):
                                ins = nc.tensor.transpose(bank[4 + b][0:F, (t - t0) * P:(t - t0 + 1) * P], own[:, s, t, :], ident[:, :])
                            ins.then_inc(madeA, 1)
                        for q, b, to, seen in ((0, 0, 6, 1), (0, 1, 4, 2), (1, 0, 5, 2), (1, 1, 6, 3)):
                            t0, t1 = CH[b]
                            pe.wait_ge(readA, 6 * n + seen)
                            nc.tensor.matmul(bank[to][:, 0:(t1 - t0) * P], Wself[:, q * P:(q + 1) * P], catT[:, s, t0 * P:t1 * P], start=True, stop=True).then_inc(madeA, 1)
                        pe.wait_ge(readA, 6 * n + 6)
                        pe.wait_ge(exs_ok, n + 1)
                        pe.sem_inc(go, 1)
                        for t in range(HS):
                            col = slice(t * P, (t + 1) * P)
                            nc.tensor.matmul(own_ps[:, t, :], catT[:, s, col], Vself[:, :], start=True, stop=False)
                            nc.tensor.matmul(own_ps[:, t, :], az[:, 0, col], attc[:, 0, :], start=False, stop=False)
                            ins = nc.tensor.matmul(own_ps[:, t, :], az[:, 1, col], attc[:, 1, :], start=False, stop=True)
                        ins.then_inc(own_made, 1)

                    def sums(n, first):
                        pe.wait_ge(msg_ok, n + 1)
                        for b, (t0, t1) in enumerate(CH):
                            pe.wait_ge(S_ok, 2 * n + b + 1)
                            for t in range(t0, t1):
                                qs = range(BAND)
                                for q in qs:
                                    mat, e = S[:, BAND * t + q, :], t + q
                                    nc.tensor.matmul(bank[t // 2][:, (t % 2) * HF:(t % 2 + 1) * HF], mat, msg[:, e, :, :].rearrange("p h f -> p (h f)"), start=(q == 0), stop=(q == BAND - 1))
                                    ins = nc.tensor.matmul(small_ps[:, t, :], mat, exs[:, e, :], start=(q == 0), stop=(q == BAND - 1))
                            ins.then_inc(sums_ok, 1)

                    def outputs(m):
                        pe.wait_ge(agg_ok, m + 1)
                        pe.sem_inc(go, 1)
                        for k, (b, q) in enumerate(((0, 0), (0, 1), (1, 0), (1, 1))):
                            t0, t1 = CH[b]
                            for t in range(t0, t1):
                                ins = nc.tensor.transpose(bank[k][:, (t - t0) * P:(t - t0 + 1) * P], agg[:, t, 2 * q:2 * q + 2, :].rearrange("p h f -> p (h f)"), ident[:, :])
                            ins.then_inc(aT_made, 1)
                        for b, (t0, t1) in enumerate(CH):
                            pe.wait_ge(aT_read, 4 * m + 2 * b + 2)
                            pe.sem_inc(go, 1)
                            for q in range(2):
                                ins = nc.tensor.matmul(bank[4 + b][0:F, 0:(t1 - t0) * P], Wst[:, q, :], aggT[:, q, t0 * P:t1 * P], start=(q == 0), stop=(q == 1))
                            ins.then_inc(madeC, 1)

                    own_rows(0, 0, True)
                    sums(0, True)
                    own_rows(0, 1, False)
                    outputs(0)
                    sums(1, False)
                    with nc.tensor.Fori(1, GI) as j:
                        for s in range(2):
                            own_rows(j, s, False)
                            outputs(2 * j + s - 1)
                            sums(2 * j + s, False)
                    outputs(NS - 1)

                @block.scalar
                def _(act):
                    A = nc.scalar

                    def own_rows(j, s, first):
                        n = 2 * j + s
                        if not first:
                            act.wait_ge(own_made, n)
                        for b, (t0, t1) in enumerate(CH):
                            act.wait_ge(madeA, 6 * n + 1 + b)
                            A.copy(catT[0:F, s, t0 * P:t1 * P], bank[4 + b][0:F, 0:(t1 - t0) * P]).then_inc(readA, 1)
                        for k, (q, b, to) in enumerate(((0, 0, 6), (0, 1, 4), (1, 0, 5), (1, 1, 6))):
                            t0, t1 = CH[b]
                            act.wait_ge(madeA, 6 * n + 3 + k)
                            A.activation(az[:, q, t0 * P:t1 * P], bank[to][:, 0:(t1 - t0) * P], ACT.Abs, bias=b_col[:, q:q + 1], scale=1.0).then_inc(readA, 1)

                    def exps(n):
                        act.wait_ge(d_ok, n + 1)
                        A.activation(d[:, :, :, :], d[:, :, :, :], ACT.Exp).then_inc(e_ok, 1)

                    def outputs(i, s, m, first):
                        for k, (b, q) in enumerate(((0, 0), (0, 1), (1, 0), (1, 1))):
                            t0, t1 = CH[b]
                            act.wait_ge(aT_made, 4 * m + k + 1)
                            A.copy(aggT[:, q, t0 * P:t1 * P], bank[k][:, 0:(t1 - t0) * P]).then_inc(aT_read, 1)
                        if not first:
                            act.wait_ge(stored[s], 16 * i)
                            act.wait_ge(stat_ok, m - 1)
                        for b, (t0, t1) in enumerate(CH):
                            act.wait_ge(madeC, 2 * m + b + 1)
                            A.activation(oT[:, s, t0 * P:t1 * P], bank[4 + b][0:F, 0:(t1 - t0) * P], ACT.Identity, bias=o_col[:, 0:1], scale=1.0 / HEADS).then_inc(readC, 1)
                        act.wait_ge(readC, 2 * m + 2)
                        act.sem_inc(go, 1)
                        act.dma_start(gat_rows[:, bass.ds((i * BODY + s * HS) * P, HS * P)], oT[:, s, :]).then_inc(stored[s], 16)

                    own_rows(0, 0, True)
                    exps(0)
                    own_rows(0, 1, False)
                    outputs(0, 0, 0, True)
                    exps(1)

                    def body(j, first):
                        own_rows(j, 0, False)
                        outputs(j - 1, 1, 2 * j - 1, first)
                        exps(2 * j)
                        own_rows(j, 1, False)
                        outputs(j, 0, 2 * j, False)
                        exps(2 * j + 1)
                    body(1, True)
                    with A.Fori(2, GI) as j:
                        body(j, False)
                    outputs(GI - 1, 1, NS - 1, False)
                    act.wait_ge(var_ok, 1)
                    A.activation(mv[:, 2:3], mv[:, 1:2], ACT.Sqrt, bias=eps[0:F, 0:1]).then_inc(sd_ok, 1)
                    for s in range(2):
                        act.wait_ge(stored[s], 16 * GI)

                @block.vector
                def _(dve):
                    v = nc.vector

                    def matrices(n, first):
                        for b, (t0, t1) in enumerate(CH):
                            if not first:
                                dve.wait_ge(sums_ok, 2 * n - 1 + b)
                            k = BAND * (t1 - t0)
                            v.tensor_tensor(S[:, BAND * t0:BAND * t1, :], node_id[:, :].unsqueeze(1).to_broadcast((P, k, P)),
                                            edge_id[:, bass.ds(n * BAND * HS + BAND * t0, k)].unsqueeze(2).to_broadcast((P, k, P)), ALU.is_equal).then_inc(S_ok, 1)

                    def exponentials(n, first):
                        dve.wait_ge(ex_made, n + 1)
                        if not first:
                            dve.wait_ge(msg_ok, n)
                            dve.wait_ge(sums_ok, 2 * n)
                        v.tensor_copy(exs[:, :, :], turned_ex).then_inc(exs_ok, 1)

                    def weights(j, s, first, following):
                        n = 2 * j + s
                        tl = bass.ds(j * BODY + s * HS, HS)
                        dve.wait_ge(own_made, n + 1)
                        dve.wait_ge(sums_ok, 2 * n + 2)
                        v.tensor_tensor(score[:, :, :], own_ps, a_const[:, :].unsqueeze(1).to_broadcast((P, HS, HEADS)), ALU.add)
                        v.tensor_tensor(me[:, :, :], small_ps[:, :, HEADS:E8], no_edge[:, tl].unsqueeze(2).to_broadcast((P, HS, HEADS)), ALU.add)
                        v.tensor_copy(den[:, 0, :, :], small_ps[:, :, 0:HEADS]).then_inc(small_read, 1)
                        v.drain()
                        v.tensor_tensor(mm[:, :, :], me[:, :, :], score[:, :, :], ALU.max)
                        v.drain()
                        v.tensor_tensor(d[:, 0, :, :], me[:, :, :], mm[:, :, :], ALU.subtract)
                        v.tensor_tensor(d[:, 1, :, :], score[:, :, :], mm[:, :, :], ALU.subtract).then_inc(d_ok, 1)
                        dve.wait_ge(e_ok, n + 1)
                        v.tensor_tensor(den[:, 0, :, :], den[:, 0, :, :], d[:, 0, :, :], ALU.mult)
                        v.drain()
                        v.scalar_tensor_tensor(den[:, 1, :, :], den[:, 0, :, :], SM_EPS, d[:, 1, :, :], ALU.add, ALU.add)
                        v.drain()
                        v.reciprocal(den[:, 0, :, :], den[:, 1, :, :])
                        v.drain()
                        v.tensor_tensor(cc[:, :, :, :], d[:, :, :, :], den[:, 0:1, :, :].to_broadcast((P, 2, HS, HEADS)), ALU.mult).then_inc(c_ok, 1)
                        if following is not None:
                            exponentials(following, False)
                        v.drain()
                        if not first:
                            dve.wait_ge(aT_made, 4 * n)
                        for t in range(0, HS, 2):
                            k = min(2, HS - t)
                            v.tensor_tensor(agg[:, t:t + k, :, :].rearrange("p t h f -> p (t h) f"), bank[t // 2][:, 0:k * HF].rearrange("p (g f) -> p g f", f=F),
                                            cc[:, 0, t:t + k, :].rearrange("p t h -> p (t h)").unsqueeze(2).to_broadcast((P, k * HEADS, F)), ALU.mult)
                        v.drain()
                        dve.wait_ge(mine_ok, n + 1)
                        v.tensor_tensor(agg[:, :, :, :].rearrange("p t h f -> p (t h f)"), agg[:, :, :, :].rearrange("p t h f -> p (t h f)"),
                                        mine[:, :, :, :].rearrange("p t h f -> p (t h f)"), ALU.add).then_inc(agg_ok, 1)

                    def moments(s, m, last):
                        width = N - (NS - 1) * HS * P if last else HS * P
                        half = HS * P // 2
                        dve.wait_ge(readC, 2 * m + 2)
                        for k in range(2):
                            lo, hi = k * half, min((k + 1) * half, width)
                            if hi > lo:
                                v.bn_stats(stats[:, bass.ds(2 * m + k, 1), :].rearrange("p o c -> p (o c)"), oT[:, s, lo:hi])
                        v.drain()
                        v.sem_inc(stat_ok, 1)

                    def step(j, s, first):
                        n = 2 * j + s
                        last = isinstance(j, int) and n == NS - 1
                        weights(j, s, first, None if last else n + 1)
                        if not last:
                            matrices(n + 1, False)
                        if not first:
                            moments(1 - s, n - 1, False)
                    exponentials(0, True)
                    matrices(0, True)
                    step(0, 0, True)
                    step(0, 1, False)
                    with v.Fori(1, GI - 1) as j:
                        for s in range(2):
                            step(j, s, False)
                    step(GI - 1, 0, False)
                    step(GI - 1, 1, False)
                    moments(1, NS - 1, True)
                    used = 2 * NS if N - (NS - 1) * HS * P > HS * P // 2 else 2 * NS - 1
                    v.bn_aggr(mv[:, 0:2], stats[:, 0:used, :].rearrange("p k c -> p (k c)"))
                    v.drain()
                    v.sem_inc(var_ok, 1)
                    dve.wait_ge(sd_ok, 1)
                    v.reciprocal(mv[:, 3:4], mv[:, 2:3])
                    v.drain()
                    v.tensor_tensor(bn_col[:, 0:1], bn_col[:, 0:1], mv[:, 3:4], ALU.mult)
                    v.drain()
                    v.tensor_tensor(mv[:, 2:3], mv[:, 0:1], bn_col[:, 0:1], ALU.mult)
                    v.drain()
                    v.tensor_tensor(bn_col[:, 1:2], bn_col[:, 1:2], mv[:, 2:3], ALU.subtract)

        def batch_norm(tag):
            with nc.cleanup_on_exit(), ExitStack() as c, nc.Block() as block:
                tb = lambda name, shape, dt=f32: c.enter_context(nc.sbuf_tensor(tag + name, shape, dt))
                sm = lambda name: nc.alloc_semaphore(tag + name)
                two = lambda name: [sm(f"{name}{s}") for s in range(2)]
                oT = tb("oT", [F, 2, HS * P]); rT = tb("rT", [F, 2, HS * P])
                xn = tb("xn", [P, 2, HS, F]); h = tb("h", [P, 2, HS, F])
                bs = tb("bs", [P, 2, HS, 6]); ln = tb("ln", [P, 2, 8, HS])
                loaded, r_ok, turned, x_ok, x_kept, var_ok, sd_ok, ln_ok, h_ok, stored, go = (
                    two("loaded"), two("r_ok"), two("turned"), two("x_ok"), two("x_kept"), two("var_ok"), two("sd_ok"), two("ln_ok"), two("h_ok"), two("stored"), sm("go"))

                @block.sync
                def _(sp):
                    def body(j, first):
                        for s in range(2):
                            if not first:
                                sp.wait_ge(r_ok[s], j)
                            sp.dma_start(oT[:, s, :], gat_rows[:, bass.ds((j * BODY + s * HS) * P, HS * P)]).then_inc(loaded[s], 16)
                    body(0, True)
                    with nc.sync.Fori(1, GI) as j:
                        body(j, False)

                @block.gpsimd
                def _(pool):
                    with nc.gpsimd.Fori(0, GI) as j:
                        for s in range(2):
                            pool.wait_ge(h_ok[s], j + 1)
                            pool.sem_inc(go, 1)
                            pool.dma_start(tiles(node_g[bass.ds((j * BODY + s * HS) * P, HS * P), :]), h[:, s, :, :]).then_inc(stored[s], 16)
                    for s in range(2):
                        pool.wait_ge(stored[s], 16 * GI)

                @block.tensor
                def _(pe):
                    def body(j, first):
                        for s in range(2):
                            pe.wait_ge(r_ok[s], j + 1)
                            if not first:
                                pe.wait_ge(x_ok[s], j)
                            pe.sem_inc(go, 1)
                            for t in range(HS):
                                ins = nc.tensor.transpose(bank[s][:, t * F:(t + 1) * F], rT[:, s, t * P:(t + 1) * P], ident[0:F, 0:F])
                            ins.then_inc(turned[s], 1)
                    body(0, True)
                    with nc.tensor.Fori(1, GI) as j:
                        body(j, False)

                @block.scalar
                def _(act):
                    A = nc.scalar

                    def affine(j, s, first):
                        act.wait_ge(loaded[s], 16 * (j + 1))
                        if not first:
                            act.wait_ge(turned[s], j)
                        A.activation(rT[:, s, :], oT[:, s, :], ACT.Relu, bias=bn_col[:, 1:2], scale=bn_col[:, 0:1]).then_inc(r_ok[s], 1)

                    def rows_out(j, s, first):
                        act.wait_ge(x_ok[s], j + 1)
                        A.copy(x_sb[:, bass.ds(j * BODY + s * HS, HS), :], xn[:, s, :, :]).then_inc(x_kept[s], 1)
                        act.wait_ge(var_ok[s], j + 1)
                        A.activation(ln[:, s, 4, :], ln[:, s, 3, :], ACT.Sqrt, bias=eps[:, 0:1], scale=1.0 / F).then_inc(sd_ok[s], 1)
                        act.wait_ge(ln_ok[s], j + 1)
                        if not first:
                            act.wait_ge(stored[s], 16 * j)
                        for t in range(HS):
                            ins = A.activation(h[:, s, t, :], xn[:, s, t, :], ACT.Relu, bias=ln[:, s, 6, t:t + 1], scale=ln[:, s, 5, t:t + 1])
                        ins.then_inc(h_ok[s], 1)

                    def body(j, first, last):
                        for s in range(2):
                            rows_out(j, s, first)
                            if not last:
                                affine(j + 1, s, False)
                    for s in range(2):
                        affine(0, s, True)
                    body(0, True, False)
                    with A.Fori(1, GI - 1) as j:
                        body(j, False, False)
                    body(GI - 1, False, True)

                @block.vector
                def _(dve):
                    v = nc.vector

                    def body(j, first):
                        for s in range(2):
                            tl = bass.ds(j * BODY + s * HS, HS)
                            dve.wait_ge(turned[s], j + 1)
                            if not first:
                                dve.wait_ge(x_kept[s], j)
                                dve.wait_ge(h_ok[s], j)
                            v.tensor_tensor(xn[:, s, :, :], bank[s][:, 0:HS * F].rearrange("p (t f) -> p t f", t=HS), x_sb[:, tl, :], ALU.add).then_inc(x_ok[s], 1)
                            v.drain()
                            normalise(dve, j, s, tl, xn, bs, ln, var_ok, sd_ok, ln_ok, False)
                    body(0, True)
                    with v.Fori(1, GI) as j:
                        body(j, False)

        prepare()
        plan()
        nodes("n0", "start")
        regular = nc.values_load(fast[0:1, 0:1], min_val=0, max_val=1)
        with nc.If(regular):
            layer("l0", "conv", node_g, node_g2)
            layer("l1", "sage", node_g2, node_g)
            attention_weights()
            edge_scores("fs")
            segment_max("fm", True)
            attention("fa")
            batch_norm("fb")
            for k in range(3):
                layer(f"l{3 + k}", "typed", (node_g, node_g2, node_g)[k], (node_g2, node_g, None)[k], k)
        with nc.Else():
            clear_sums()
            edge_sums("e0", "wide", 2 * F, sums_w)
            nodes("n1", "conv")
            edge_sums("e1", "plain", F, sums_n)
            nodes("n2", "sage")
            edge_scores("es")
            segment_max("sm", False)
            edge_sums("e2", "gat", GATW, sums_a)
            attend("at")
            variance("bv")
            nodes("n3", "bn")
            for k in range(3):
                edge_sums(f"f{k}", "typed", 2 * F, sums_w)
                nodes(f"r{k}", "rel", k)


INPUTS = ["x", "src", "dst", "edge_attr_64", "edge_type_2", "L0_gnn_weight", "L0_gnn_bias", "L1_gnn_W", "L1_gnn_b",
          "L2_gnn_W_l", "L2_gnn_b_l", "L2_gnn_W_r", "L2_gnn_b_r", "L2_gnn_W_e", "L2_gnn_att", "L2_gnn_bias",
          "L2_gnn_gamma", "L2_gnn_beta", "L3_gnn_W0", "L3_gnn_Ws0", "L3_gnn_b0", "L3_gnn_W1", "L3_gnn_Ws1",
          "L3_gnn_b1", "L3_gnn_W2", "L3_gnn_Ws2", "L3_gnn_b2"]


def kernel(**inputs):
    import numpy as np
    import concourse.bacc as bacc
    from concourse.bass_utils import run_bass_kernel_spmd

    nc = bacc.Bacc("TRN2", target_bir_lowering=False, num_devices=1)
    arrays, args = {}, {}
    for name in INPUTS:
        v = np.ascontiguousarray(inputs[name])
        arrays[f"in_{name}"] = v
        args[name] = nc.dram_tensor(f"in_{name}", v.shape, mybir.dt.from_np(v.dtype), kind="ExternalInput").ap()
    shape = tuple(inputs["x"].shape)
    result = nc.dram_tensor("result", shape, mybir.dt.float32, kind="ExternalOutput").ap()
    build_gnn(nc, args, result)
    return run_bass_kernel_spmd(nc, [arrays], core_ids=[0]).results[0]["result"]
```

```python
import concourse.bass as bass
from concourse import mybir
from contextlib import ExitStack

P = 128
F = 64
HEADS = 4
HF = HEADS * F
HS = 7
BODY = 2 * HS
NBLK = 4
NEG = -1.0e30
SKIP = 2 ** 20
WT = HS + 1
WR = WT * P
SPLIT = 5
BAND = 2
FRONT = P
LN_EPS = 1e-5
BN_EPS = 1e-5
SM_EPS = 1e-16
SLOPE = 0.2
GATW = HF + 2 * HEADS


def build_gnn(nc, a, out):
    f32, bf16, i32 = mybir.dt.float32, mybir.dt.bfloat16, mybir.dt.int32
    ALU, ACT, AX = mybir.AluOpType, mybir.ActivationFunctionType, mybir.AxisListType

    N = a["x"].shape[0]
    FULL, REM = N // P, N % P
    T = -(-N // (P * 2 * BODY)) * 2 * BODY
    NP = T * P
    R = T // NBLK
    GI = T // BODY
    NS = T // HS
    HI = NP // 256
    assert a["src"].shape[0] == N and HI == 2 * R and R <= P

    def scratch(name, shape, dt=f32):
        return nc.dram_tensor(name, shape, dt, kind="Internal").ap()

    ER = FRONT + NP + WR
    dst_all = scratch("dst_rows", (ER,))
    dst_rows = dst_all[FRONT:ER]
    node_h = scratch("node_h", (NP, F))
    node_g = scratch("node_g", (NP, F))
    edge_all = scratch("edge_h", (ER, F))
    edge_h = edge_all[FRONT:ER, :]
    sums_w = scratch("sums_w", (NP, 2 * F))
    sums_n = scratch("sums_n", (NP, F))
    sums_a = scratch("sums_a", (NP, GATW))
    type_all = scratch("type_rows", (ER,))
    type_rows = type_all[FRONT:ER]
    src_all = scratch("src_rows", (ER,))
    src_rows = src_all[FRONT:ER]
    src_win = scratch("src_win", (NS * WR,))
    dst_win = scratch("dst_win", (NS * WR,))
    type_win = scratch("type_win", (NS * WR,))
    attr_all = scratch("edge_a", (ER, F))
    node_g2 = scratch("node_g2", (NP, F))
    inv_row = scratch("inv_row", (NP,))
    loop_rows = scratch("loop_rows", (F, NP))
    gat_out = scratch("gat_out", (NP, F))
    gat_rows = scratch("gat_rows", (F, NP))
    exp_all = scratch("edge_x", (2 * HEADS, ER))
    ends_d = scratch("ends_d", (HEADS, T, 2))
    ends_k = scratch("ends_k", (T, 2))
    ends_m = scratch("ends_m", (HEADS, T, 2))

    tiles = lambda ap: ap.rearrange("(t p) f -> p t f", p=P)

    ctx = ExitStack()
    with ctx:
        sb = lambda name, shape, dt=f32: ctx.enter_context(nc.sbuf_tensor(name, shape, dt))
        sem = lambda name: ctx.enter_context(nc.semaphore(name))
        bank = [ctx.enter_context(nc.psum_tensor(f"bank{i}", [P, 512], f32)) for i in range(8)]

        ident = sb("ident", [P, P])
        x_sb = sb("x_sb", [P, T, F])
        early = sb("early", [P, 12 * T + 2 * (T + BODY)])
        src_i, dst_i = (early[:, 12 * T + k * (T + BODY):12 * T + (k + 1) * (T + BODY)].bitcast(i32) for k in range(2))
        per_tile = early[:, 0:12 * T].rearrange("p (k t) -> p k t", t=T)
        put_i = per_tile[:, 0, :].bitcast(i32)
        dst_f, is_last, prev_f, norm, rs_send, upd_scale, inv_cnt = (per_tile[:, k, :] for k in range(1, 8))
        rel = per_tile[:, 8:10, :]
        cnt, real = per_tile[:, 10, :], per_tile[:, 11, :]
        no_edge = sb("no_edge", [P, T])
        eps = sb("eps", [P, 1])
        starts = sb("starts", [1, NS], i32)
        fast = sb("fast", [1, 1], i32)
        node_id = sb("node_id", [P, P])
        edge_id = sb("edge_id", [P, max(NS * HS * BAND, 3 * HF)])
        rel_w = sb("rel_w", [P, 2, NS * WT])
        src_w = sb("src_w", [P, NS * WT], i32)
        W1s = sb("W1s", [2 * F, F])
        attc = sb("attc", [P, 2, HEADS])
        attp = sb("attp", [P, 2, HEADS]); Vself = sb("Vself", [2 * F, HEADS])
        a_const = sb("a_const", [P, HEADS]); b_col = sb("b_col", [P, 4])
        o_col = sb("o_col", [F, 1]); bn_col = sb("bn_col", [F, 2])
        alpha = sb("alpha", [P, T, HEADS])
        amax = sb("amax", [P, T, HEADS])

        W0 = sb("W0", [F, F]); b0 = sb("b0", [P, F])
        W1 = sb("W1", [2 * F, F]); b1 = sb("b1", [P, F])
        Wlr = sb("Wlr", [2 * F, HF]); Wea = sb("Wea", [F, HF]); Wself = sb("Wself", [2 * F, HF])
        b_sum = sb("b_sum", [1, HF])
        Wr0 = edge_id[0:F, 2 * HF:3 * HF]
        brow = edge_id[0:1, 0:2 * HF].rearrange("p (j c) -> p j c", j=2)
        attb = sb("attb", [P, HF]); Wst = sb("Wst", [P, 2, F]); blb = sb("blb", [P, HF])
        b2 = sb("b2", [P, F]); gamma = sb("gamma", [P, F]); beta = sb("beta", [P, F])
        W3 = sb("W3", [P, 3, F]); Ws3 = sb("Ws3", [F, 3, F]); b3 = sb("b3", [P, 3, F])
        mu = sb("mu", [P, F]); bn_a = sb("bn_a", [P, F])
        ones1 = sb("ones1", [1, P]); onesP = sb("onesP", [P, P]); zeros_w = sb("zeros_w", [P, HS * F])


        def lent(buf, two_slots, fresh):
            flat = buf[:, :, :].rearrange("p a b -> p (a b)")
            if flat.shape[1] < two_slots:
                flat = fresh([P, two_slots])[:, :]
            return flat[:, 0:two_slots].rearrange("p (s t f) -> p s t f", s=2, f=F)

        def prepare():
            with nc.cleanup_on_exit(), ExitStack() as c, nc.Block() as block:
                tb = lambda name, shape, dt=f32: c.enter_context(nc.sbuf_tensor(name, shape, dt))
                sm = lambda name: nc.alloc_semaphore("pre_" + name)
                BP = NBLK * P
                work = tb("work", [P, max(9 * BP, 8 * T)])
                blocks = lambda lo, n: work[0:R, lo * BP:(lo + n) * BP].rearrange("r (j b p) -> r j b p", b=NBLK, p=P)
                raw = blocks(0, 3).bitcast(i32)
                rows = blocks(3, 4)
                nxt, last = blocks(7, 1)[:, 0], blocks(8, 1)[:, 0]
                row_i = tb("row_i", [P, P], i32); col_i = tb("col_i", [P, 1], i32)
                row_f = node_id; col_f = tb("col_f", [P, 1]); m127 = tb("m127", [P, 2])
                end_row = tb("end_row", [WT, 2, P])
                digits = lambda buf: buf[:, :, :].rearrange("p t h -> p (t h)").rearrange("p (j t) -> p j t", j=4)
                dig_i, dig = digits(amax).bitcast(i32), digits(alpha)
                iota_i = tb("iota_i", [P, 256], i32); iota_b = tb("iota_b", [P, 256], bf16)
                hi = tb("hi", [P, 2, 2, HS, HI], bf16)
                lo = tb("lo", [P, 2, 2, HS, 256], bf16)
                zb = zeros_w[:, 0:256].bitcast(bf16)
                hist = lo[0:R, 0, :, :, :].rearrange("p j t n -> p (j t n)")[:, 0:2048].bitcast(f32).rearrange("p (j n) -> p j n", j=2)
                cols = lambda lo, n: work[:, lo * T:(lo + n) * T].rearrange("p (j t) -> p j t", t=T)
                deg, sq, tmp = cols(0, 2), cols(2, 3), cols(5, 3)
                filled = sm("filled"); raw_in = sm("raw_in"); floats = sm("floats"); sent = sm("sent")
                dst_out = sm("dst_out"); nxt_in = sm("nxt_in"); put = sm("put"); ident_ok = sm("ident_ok")
                iotas = sm("iotas"); turned = sm("turned"); taken = sm("taken"); w_in = sm("w_in")
                x_in = sm("x_in"); oh = sm("oh"); counted = sm("counted"); hist_ok = sm("hist_ok")
                cleared = sm("cleared"); hist_t = sm("hist_t"); sq_in = sm("sq_in"); sq_out = sm("sq_out")
                oh_low = sm("oh_low"); low = tb("low", [P, 2, HS])
                dist = tb("dist", [P, SPLIT, 256], bf16)
                tails = sm("tails"); types_out = sm("types_out"); summed = sm("summed"); w_n = sm("w_n")
                x_parts = [(k * FULL // 4, (k + 1) * FULL // 4) for k in range(4)]
                names = ["src", "dst", "edge_type_2"]
                whole = (N // (R * P))
                rem_rows = (N - whole * R * P) // P

                @block.sync
                def _(sp):
                    sp.wait_ge(filled, 1)
                    n = 0
                    for j, name in enumerate(names):
                        v = a[name]
                        sp.dma_start(raw[:, j, 0:whole, :], v[0:whole * R * P].rearrange("(b r p) -> r b p", r=R, p=P)).then_inc(raw_in, 16)
                        at = whole * R * P
                        if rem_rows:
                            sp.dma_start(raw[0:rem_rows, j, whole, :], v[at:at + rem_rows * P].rearrange("(r p) -> r p", p=P)).then_inc(raw_in, 16)
                            n += 1
                        if REM:
                            sp.dma_start(raw[rem_rows:rem_rows + 1, j, whole, 0:REM], v[FULL * P:N].rearrange("(o p) -> o p", o=1)).then_inc(raw_in, 16)
                            n += 1
                        n += 1
                    sp.sem_inc(w_n, 1)
                    sp.wait_ge(floats, 1)
                    sp.dma_start(dst_rows[0:NP].rearrange("(b r p) -> r b p", r=R, p=P), rows[:, 1, :, :]).then_inc(dst_out, 16)
                    sp.dma_start(dst_rows[NP:NP + WR].rearrange("(q p) -> q p", p=P), end_row[:, 0, :]).then_inc(dst_out, 16)
                    sp.wait_ge(dst_out, 32)
                    sp.dma_start(nxt[:, :, :], dst_rows[1:NP + 1].rearrange("(b r p) -> r b p", r=R, p=P)).then_inc(nxt_in, 16)
                    for lo_t, hi_t in x_parts:
                        sp.dma_start(x_sb[:, lo_t:hi_t, :], tiles(a["x"][lo_t * P:hi_t * P, :])).then_inc(x_in, 16)
                    if REM:
                        sp.dma_start(x_sb[0:REM, FULL, :], a["x"][FULL * P:N, :]).then_inc(x_in, 16)
                    sp.dma_start(type_rows[0:NP].rearrange("(b r p) -> r b p", r=R, p=P), rows[:, 2, :, :]).then_inc(types_out, 16)
                    sp.dma_start(type_rows[NP:NP + WR].rearrange("(q p) -> q p", p=P), end_row[:, 1, :]).then_inc(tails, 16)
                    sp.dma_start(src_rows[0:NP].rearrange("(b r p) -> r b p", r=R, p=P), rows[:, 0, :, :]).then_inc(types_out, 16)
                    sp.dma_start(src_rows[NP:NP + WR].rearrange("(q p) -> q p", p=P), end_row[:, 1, :]).then_inc(tails, 16)
                    n = 2
                    for to, j in ((dst_all, 0), (type_all, 1), (src_all, 1)):
                        sp.dma_start(to[0:FRONT].rearrange("(o p) -> o p", p=P), end_row[0:1, j, :]).then_inc(tails, 16)
                        n += 1
                    for to, lo, hi_row in ((attr_all, 0, FRONT), (edge_all, 0, FRONT), (attr_all, FRONT + N, ER), (edge_all, FRONT + NP, ER)):
                        for r0 in range(lo, hi_row, P):
                            r1 = min(r0 + P, hi_row)
                            sp.dma_start(to[r0:r1, :], zeros_w[0:r1 - r0, 0:F]).then_inc(tails, 16)
                            n += 1
                    CUT = 16 if N % 16 == 0 else 8
                    sp.dma_start(attr_all[FRONT:FRONT + N, :].rearrange("(c n) f -> c (n f)", c=CUT), a["edge_attr_64"].rearrange("(c n) f -> c (n f)", c=CUT)).then_inc(tails, 16)
                    sp.wait_ge(tails, 16 * (n + 1))
                    sp.wait_ge(x_in, 16 * (len(x_parts) + (1 if REM else 0)))

                n_raw = 3 * (1 + (1 if rem_rows else 0) + (1 if REM else 0))

                @block.scalar
                def _(act):
                    bc = lambda v: v.rearrange("(o f) -> o f", o=1).to_broadcast((P, v.shape[0]))
                    att = a["L2_gnn_att"].rearrange("h f -> (h f)")
                    wl = a["L2_gnn_W_l"]
                    loads = [
                        (W0[:, :], a["L0_gnn_weight"]), (b0[:, :], bc(a["L0_gnn_bias"])),
                        (W1[:, :], a["L1_gnn_W"]), (W1s[0:F, :], a["L1_gnn_W"][F:2 * F, :]), (W1s[F:2 * F, :], a["L1_gnn_W"][0:F, :]), (b1[:, :], bc(a["L1_gnn_b"])),
                        (Wlr[0:F, :], wl), (Wlr[F:2 * F, :], a["L2_gnn_W_r"]), (Wr0[:, :], a["L2_gnn_W_r"]),
                        (Wea[:, :], a["L2_gnn_W_e"]), (Wself[0:F, :], wl), (Wself[F:2 * F, :], a["L2_gnn_W_e"]),
                        (brow[0:1, 0, :], a["L2_gnn_b_l"].rearrange("(o f) -> o f", o=1)),
                        (brow[0:1, 1, :], a["L2_gnn_b_r"].rearrange("(o f) -> o f", o=1)),
                        (attb[:, :], bc(att)), (blb[:, :], bc(a["L2_gnn_b_l"])),
                        (b2[:, :], bc(a["L2_gnn_bias"])), (gamma[:, :], bc(a["L2_gnn_gamma"])), (beta[:, :], bc(a["L2_gnn_beta"])),
                    ]
                    for h in range(HEADS):
                        loads.append((Wst[(h % 2) * F:(h % 2 + 1) * F, h // 2, :], wl[:, h * F:(h + 1) * F]))
                    for k in range(3):
                        loads.append((W3[:, k, :], a[f"L3_gnn_W{k}"].rearrange("r d o -> (r d) o")))
                        loads.append((Ws3[:, k, :], a[f"L3_gnn_Ws{k}"]))
                        loads.append((b3[:, k, :], bc(a[f"L3_gnn_b{k}"])))
                    for to, of in loads:
                        act.dma_start(to, of).then_inc(w_in, 16)
                    act.wait_ge(cleared, 1)
                    A = nc.scalar

                    def body(i, first):
                        for s in range(2):
                            A.mul(low[:, s, :], dig[:, 1, bass.ds(i * BODY + s * HS, HS)], -1.0)
                            act.drain()
                            for t in range(SPLIT):
                                A.activation(dist[:, t, :], iota_b[:, :], ACT.Abs, bias=low[:, s, t:t + 1], scale=1.0)
                            act.drain()
                            if not first:
                                act.wait_ge(counted, 2 * i + s - 1)
                            A.activation(lo[:, s, 0, 0:SPLIT, :], dist[:, :, :], ACT.Relu, bias=onesP[:, 0:1], scale=-1.0).then_inc(oh_low, 1)
                    body(0, True)
                    with A.Fori(1, GI) as i:
                        body(i, False)
                    act.wait_ge(w_in, 16 * len(loads))
                    act.sem_inc(w_n, 1)
                    act.wait_ge(sq_in, 1)
                    nc.scalar.activation(sq[:, :, :], tmp[:, :, :], ACT.Sqrt).then_inc(sq_out, 1)

                @block.gpsimd
                def _(pool):
                    nc.gpsimd.iota(row_i[:, :], pattern=[[1, P]], base=0, channel_multiplier=0)
                    nc.gpsimd.iota(col_i[:, :], pattern=[[0, 1]], base=0, channel_multiplier=1)
                    nc.gpsimd.iota(iota_i[:, :], pattern=[[1, 256]], base=0, channel_multiplier=0).then_inc(iotas, 1)

                @block.vector
                def _(dve):
                    v = nc.vector
                    for j in range(2):
                        v.memset(raw[:, j, :, :], NP - 1)
                    v.memset(raw[:, 2, :, :], 0)
                    v.memset(x_sb[:, FULL:T, :], 0.0)
                    v.memset(end_row[:, 0, :], float(NP))
                    v.memset(end_row[:, 1, :], 0.0)
                    v.memset(src_i[:, T:], 0)
                    v.memset(dst_i[:, T:], 0)
                    v.memset(eps[:, :], LN_EPS)
                    v.memset(ones1[:, :], 1.0)
                    v.memset(onesP[:, :], 1.0)
                    v.memset(zeros_w[:, :], 0.0).then_inc(filled, 1)
                    dve.wait_ge(iotas, 1)
                    v.tensor_copy(row_f[:, :], row_i[:, :])
                    v.tensor_copy(col_f[:, :], col_i[:, :])
                    v.tensor_copy(iota_b[:, :], iota_i[:, :])
                    v.drain()
                    v.tensor_scalar(ident[:, :], row_f[:, :], col_f[:, 0:1], None, ALU.is_equal).then_inc(ident_ok, 1)
                    v.tensor_scalar(m127[:, 0:1], col_f[:, :], float(P - 1), None, ALU.is_equal)
                    v.tensor_scalar(m127[:, 1:2], col_f[:, :], float(P - 1), -1.0, ALU.not_equal, ALU.mult)
                    dve.wait_ge(raw_in, 16 * n_raw)
                    v.tensor_copy(rows[:, 0:3, :, :].rearrange("r j b p -> r (j b p)"), raw[:, :, :, :].rearrange("r j b p -> r (j b p)")).then_inc(floats, 1)
                    dve.wait_ge(nxt_in, 16)
                    v.tensor_tensor(last[:, :, :], rows[:, 1, :, :], nxt[:, :, :], ALU.is_equal)
                    v.drain()
                    v.scalar_tensor_tensor(rows[:, 3, :, :], last[:, :, :], float(SKIP), rows[:, 1, :, :], ALU.mult, ALU.add).then_inc(put, 1)
                    dve.wait_ge(turned, 1)
                    v.tensor_copy(src_i[:, 0:T], bank[0][:, 0:T])
                    v.tensor_copy(dst_f[:, :], bank[1][:, 0:T])
                    v.tensor_copy(dst_i[:, 0:T], bank[1][:, 0:T])
                    v.tensor_scalar(rel[:, 0, :], bank[2][:, 0:T], 0.0, None, ALU.is_equal)
                    v.tensor_scalar(rel[:, 1, :], bank[2][:, 0:T], 0.0, None, ALU.not_equal)
                    v.tensor_copy(put_i[:, :], bank[3][:, 0:T])
                    v.tensor_scalar(is_last[:, :], bank[3][:, 0:T], float(SKIP), None, ALU.is_lt)
                    v.drain()
                    v.memset(prev_f[:, 0:1], -1.0)
                    v.tensor_scalar(prev_f[:, 1:T], dst_f[:, 0:T - 1], m127[:, 0:1], m127[:, 1:2], ALU.mult, ALU.add)
                    for j, idx in enumerate((src_i, dst_i)):
                        v.tensor_scalar(dig_i[:, 2 * j, :], idx[:, 0:T], 8, None, ALU.arith_shift_right)
                        v.tensor_scalar(dig_i[:, 2 * j + 1, :], idx[:, 0:T], 255, None, ALU.bitwise_and)
                    v.drain()
                    v.tensor_copy(dig[:, :, :], dig_i[:, :, :])
                    v.memset(real[:, 0:FULL], 1.0)
                    v.memset(real[:, FULL:T], 0.0)
                    v.drain()
                    if REM:
                        v.memset(real[0:REM, FULL:FULL + 1], 1.0)
                    v.drain()
                    v.sem_inc(cleared, 1)

                    def body(i, first):
                        for s in range(2):
                            if not first:
                                dve.wait_ge(counted, 2 * i + s - 1)
                            for t in range(HS):
                                for j in range(2):
                                    g = i * BODY + s * HS + t
                                    ins = v.tensor_scalar(hi[:, s, j, t, :], iota_b[:, 0:HI], dig[:, 2 * j, bass.ds(g, 1)], None, ALU.is_equal)
                                    if j == 1 or t >= SPLIT:
                                        ins = v.tensor_scalar(lo[:, s, j, t, :], iota_b[:, :], dig[:, 2 * j + 1, bass.ds(g, 1)], None, ALU.is_equal)
                            ins.then_inc(oh, 1)
                    body(0, True)
                    with v.Fori(1, GI) as i:
                        body(i, False)
                    dve.wait_ge(summed, 1)
                    for j in range(2):
                        ins = v.tensor_copy(hist[:, j, :], bank[4 + j][0:R, :])
                    ins.then_inc(hist_ok, 1)
                    dve.wait_ge(hist_t, 1)
                    dve.wait_ge(types_out, 32)
                    for j in range(2):
                        for k in range(2):
                            for half in range(2):
                                d0 = deg[:, j, :].rearrange("p (k r h) -> p k r h", k=2, h=2)[:, k, :, half]
                                v.tensor_copy(d0, bank[j][:, (2 * k + half) * R:(2 * k + half + 1) * R])
                    v.drain()
                    v.tensor_copy(cnt[:, :], deg[:, 1, :])
                    v.tensor_scalar(tmp[:, 0, :], deg[:, 1, :], 1.0, None, ALU.max)
                    v.tensor_scalar(tmp[:, 1, :], deg[:, 0, :], 1.0, None, ALU.add)
                    v.tensor_scalar(tmp[:, 2, :], deg[:, 1, :], 1.0, None, ALU.add)
                    v.tensor_scalar(no_edge[:, :], deg[:, 1, :], 0.0, NEG, ALU.is_equal, ALU.mult)
                    v.drain()
                    v.sem_inc(sq_in, 1)
                    v.reciprocal(inv_cnt[:, :], tmp[:, 0, :])
                    dve.wait_ge(sq_out, 1)
                    v.reciprocal(norm[:, :], sq[:, 0, :])
                    v.reciprocal(rs_send[:, :], sq[:, 1, :])
                    v.tensor_tensor(upd_scale[:, :], sq[:, 2, :], tmp[:, 2, :], ALU.mult)
                    v.drain()
                    v.reciprocal(upd_scale[:, :], upd_scale[:, :])
                    dve.wait_ge(w_n, 2)
                    v.tensor_tensor(Wself[0:F, :], Wself[0:F, :], Wr0[:, :], ALU.add)
                    v.tensor_tensor(b_sum[:, :], brow[0:1, 0, :], brow[0:1, 1, :], ALU.add)
                    v.tensor_reduce(mu[:, :], blb[:, :].rearrange("p (h o) -> p o h", h=HEADS), AX.X, ALU.add)
                    v.drain()
                    v.scalar_tensor_tensor(b2[:, :], mu[:, :], 1.0 / HEADS, b2[:, :], ALU.mult, ALU.add)

                @block.tensor
                def _(pe):
                    pe.wait_ge(ident_ok, 1)
                    pe.wait_ge(floats, 1)
                    pe.wait_ge(put, 1)
                    for j in range(4):
                        for b in range(NBLK):
                            ins = nc.tensor.transpose(bank[j][:, b * R:(b + 1) * R], rows[:, j, b, :], ident[0:R, 0:R])
                    ins.then_inc(turned, 1)
                    pe.wait_ge(cleared, 1)
                    for j in range(2):
                        nc.tensor.matmul(bank[4 + j][0:R, :], zb[:, 0:R], zb[:, :], start=True, stop=False)

                    def body(i, first):
                        for s in range(2):
                            pe.wait_ge(oh, 2 * i + s + 1)
                            pe.wait_ge(oh_low, 2 * i + s + 1)
                            for t in range(HS):
                                for j in range(2):
                                    for k in range(2):
                                        ins = nc.tensor.matmul(bank[4 + j][0:R, k * 256:(k + 1) * 256], hi[:, s, j, t, k * R:(k + 1) * R],
                                                               lo[:, s, j, t, :], start=False, stop=False)
                            ins.then_inc(counted, 1)
                    with nc.tensor.Fori(0, GI) as i:
                        body(i, False)
                    for j in range(2):
                        ins = nc.tensor.matmul(bank[4 + j][0:R, :], zb[:, 0:R], zb[:, :], start=False, stop=True)
                    ins.then_inc(summed, 1)
                    pe.wait_ge(hist_ok, 1)
                    for j in range(2):
                        for k in range(2):
                            for half in range(2):
                                ins = nc.tensor.transpose(bank[j][:, (2 * k + half) * R:(2 * k + half + 1) * R],
                                                          hist[:, j, k * 256 + half * P:k * 256 + (half + 1) * P], ident[0:R, 0:R])
                    ins.then_inc(hist_t, 1)

        def edge_sums(tag, kind, W, sums):
            with nc.cleanup_on_exit(), ExitStack() as c, nc.Block() as block:
                tb = lambda name, shape, dt=f32: c.enter_context(nc.sbuf_tensor(tag + name, shape, dt))
                sm = lambda name: nc.alloc_semaphore(tag + name)
                two = lambda name: [sm(f"{name}{s}") for s in range(2)]
                drow = tb("drow", [P, 2, HS, P])
                same = tb("same", [P, 2, HS, P]); carry = tb("carry", [P, 2, HS, P])
                got = None
                if kind in ("typed", "gat"):
                    got = lent(rel_w, 2 * HS * F, lambda shape: tb("got", shape))
                msg = tb("msg", [P, 2, HS, W])
                tot = tb("tot", [P, 2, HS, W])
                src_st = tb("src_st", [P, 2, HS], i32); put_st = tb("put_st", [P, 2, HS], i32)
                ex = tb("ex", [P, 2, HS, HEADS]) if kind == "gat" else None
                zero = tb("zero", [P, 1848]) if kind == "wide" else None
                rows_in, side_in, gathered, src_ok, put_ok = two("rows_in"), two("side_in"), two("gathered"), two("src_ok"), two("put_ok")
                built, msg_ok, scat = two("built"), two("msg_ok"), two("scat")
                sums_ok, tot_ok, start0, go, exp_in, exp_ok = sm("sums_ok"), sm("tot_ok"), sm("start0"), sm("go"), two("exp_in"), two("exp_ok")
                zeroed = sm("zeroed"); z0 = sm("z0")
                uses_gather = kind != "gat"
                direct = kind in ("wide", "plain")
                gbuf = msg if direct else got
                PER = 16 * HS

                @block.sync
                def _(sp):
                    if kind == "wide":
                        sp.wait_ge(z0, 1)
                        per = 1848 // GATW
                        za = sums_a.rearrange("(g p r) f -> g p (r f)", p=P, r=per)
                        for g in range(za.shape[0]):
                            sp.dma_start(za[g], zero[:, 0:per * GATW]).then_inc(zeroed, 16)

                    def body(i, first, last):
                        for s in range(2):
                            at = i * BODY + s * HS
                            if not first:
                                sp.wait_ge(built[s], i)
                            sp.dma_start(drow[:, s, :, :].rearrange("p t q -> p (t q)"),
                                         dst_rows[bass.ds(at * P, HS * P)].rearrange("(o n) -> o n", o=1).to_broadcast((P, HS * P))).then_inc(rows_in[s], 16)
                            if kind == "wide":
                                if not first:
                                    sp.wait_ge(sums_ok, (i - 1) * BODY + (s + 1) * HS)
                                if not last or (i * BODY + s * HS + HS) <= FULL:
                                    sp.dma_start(msg[:, s, :, F:2 * F], tiles(a["edge_attr_64"][bass.ds(at * P, HS * P), :])).then_inc(side_in[s], 16)
                                else:
                                    n = FULL - at
                                    if n > 0:
                                        sp.dma_start(msg[:, s, 0:n, F:2 * F], tiles(a["edge_attr_64"][at * P:FULL * P, :])).then_inc(side_in[s], 16)
                                    if REM:
                                        sp.dma_start(msg[0:REM, s, n, F:2 * F], a["edge_attr_64"][FULL * P:N, :]).then_inc(side_in[s], 16)
                            if kind == "gat":
                                if not first:
                                    sp.wait_ge(msg_ok[s], i)
                                sp.dma_start(got[:, s, :, :], tiles(edge_h[bass.ds(at * P, HS * P), :])).then_inc(side_in[s], 16)
                    body(0, True, False)
                    with nc.sync.Fori(1, GI - 1) as i:
                        body(i, False, False)
                    body(GI - 1, False, True)
                    if kind == "wide":
                        sp.wait_ge(zeroed, 16 * (NP // P // (1848 // GATW)))

                def side_total(i, s, last):
                    if last and kind == "wide" and (i * BODY + s * HS + HS) > FULL:
                        n = FULL - (i * BODY + s * HS)
                        return 16 * i + 16 * ((1 if n > 0 else 0) + (1 if REM else 0))
                    return 16 * (i + 1)

                @block.gpsimd
                def _(pool):
                    def gather(i, s, first):
                        pool.wait_ge(src_ok[s], i + 1)
                        if not first:
                            if direct:
                                pool.wait_ge(sums_ok, (i - 1) * BODY + (s + 1) * HS)
                            else:
                                pool.wait_ge(msg_ok[s], i)
                        pool.sem_inc(go, 1)
                        for t in range(HS):
                            pool.indirect_dma_start(out=gbuf[:, s, t, 0:F], out_offset=None, in_=node_g,
                                                    in_offset=bass.IndirectOffsetOnAxis(ap=src_st[:, s, t:t + 1], axis=0)).then_inc(gathered[s], 16)

                    def scatter(i, s):
                        pool.wait_ge(put_ok[s], i + 1)
                        pool.wait_ge(tot_ok, i * BODY + (s + 1) * HS)
                        pool.sem_inc(go, 1)
                        for t in range(HS):
                            pool.indirect_dma_start(out=sums, out_offset=bass.IndirectOffsetOnAxis(ap=put_st[:, s, t:t + 1], axis=0),
                                                    in_=tot[:, s, t, :], in_offset=None, bounds_check=NP - 1, oob_is_err=False).then_inc(scat[s], 16)

                    def body(i, first, last):
                        if uses_gather:
                            gather(i, 1, first)
                        scatter(i, 0)
                        if uses_gather and not last:
                            gather(i + 1, 0, False)
                        scatter(i, 1)
                    if uses_gather:
                        gather(0, 0, True)
                    body(0, True, False)
                    with nc.gpsimd.Fori(1, GI - 1) as i:
                        body(i, False, False)
                    body(GI - 1, False, True)
                    for s in range(2):
                        pool.wait_ge(scat[s], PER * GI)

                @block.vector
                def _(dve):
                    v = nc.vector
                    if kind == "wide":
                        v.memset(zero[:, :], 0.0).then_inc(z0, 1)
                    v.memset(tot[:, 1, HS - 1, :], 0.0)
                    v.drain()
                    v.sem_inc(start0, 1)
                    if uses_gather:
                        for s in range(2):
                            v.tensor_copy(src_st[:, s, :], src_i[:, s * HS:(s + 1) * HS]).then_inc(src_ok[s], 1)

                    def body(i, first):
                        for s in range(2):
                            at = i * BODY + s * HS
                            dve.wait_ge(rows_in[s], 16 * (i + 1))
                            if not first:
                                dve.wait_ge(sums_ok, (i - 1) * BODY + (s + 1) * HS)
                            v.tensor_tensor(same[:, s, :, :], drow[:, s, :, :], dst_f[:, bass.ds(at, HS)].unsqueeze(2).to_broadcast((P, HS, P)), ALU.is_equal)
                            v.tensor_tensor(carry[:, s, :, :], drow[:, s, :, :], prev_f[:, bass.ds(at, HS)].unsqueeze(2).to_broadcast((P, HS, P)), ALU.is_equal).then_inc(built[s], 1)
                            if not first:
                                dve.wait_ge(scat[s], PER * i)
                                dve.wait_ge(start0, 1)
                            v.tensor_copy(put_st[:, s, :], put_i[:, bass.ds(at, HS)]).then_inc(put_ok[s], 1)
                            if kind == "typed":
                                dve.wait_ge(gathered[s], PER * (i + 1))
                                for r in range(2):
                                    ins = v.tensor_tensor(msg[:, s, :, r * F:(r + 1) * F], got[:, s, :, :],
                                                          rel[:, r, bass.ds(at, HS)].unsqueeze(2).to_broadcast((P, HS, F)), ALU.mult)
                                ins.then_inc(msg_ok[s], 1)
                            if kind == "gat":
                                v.tensor_tensor(ex[:, s, :, :], alpha[:, bass.ds(at, HS), :], amax[:, bass.ds(at, HS), :], ALU.subtract).then_inc(exp_in[s], 1)
                                v.tensor_tensor(msg[:, s, :, HF + HEADS:GATW], amax[:, bass.ds(at, HS), :],
                                                is_last[:, bass.ds(at, HS)].unsqueeze(2).to_broadcast((P, HS, HEADS)), ALU.mult)
                                dve.wait_ge(exp_ok[s], i + 1)
                                v.tensor_copy(msg[:, s, :, HF:HF + HEADS], ex[:, s, :, :])
                                dve.wait_ge(side_in[s], 16 * (i + 1))
                                for h in range(HEADS):
                                    ins = v.tensor_tensor(msg[:, s, :, h * F:(h + 1) * F], got[:, s, :, :],
                                                          ex[:, s, :, h:h + 1].to_broadcast((P, HS, F)), ALU.mult)
                                ins.then_inc(msg_ok[s], 1)
                            if uses_gather:
                                dve.wait_ge(gathered[s], PER * (i + 1))
                                dve.wait_ge(start0, 1)
                                v.tensor_copy(src_st[:, s, :], src_i[:, bass.ds(at + BODY, HS)]).then_inc(src_ok[s], 1)
                    body(0, True)
                    with v.Fori(1, GI) as i:
                        body(i, False)

                @block.tensor
                def _(pe):
                    pe.wait_ge(start0, 1)

                    def tile_sums(i, s, t, first):
                        k = i * BODY + s * HS + t
                        if not (first and s == 0):
                            pe.wait_ge(tot_ok, k - HS + 1)
                        nc.tensor.matmul(bank[t][:, 0:W], same[:, s, t, :], msg[:, s, t, :], start=True, stop=False)

                    def tile_carry(i, s, t, first):
                        k = i * BODY + s * HS + t
                        if not (first and s == 0 and t == 0):
                            pe.wait_ge(tot_ok, k)
                        prev = tot[:, s, t - 1, :] if t else tot[:, 1 - s, HS - 1, :]
                        nc.tensor.matmul(bank[t][:, 0:W], carry[:, s, t, :], prev, start=False, stop=True).then_inc(sums_ok, 1)

                    def body(i, first, last):
                        for s in range(2):
                            pe.wait_ge(built[s], i + 1)
                            if direct:
                                pe.wait_ge(gathered[s], PER * (i + 1))
                            if kind == "wide":
                                pe.wait_ge(side_in[s], side_total(i, s, last))
                            if not direct:
                                pe.wait_ge(msg_ok[s], i + 1)
                            tile_sums(i, s, 0, first)
                            for t in range(HS):
                                if t + 1 < HS:
                                    tile_sums(i, s, t + 1, first)
                                tile_carry(i, s, t, first)
                    body(0, True, False)
                    with nc.tensor.Fori(1, GI - 1) as i:
                        body(i, False, False)
                    body(GI - 1, False, True)

                @block.scalar
                def _(act):
                    act.wait_ge(start0, 1)

                    def body(i, first):
                        for s in range(2):
                            if kind == "gat":
                                act.wait_ge(exp_in[s], i + 1)
                                nc.scalar.activation(ex[:, s, :, :], ex[:, s, :, :], ACT.Exp).then_inc(exp_ok[s], 1)
                            if not first:
                                act.wait_ge(scat[s], PER * i)
                            for t in range(HS):
                                act.wait_ge(sums_ok, i * BODY + s * HS + t + 1)
                                nc.scalar.copy(tot[:, s, t, :], bank[t][:, 0:W]).then_inc(tot_ok, 1)
                    body(0, True)
                    with nc.scalar.Fori(1, GI) as i:
                        body(i, False)

        def nodes(tag, kind, layer=0):
            with nc.cleanup_on_exit(), ExitStack() as c, nc.Block() as block:
                tb = lambda name, shape, dt=f32: c.enter_context(nc.sbuf_tensor(tag + name, shape, dt))
                sm = lambda name: nc.alloc_semaphore(tag + name)
                two = lambda name: [sm(f"{name}{s}") for s in range(2)]
                adds = kind in ("conv", "sage", "bn")
                norms = kind in ("start", "conv", "sage", "bn")
                turn = {"conv": F, "sage": 2 * F, "rel": 2 * F}.get(kind, 0)
                inp = tb("inp", [P, 2, HS, turn or F])
                inp2 = tb("inp2", [P, 2, HS, F])
                inpT = tb("inpT", [P, 2, HS, P]); inp2T = tb("inp2T", [F, 2, HS, P])
                o = tb("o", [P, 2, HS, F])
                xc = tb("xc", [P, 2, HS, F]); sq = tb("sq", [P, 2, HS, F])
                st = tb("st", [P, 2, 4, HS])
                h = tb("h", [P, 2, HS, F]); g = tb("g", [P, 2, HS, F])
                loaded, tin, turned, tout = two("loaded"), two("tin"), two("turned"), two("tout")
                prod, xc_ok, sq_ok, var_ok, sd_ok, z_ok, h_ok, g_ok, stored = (two(n) for n in ("prod", "xc_ok", "sq_ok", "var_ok", "sd_ok", "z_ok", "h_ok", "g_ok", "stored"))
                used, o_free, go = two("used"), two("o_free"), sm("go")
                scaled = {"start": norm, "conv": rs_send}.get(kind)
                n_in = {"start": 0, "conv": 1, "sage": 3, "bn": 1, "rel": 2}[kind]
                n_out = 2 if kind == "conv" else 1
                final = kind == "rel" and layer == 2
                CH = [(0, 4), (4, HS)]

                @block.sync
                def _(sp):
                    def body(i, first):
                        for s in range(2):
                            at = bass.ds((i * BODY + s * HS) * P, HS * P)
                            if not first and n_in:
                                sp.wait_ge(used[s], i)
                            if kind == "conv":
                                sp.dma_start(inp[:, s, :, :], tiles(sums_w[at, 0:F])).then_inc(loaded[s], 16)
                            if kind == "sage":
                                sp.dma_start(inp[:, s, :, 0:F], tiles(node_h[at, :])).then_inc(loaded[s], 16)
                                sp.dma_start(inp[:, s, :, F:2 * F], tiles(sums_n[at, :])).then_inc(loaded[s], 16)
                                sp.dma_start(inp2[:, s, :, :], tiles(node_g[at, :])).then_inc(loaded[s], 16)
                            if kind == "bn":
                                sp.dma_start(inp2[:, s, :, :], tiles(gat_out[at, :])).then_inc(loaded[s], 16)
                            if kind == "rel":
                                sp.dma_start(inp[:, s, :, :], tiles(sums_w[at, :])).then_inc(loaded[s], 16)
                                sp.dma_start(inp2[:, s, :, :], tiles(node_g[at, :])).then_inc(loaded[s], 16)
                    if n_in:
                        body(0, True)
                        with nc.sync.Fori(1, GI) as i:
                            body(i, False)

                @block.gpsimd
                def _(pool):
                    pool.drain()
                    def body(i, first):
                        for s in range(2):
                            at = bass.ds((i * BODY + s * HS) * P, HS * P)
                            tl = bass.ds(i * BODY + s * HS, HS)
                            pool.wait_ge(h_ok[s], i + 1)
                            if scaled is not None:
                                pool.wait_ge(g_ok[s], i + 1)
                            pool.sem_inc(go, 1)
                            if kind == "conv":
                                pool.dma_start(tiles(node_h[at, :]), h[:, s, :, :]).then_inc(stored[s], 16)
                            if scaled is not None:
                                pool.dma_start(tiles(node_g[at, :]), g[:, s, :, :]).then_inc(stored[s], 16)
                            else:
                                pool.dma_start(tiles(node_g[at, :]), h[:, s, :, :]).then_inc(stored[s], 16)
                    if not final:
                        body(0, True)
                        with nc.gpsimd.Fori(1, GI) as i:
                            body(i, False)
                        for s in range(2):
                            pool.wait_ge(stored[s], 16 * n_out * GI)
                    else:
                        def tail(i, last):
                            for s in range(2):
                                at = i * BODY + s * HS
                                pool.wait_ge(h_ok[s], i + 1)
                                pool.sem_inc(go, 1)
                                if not last or at + HS <= FULL:
                                    pool.dma_start(tiles(out[bass.ds(at * P, HS * P), :]), h[:, s, :, :]).then_inc(stored[s], 16)
                                else:
                                    n = FULL - at
                                    if n > 0:
                                        pool.dma_start(tiles(out[at * P:FULL * P, :]), h[:, s, 0:n, :]).then_inc(stored[s], 16)
                                    if REM:
                                        pool.dma_start(out[FULL * P:N, :], h[0:REM, s, n, :]).then_inc(stored[s], 16)
                        with nc.gpsimd.Fori(0, GI - 1) as i:
                            tail(i, False)
                        tail(GI - 1, True)
                        for s in range(2):
                            at = (GI - 1) * BODY + s * HS
                            extra = 1 if at + HS <= FULL else (1 if FULL > at else 0) + (1 if REM else 0)
                            pool.wait_ge(stored[s], 16 * (GI - 1 + extra))

                @block.tensor
                def _(pe):
                    if not turn:
                        return
                    W = {"conv": W0[:, :], "sage": W1[:, :], "rel": W3[:, layer, :]}[kind]

                    def body(i, first):
                        for s in range(2):
                            pe.wait_ge(loaded[s], 16 * n_in * (i + 1))
                            if kind == "sage":
                                pe.wait_ge(tin[s], i + 1)
                            if not (first and s == 0):
                                pe.wait_ge(tout[1 - s], i + s)
                            pe.sem_inc(go, 1)
                            for b, (t0, t1) in enumerate(CH):
                                for t in range(t0, t1):
                                    ins = nc.tensor.transpose(bank[b][0:turn, (t - t0) * P:(t - t0 + 1) * P], inp[:, s, t, :], ident[:, :])
                            if kind == "rel":
                                for b, (t0, t1) in enumerate(CH):
                                    for t in range(t0, t1):
                                        ins = nc.tensor.transpose(bank[2 + b][0:F, (t - t0) * P:(t - t0 + 1) * P], inp2[:, s, t, :], ident[:, :])
                            ins.then_inc(turned[s], 1)
                            pe.wait_ge(tout[s], i + 1)
                            if not first:
                                pe.wait_ge(o_free[s], i)
                            for t in range(HS):
                                ins = nc.tensor.matmul(bank[4 + s][:, t * F:(t + 1) * F], inpT[0:turn, s, t, :], W, start=True, stop=kind != "rel")
                                if kind == "rel":
                                    ins = nc.tensor.matmul(bank[4 + s][:, t * F:(t + 1) * F], inp2T[:, s, t, :], Ws3[:, layer, :], start=False, stop=True)
                            ins.then_inc(prod[s], 1)
                    body(0, True)
                    with nc.tensor.Fori(1, GI) as i:
                        body(i, False)

                @block.scalar
                def _(act):
                    A = nc.scalar

                    def body(i, first):
                        if turn:
                            for s in range(2):
                                act.wait_ge(turned[s], i + 1)
                                if not first:
                                    act.wait_ge(prod[s], i)
                                for b, (t0, t1) in enumerate(CH):
                                    ins = A.copy(inpT[0:turn, s, t0:t1, :].rearrange("p t q -> p (t q)"), bank[b][0:turn, 0:(t1 - t0) * P])
                                    if kind == "rel":
                                        ins = A.copy(inp2T[:, s, t0:t1, :].rearrange("p t q -> p (t q)"), bank[2 + b][0:F, 0:(t1 - t0) * P])
                                ins.then_inc(tout[s], 1)
                        if norms:
                            for s in range(2):
                                act.wait_ge(xc_ok[s], i + 1)
                                A.activation(sq[:, s, :, :], xc[:, s, :, :], ACT.Square).then_inc(sq_ok[s], 1)
                            for s in range(2):
                                act.wait_ge(var_ok[s], i + 1)
                                A.activation(st[:, s, 2, :], st[:, s, 1, :], ACT.Sqrt, bias=eps[:, 0:1], scale=1.0 / F).then_inc(sd_ok[s], 1)
                        for s in range(2):
                            act.wait_ge(z_ok[s], i + 1)
                            if not first:
                                act.wait_ge(stored[s], 16 * n_out * i)
                            A.activation(h[:, s, :, :], xc[:, s, :, :], ACT.Copy if final else ACT.Relu).then_inc(h_ok[s], 1)
                    body(0, True)
                    with A.Fori(1, GI) as i:
                        body(i, False)

                @block.vector
                def _(dve):
                    v = nc.vector

                    def body(i, first):
                        tl = [bass.ds(i * BODY + s * HS, HS) for s in range(2)]
                        wide = lambda ap: ap.unsqueeze(2).to_broadcast((P, HS, F))
                        rowb = lambda ap: ap.unsqueeze(1).to_broadcast((P, HS, F))
                        if kind == "sage":
                            for s in range(2):
                                dve.wait_ge(loaded[s], 16 * n_in * (i + 1))
                                v.tensor_tensor(inp2[:, s, :, :], inp2[:, s, :, :], inp[:, s, :, F:2 * F], ALU.add)
                            v.drain()
                            for s in range(2):
                                v.tensor_tensor(inp[:, s, :, F:2 * F], inp2[:, s, :, :], wide(upd_scale[:, tl[s]]), ALU.mult).then_inc(tin[s], 1)
                        po = [bank[4 + s][:, 0:HS * F].rearrange("p (t f) -> p t f", t=HS) for s in range(2)]
                        if kind == "conv":
                            for s in range(2):
                                dve.wait_ge(prod[s], i + 1)
                                v.tensor_tensor(o[:, s, :, :], po[s], wide(norm[:, tl[s]]), ALU.mult).then_inc(o_free[s], 1)
                            v.drain()
                            for s in range(2):
                                v.tensor_tensor(o[:, s, :, :], o[:, s, :, :], rowb(b0[:, :]), ALU.add)
                            v.drain()
                            for s in range(2):
                                v.scalar_tensor_tensor(x_sb[:, tl[s], :], o[:, s, :, :], 0.0, x_sb[:, tl[s], :], ALU.max, ALU.add).then_inc(used[s], 1)
                            v.drain()
                        if kind == "sage":
                            for s in range(2):
                                dve.wait_ge(prod[s], i + 1)
                                v.tensor_tensor(o[:, s, :, :], po[s], rowb(b1[:, :]), ALU.add).then_inc(o_free[s], 1)
                            v.drain()
                            for s in range(2):
                                v.tensor_tensor(x_sb[:, tl[s], :], o[:, s, :, :], x_sb[:, tl[s], :], ALU.add).then_inc(used[s], 1)
                            v.drain()
                        if kind == "rel":
                            for s in range(2):
                                dve.wait_ge(prod[s], i + 1)
                                if not first:
                                    dve.wait_ge(h_ok[s], i)
                                v.tensor_tensor(o[:, s, :, :] if final else xc[:, s, :, :], po[s], rowb(b3[:, layer, :]), ALU.add).then_inc(o_free[s], 1)
                            v.drain()
                            for s in range(2):
                                if final:
                                    v.tensor_tensor(xc[:, s, :, :], o[:, s, :, :], x_sb[:, tl[s], :], ALU.add).then_inc(z_ok[s], 1)
                                else:
                                    v.sem_inc(z_ok[s], 1)
                                v.sem_inc(used[s], 1)
                            return
                        if kind == "bn":
                            for s in range(2):
                                dve.wait_ge(loaded[s], 16 * n_in * (i + 1))
                                v.tensor_tensor(o[:, s, :, :], inp2[:, s, :, :], rowb(mu[:, :]), ALU.subtract).then_inc(used[s], 1)
                            v.drain()
                            for s in range(2):
                                v.tensor_tensor(o[:, s, :, :], o[:, s, :, :], rowb(bn_a[:, :]), ALU.mult)
                            v.drain()
                            for s in range(2):
                                v.tensor_tensor(o[:, s, :, :], o[:, s, :, :], rowb(beta[:, :]), ALU.add)
                            v.drain()
                            for s in range(2):
                                v.scalar_tensor_tensor(x_sb[:, tl[s], :], o[:, s, :, :], 0.0, x_sb[:, tl[s], :], ALU.max, ALU.add)
                            v.drain()
                        for s in range(2):
                            v.tensor_reduce(st[:, s, 0, :], x_sb[:, tl[s], :], AX.X, ALU.add)
                        v.drain()
                        for s in range(2):
                            if not first:
                                dve.wait_ge(h_ok[s], i)
                            v.scalar_tensor_tensor(xc[:, s, :, :], wide(st[:, s, 0, :]), -1.0 / F, x_sb[:, tl[s], :], ALU.mult, ALU.add).then_inc(xc_ok[s], 1)
                        for s in range(2):
                            dve.wait_ge(sq_ok[s], i + 1)
                            v.tensor_reduce(st[:, s, 1, :], sq[:, s, :, :], AX.X, ALU.add).then_inc(var_ok[s], 1)
                        for s in range(2):
                            dve.wait_ge(sd_ok[s], i + 1)
                            v.reciprocal(st[:, s, 3, :], st[:, s, 2, :])
                        v.drain()
                        for s in range(2):
                            v.tensor_tensor(xc[:, s, :, :], xc[:, s, :, :], wide(st[:, s, 3, :]), ALU.mult).then_inc(z_ok[s], 1)
                        if scaled is not None:
                            for s in range(2):
                                dve.wait_ge(h_ok[s], i + 1)
                                if not first:
                                    dve.wait_ge(stored[s], 16 * n_out * i)
                                v.tensor_tensor(g[:, s, :, :], h[:, s, :, :], wide(scaled[:, tl[s]]), ALU.mult).then_inc(g_ok[s], 1)
                    body(0, True)
                    with v.Fori(1, GI) as i:
                        body(i, False)

        def edge_scores(tag):
            with nc.cleanup_on_exit(), ExitStack() as c, nc.Block() as block:
                tb = lambda name, shape, dt=f32: c.enter_context(nc.sbuf_tensor(tag + name, shape, dt))
                sm = lambda name: nc.alloc_semaphore(tag + name)
                two = lambda name: [sm(f"{name}{s}") for s in range(2)]
                cat = tb("cat", [P, 2, HS, 2 * F]); ea = tb("ea", [P, 2, HS, F])
                catT = tb("catT", [P, HS * P]); eaT = tb("eaT", [F, HS * P])
                y = tb("y", [P, 2, 4 * P]); lz = tb("lz", [P, 2, HS * P])
                src_st = tb("src_st", [P, 2, HS], i32); dst_st = tb("dst_st", [P, 2, HS], i32)
                gathered, idx_ok, ea_in, kept = two("gathered"), two("idx_ok"), two("ea_in"), two("kept")
                turned, catT_ok, eaT_ok, z_ok, y_ok, z_read, scored, score_read, go = (
                    sm(n) for n in ("turned", "catT_ok", "eaT_ok", "z_ok", "y_ok", "z_read", "scored", "score_read", "go"))
                PER = 2 * 16 * HS
                CH = [(0, 4), (4, HS)]
                Z = [(0, 0, 4), (0, 1, 5), (1, 0, 6), (1, 1, 4)]

                @block.sync
                def _(sp):
                    def attributes(i, s, first):
                        if not first:
                            sp.wait_ge(turned, 2 * (2 * i + s) - 2)
                        sp.dma_start(ea[:, s, :, :], tiles(attr_all[bass.ds(FRONT + (i * BODY + s * HS) * P, HS * P), :])).then_inc(ea_in[s], 16)

                    def body(i, first):
                        for s in range(2):
                            attributes(i, s, first)
                            sp.wait_ge(gathered[s], PER * (i + 1))
                            sp.dma_start(tiles(edge_h[bass.ds((i * BODY + s * HS) * P, HS * P), :]), cat[:, s, :, 0:F]).then_inc(kept[s], 16)
                    body(0, True)
                    with nc.sync.Fori(1, GI) as i:
                        body(i, False)
                    for s in range(2):
                        sp.wait_ge(kept[s], 16 * GI)

                @block.gpsimd
                def _(pool):
                    def gather(i, s, first):
                        if not first:
                            pool.wait_ge(gathered[s], PER * i)
                            pool.sem_inc(go, 1)
                        nc.gpsimd.tensor_copy(src_st[:, s, :], src_i[:, bass.ds(i * BODY + s * HS, HS)])
                        nc.gpsimd.tensor_copy(dst_st[:, s, :], dst_i[:, bass.ds(i * BODY + s * HS, HS)]).then_inc(idx_ok[s], 1)
                        pool.wait_ge(idx_ok[s], i + 1)
                        if not first:
                            pool.wait_ge(kept[s], 16 * i)
                            pool.wait_ge(turned, 2 * (2 * i + s) - 2)
                        pool.sem_inc(go, 1)
                        for t in range(HS):
                            pool.indirect_dma_start(out=cat[:, s, t, 0:F], out_offset=None, in_=node_g,
                                                    in_offset=bass.IndirectOffsetOnAxis(ap=src_st[:, s, t:t + 1], axis=0)).then_inc(gathered[s], 16)
                            pool.indirect_dma_start(out=cat[:, s, t, F:2 * F], out_offset=None, in_=node_g,
                                                    in_offset=bass.IndirectOffsetOnAxis(ap=dst_st[:, s, t:t + 1], axis=0)).then_inc(gathered[s], 16)
                    for s in range(2):
                        gather(0, s, True)
                    with nc.gpsimd.Fori(1, GI) as i:
                        for s in range(2):
                            gather(i, s, False)

                @block.tensor
                def _(pe):
                    def turn(i, s, first):
                        n = 2 * i + s
                        pe.wait_ge(ea_in[s], 16 * (i + 1))
                        if not first:
                            pe.wait_ge(eaT_ok, n)
                        pe.sem_inc(go, 1)
                        for b, (t0, t1) in enumerate(CH):
                            for t in range(t0, t1):
                                ins = nc.tensor.transpose(bank[2 + b][0:F, (t - t0) * P:(t - t0 + 1) * P], ea[:, s, t, :], ident[:, :])
                        ins.then_inc(turned, 1)
                        pe.wait_ge(gathered[s], PER * (i + 1))
                        if not first:
                            pe.wait_ge(catT_ok, n)
                        pe.sem_inc(go, 1)
                        for b, (t0, t1) in enumerate(CH):
                            for t in range(t0, t1):
                                ins = nc.tensor.transpose(bank[b][:, (t - t0) * P:(t - t0 + 1) * P], cat[:, s, t, :], ident[:, :])
                        ins.then_inc(turned, 1)

                    def inputs(n, first):
                        pe.wait_ge(catT_ok, n + 1)
                        pe.wait_ge(eaT_ok, n + 1)
                        for k, (q, b, to) in enumerate(Z):
                            t0, t1 = CH[b]
                            if k == 3:
                                pe.wait_ge(z_read, 4 * n + 1)
                            elif not first:
                                pe.wait_ge(z_read, 4 * n if k == 0 else 4 * n - 3 + k)
                            out_z = bank[to][:, 0:(t1 - t0) * P]
                            nc.tensor.matmul(out_z, Wlr[:, q * P:(q + 1) * P], catT[:, t0 * P:t1 * P], start=True, stop=False)
                            nc.tensor.matmul(out_z, Wea[:, q * P:(q + 1) * P], eaT[:, t0 * P:t1 * P], start=False, stop=True).then_inc(z_ok, 1)

                    def scores(n, first):
                        pe.wait_ge(z_read, 4 * n + 4)
                        if not first:
                            pe.wait_ge(score_read, n)
                        pe.sem_inc(go, 1)
                        for t in range(HS):
                            for q in range(2):
                                ins = nc.tensor.matmul(bank[7][:, t * HEADS:(t + 1) * HEADS], lz[:, q, t * P:(t + 1) * P], attp[:, q, :], start=(q == 0), stop=(q == 1))
                        ins.then_inc(scored, 1)

                    turn(0, 0, True)
                    inputs(0, True)
                    turn(0, 1, False)
                    scores(0, True)
                    with nc.tensor.Fori(1, GI) as i:
                        inputs(2 * i - 1, False)
                        turn(i, 0, False)
                        scores(2 * i - 1, False)
                        inputs(2 * i, False)
                        turn(i, 1, False)
                        scores(2 * i, False)
                    inputs(NS - 1, False)
                    scores(NS - 1, False)

                @block.scalar
                def _(act):
                    A = nc.scalar

                    def turn(n, first):
                        act.wait_ge(turned, 2 * n + 2)
                        if not first:
                            act.wait_ge(z_ok, 4 * n)
                        for b, (t0, t1) in enumerate(CH):
                            ins = A.copy(catT[:, t0 * P:t1 * P], bank[b][:, 0:(t1 - t0) * P])
                        ins.then_inc(catT_ok, 1)

                    def slopes(n, first):
                        for k, (q, b, to) in enumerate(Z):
                            w = (CH[b][1] - CH[b][0]) * P
                            act.wait_ge(z_ok, 4 * n + k + 1)
                            if k >= 2 or not first:
                                act.wait_ge(z_read, 4 * n + k - 1)
                            A.activation(y[:, k % 2, 0:w], bank[to][:, 0:w], ACT.Identity, bias=b_col[:, 2 + q:3 + q], scale=SLOPE).then_inc(y_ok, 1)

                    turn(0, True)
                    slopes(0, True)
                    with A.Fori(1, NS) as n:
                        turn(n, False)
                        slopes(n, False)

                @block.vector
                def _(dve):
                    v = nc.vector

                    def turn(n, first):
                        dve.wait_ge(turned, 2 * n + 1)
                        if not first:
                            dve.wait_ge(z_ok, 4 * n)
                        for b, (t0, t1) in enumerate(CH):
                            ins = v.tensor_copy(eaT[:, t0 * P:t1 * P], bank[2 + b][0:F, 0:(t1 - t0) * P])
                        ins.then_inc(eaT_ok, 1)

                    def leaky(n, first):
                        if not first:
                            dve.wait_ge(scored, n)
                        for k, (q, b, to) in enumerate(Z):
                            t0, t1 = CH[b]
                            w = (t1 - t0) * P
                            dve.wait_ge(y_ok, 4 * n + k + 1)
                            v.scalar_tensor_tensor(lz[:, q, t0 * P:t1 * P], bank[to][:, 0:w], b_col[:, q:q + 1], y[:, k % 2, 0:w], ALU.add, ALU.max).then_inc(z_read, 1)

                    def keep(n):
                        dve.wait_ge(scored, n + 1)
                        v.tensor_copy(alpha[:, bass.ds(n * HS, HS), :], bank[7][:, 0:HS * HEADS].rearrange("p (t h) -> p t h", h=HEADS)).then_inc(score_read, 1)

                    turn(0, True)
                    leaky(0, True)
                    turn(1, False)
                    keep(0)
                    with v.Fori(1, NS - 1) as n:
                        leaky(n, False)
                        turn(n + 1, False)
                        keep(n)
                    leaky(NS - 1, False)
                    keep(NS - 1)

        def segment_max(tag, windows):
            with nc.cleanup_on_exit(), ExitStack() as c, nc.Block() as block:
                tb = lambda name, shape, dt=f32: c.enter_context(nc.sbuf_tensor(tag + name, shape, dt))
                sm = lambda name: nc.alloc_semaphore(tag + name)
                W = NBLK * P
                key = tb("key", [R, NBLK, P]); pen = tb("pen", [R, 2, NBLK, P]); penf, penb = pen[:, 0], pen[:, 1]
                mf = tb("mf", [R, HEADS, W]); mb = tb("mb", [R, HEADS, W]); m = tb("m", [R, HEADS, NBLK, P])
                ekey = tb("ekey", [HEADS, 2 * T]); e = tb("e", [HEADS, 2 * T]); ef = tb("ef", [HEADS, 2 * T]); eb = tb("eb", [HEADS, 2 * T])
                epf, epb = (mb[0:HEADS, :, :].rearrange("r h w -> r (h w)")[:, k * 2 * T:(k + 1) * 2 * T] for k in range(2))
                back = tb("back", [R, HEADS, NBLK, 2]); off = pen
                nxt = tb("nxt", [R, NBLK, P]) if windows else None
                exps, lasts = mf, mb
                cand = mf[:, 0:2, :].rearrange("r s (b p) -> r s b p", p=P)
                nxt_in, x_ok, lasts_ok, exp_ok, x_out = (sm(n) for n in ("nxt_in", "x_ok", "lasts_ok", "exp_ok", "x_out"))
                key_in, turned, ends_ok, ends_out, e_in, em_ok, em_out, back_in, m_ok, backT = (
                    sm(n) for n in ("key_in", "turned", "ends_ok", "ends_out", "e_in", "em_ok", "em_out", "back_in", "m_ok", "backT"))

                @block.sync
                def _(sp):
                    sp.dma_start(key[:, :, :], dst_rows[0:NP].rearrange("(b r p) -> r b p", r=R, p=P)).then_inc(key_in, 16)
                    sp.wait_ge(key_in, 16)
                    with nc.allow_non_contiguous_dma(reason="two values a tile"):
                        for side in range(2):
                            col = side * (P - 1)
                            sp.dma_start(ends_k[:, side].rearrange("(b r) -> r b", r=R), key[:, :, col]).then_inc(ends_out, 16)
                        sp.wait_ge(ends_ok, 1)
                        for h in range(HEADS):
                            for side in range(2):
                                col = side * (P - 1)
                                sp.dma_start(ends_d[h, :, side].rearrange("(b r) -> r b", r=R), m[:, h, :, col]).then_inc(ends_out, 16)
                        sp.wait_ge(ends_out, 16 * (2 + 2 * HEADS))
                        sp.dma_start(e[:, :], ends_d.rearrange("h t l -> h (t l)")).then_inc(e_in, 16)
                        sp.dma_start(ekey[:, :], ends_k.rearrange("(o t) l -> o (t l)", o=1).to_broadcast((HEADS, 2 * T))).then_inc(e_in, 16)
                        sp.wait_ge(em_ok, 1)
                        sp.dma_start(ends_m.rearrange("h t l -> h (t l)"), e[:, :]).then_inc(em_out, 16)
                        sp.wait_ge(em_out, 16)
                        for h in range(HEADS):
                            sp.dma_start(back[:, h, :, :], ends_m[h].rearrange("(b r) l -> r b l", r=R)).then_inc(back_in, 16)
                    if windows:
                        sp.dma_start(nxt[:, :, :], dst_rows[1:NP + 1].rearrange("(b r p) -> r b p", r=R, p=P)).then_inc(nxt_in, 16)
                        for lo in [0] + [FRONT + NP + k * P for k in range(WT)]:
                            sp.dma_start(exp_all[:, lo:lo + P], zeros_w[0:2 * HEADS, 0:P]).then_inc(x_out, 16)
                        rows_of = lambda c: exp_all[c, FRONT:FRONT + NP].rearrange("(b r p) -> r b p", r=R, p=P)
                        sp.wait_ge(lasts_ok, 1)
                        for h in range(HEADS):
                            sp.dma_start(rows_of(HEADS + h), lasts[:, h, :].rearrange("r (b p) -> r b p", p=P)).then_inc(x_out, 16)
                        sp.wait_ge(exp_ok, 1)
                        for h in range(HEADS):
                            sp.dma_start(rows_of(h), exps[:, h, :].rearrange("r (b p) -> r b p", p=P)).then_inc(x_out, 16)
                        sp.wait_ge(x_out, 16 * (1 + WT + 2 * HEADS))

                if windows:
                    @block.scalar
                    def _(act):
                        act.wait_ge(x_ok, 1)
                        nc.scalar.activation(exps[:, :, :], exps[:, :, :], ACT.Exp).then_inc(exp_ok, 1)

                @block.tensor
                def _(pe):
                    for h in range(HEADS):
                        for b in range(NBLK):
                            ins = nc.tensor.transpose(bank[h][0:R, b * P:(b + 1) * P], alpha[:, b * R:(b + 1) * R, h], ident[:, :])
                    ins.then_inc(turned, 1)
                    if windows:
                        return
                    pe.wait_ge(m_ok, 1)
                    for h in range(HEADS):
                        for b in range(NBLK):
                            ins = nc.tensor.transpose(bank[4 + h][:, b * R:(b + 1) * R], m[:, h, b, :], ident[0:R, 0:R])
                    ins.then_inc(backT, 1)

                @block.vector
                def _(dve):
                    v = nc.vector
                    dve.wait_ge(key_in, 16)
                    v.memset(penf[:, :, 0:1], NEG)
                    v.memset(penb[:, :, P - 1:P], NEG)
                    v.tensor_tensor(penf[:, :, 1:P], key[:, :, 1:P], key[:, :, 0:P - 1], ALU.not_equal)
                    v.tensor_tensor(penb[:, :, 0:P - 1], key[:, :, 0:P - 1], key[:, :, 1:P], ALU.not_equal)
                    v.drain()
                    v.tensor_scalar(penf[:, :, 1:P], penf[:, :, 1:P], NEG, None, ALU.mult)
                    v.tensor_scalar(penb[:, :, 0:P - 1], penb[:, :, 0:P - 1], NEG, None, ALU.mult)
                    dve.wait_ge(turned, 1)
                    v.drain()
                    pf, pb = penf[:, :, :].rearrange("r b p -> r (b p)"), penb[:, :, :].rearrange("r b p -> r (b p)")
                    for h in range(HEADS):
                        v.tensor_tensor_scan(mf[:, h, :], pf, bank[h][0:R, :], NEG, ALU.add, ALU.max)
                        v.tensor_tensor_scan(mb[:, h, W - 1::-1], pb[:, W - 1::-1], bank[h][0:R, W - 1::-1], NEG, ALU.add, ALU.max)
                    v.drain()
                    v.tensor_tensor(m[:, :, :, :].rearrange("r h b p -> r (h b p)"), mf[:, :, :].rearrange("r h w -> r (h w)"),
                                    mb[:, :, :].rearrange("r h w -> r (h w)"), ALU.max).then_inc(ends_ok, 1)
                    for side in range(2):
                        col = side * (P - 1)
                        v.tensor_tensor(off[:, side, :, :], key[:, :, :], key[:, :, col:col + 1].to_broadcast((R, NBLK, P)), ALU.not_equal)
                    dve.wait_ge(e_in, 32)
                    L = 2 * T
                    v.drain()
                    v.memset(epf[:, 0:1], NEG)
                    v.memset(epb[:, L - 1:L], NEG)
                    v.tensor_tensor(epf[:, 1:L], ekey[:, 1:L], ekey[:, 0:L - 1], ALU.not_equal)
                    v.tensor_tensor(epb[:, 0:L - 1], ekey[:, 0:L - 1], ekey[:, 1:L], ALU.not_equal)
                    v.drain()
                    v.tensor_scalar(epf[:, 1:L], epf[:, 1:L], NEG, None, ALU.mult)
                    v.tensor_scalar(epb[:, 0:L - 1], epb[:, 0:L - 1], NEG, None, ALU.mult)
                    v.drain()
                    v.tensor_tensor_scan(ef[:, :], epf[:, :], e[:, :], NEG, ALU.add, ALU.max)
                    v.tensor_tensor_scan(eb[:, L - 1::-1], epb[:, L - 1::-1], e[:, L - 1::-1], NEG, ALU.add, ALU.max)
                    v.drain()
                    v.tensor_tensor(e[:, :], ef[:, :], eb[:, :], ALU.max).then_inc(em_ok, 1)
                    dve.wait_ge(back_in, 16 * HEADS)
                    for h in range(HEADS):
                        for side in range(2):
                            v.drain()
                            v.scalar_tensor_tensor(cand[:, side, :, :], off[:, side, :, :], NEG, back[:, h, :, side:side + 1].to_broadcast((R, NBLK, P)), ALU.mult, ALU.add)
                            v.drain()
                            ins = v.tensor_tensor(m[:, h, :, :], m[:, h, :, :], cand[:, side, :, :], ALU.max)
                    ins.then_inc(m_ok, 1)
                    if windows:
                        dve.wait_ge(nxt_in, 16)
                        v.drain()
                        v.tensor_tensor(nxt[:, :, :], key[:, :, :], nxt[:, :, :], ALU.not_equal)
                        for h in range(HEADS):
                            v.tensor_tensor(exps[:, h, :], bank[h][0:R, :], m[:, h, :, :].rearrange("r b p -> r (b p)"), ALU.subtract)
                        v.drain()
                        v.sem_inc(x_ok, 1)
                        for h in range(HEADS):
                            v.tensor_tensor(lasts[:, h, :].rearrange("r (b p) -> r b p", p=P), m[:, h, :, :], nxt[:, :, :], ALU.mult)
                        v.drain()
                        v.sem_inc(lasts_ok, 1)
                        return
                    dve.wait_ge(backT, 1)
                    for h in range(HEADS):
                        v.tensor_copy(amax[:, :, h], bank[4 + h][:, 0:T])

        def attend(tag):
            with nc.cleanup_on_exit(), ExitStack() as c, nc.Block() as block:
                tb = lambda name, shape, dt=f32: c.enter_context(nc.sbuf_tensor(tag + name, shape, dt))
                sm = lambda name: nc.alloc_semaphore(tag + name)
                two = lambda name: [sm(f"{name}{s}") for s in range(2)]
                cat = tb("cat", [P, 2, HS, 2 * F]); sums = tb("sums", [P, 2, HS, GATW])
                catT = tb("catT", [P, HS, P]); aggT = tb("aggT", [P, HS, 2, P])
                y = tb("y", [P, HS * HF]); z = tb("z", [P, HS * HF])
                own = tb("own", [P, HS, HEADS]); me = tb("me", [P, HS, HEADS]); mm = tb("mm", [P, HS, HEADS])
                d = tb("d", [P, 2, HS, HEADS]); den = tb("den", [P, HS, HEADS]); cc = tb("cc", [P, 2, HS, HEADS])
                o = tb("o", [P, 2, HS, F])
                loaded, scaled, turned, copied, z_ok, y_ok, z_used, d_ok, e_ok, agg_ok, aT, aT_copied, prod, o_ok, stored, stat, used, first_z, stat_end, go = (
                    sm(n) for n in ("loaded", "scaled", "turned", "copied", "z_ok", "y_ok", "z_used", "d_ok", "e_ok", "agg_ok", "aT", "aT_copied", "prod", "o_ok",
                                    "stored", "stat", "used", "first_z", "stat_end", "go"))
                loads, st_s = two("loads"), two("st_s")
                GROUPS = [(0, 2), (2, 4), (4, 6), (6, HS)]
                CH = [(0, 4), (4, HS)]
                AC = [(0, 4), (4, 8), (8, 12), (12, 14)]

                @block.sync
                def _(sp):
                    def body(i, first):
                        for s in range(2):
                            at = bass.ds((i * BODY + s * HS) * P, HS * P)
                            if not first:
                                sp.wait_ge(used, 2 * i + s - 1)
                            sp.dma_start(cat[:, s, :, 0:F], tiles(node_g[at, :])).then_inc(loads[s], 16)
                            sp.dma_start(cat[:, s, :, F:2 * F], tiles(sums_w[at, F:2 * F])).then_inc(loads[s], 16)
                            sp.dma_start(sums[:, s, :, :], tiles(sums_a[at, :])).then_inc(loads[s], 16)
                    body(0, True)
                    with nc.sync.Fori(1, GI) as i:
                        body(i, False)

                @block.gpsimd
                def _(pool):
                    with nc.gpsimd.Fori(0, GI) as i:
                        for s in range(2):
                            pool.wait_ge(o_ok, 2 * i + s + 1)
                            pool.sem_inc(go, 1)
                            pool.dma_start(tiles(gat_out[bass.ds((i * BODY + s * HS) * P, HS * P), :]), o[:, s, :, :]).then_inc(st_s[s], 16)
                    for s in range(2):
                        pool.wait_ge(st_s[s], 16 * GI)

                @block.tensor
                def _(pe):
                    nc.tensor.matmul(bank[7][:, 0:HS * F], zeros_w[:, 0:P], zeros_w[:, 0:HS * F], start=True, stop=False)

                    def body(i, first):
                        for s in range(2):
                            n = 2 * i + s
                            pe.wait_ge(scaled, n + 1)
                            if not (first and s == 0):
                                pe.wait_ge(aT_copied, 4 * n)
                            pe.sem_inc(go, 1)
                            for b, (t0, t1) in enumerate(CH):
                                for t in range(t0, t1):
                                    ins = nc.tensor.transpose(bank[b][:, (t - t0) * P:(t - t0 + 1) * P], cat[:, s, t, :], ident[:, :])
                            ins.then_inc(turned, 1)
                            pe.wait_ge(copied, n + 1)
                            for j, (t0, t1) in enumerate(GROUPS):
                                if not (first and s == 0):
                                    pe.wait_ge(z_used, n)
                                for t in range(t0, t1):
                                    zt = bank[2 + j][:, (t - t0) * HF:(t - t0 + 1) * HF]
                                    nc.tensor.matmul(zt, catT[:, t, :], Wself[:, :], start=True, stop=False)
                                    ins = nc.tensor.matmul(zt, ones1[:, :], b_sum[:, :], start=False, stop=True)
                                ins.then_inc(z_ok, 1)
                            pe.wait_ge(agg_ok, n + 1)
                            for j, (k0, k1) in enumerate(AC):
                                if j >= 2:
                                    pe.wait_ge(aT_copied, 4 * n + j - 1)
                                    pe.sem_inc(go, 1)
                                for k in range(k0, k1):
                                    ins = nc.tensor.transpose(bank[j % 2][:, (k - k0) * P:(k - k0 + 1) * P], sums[:, s, k // 2, (k % 2) * P:(k % 2 + 1) * P], ident[:, :])
                                ins.then_inc(aT, 1)
                            pe.wait_ge(aT_copied, 4 * n + 4)
                            for t in range(HS):
                                for q in range(2):
                                    ins = nc.tensor.matmul(bank[6][:, t * F:(t + 1) * F], aggT[:, t, q, :], Wst[:, q, :], start=(q == 0), stop=(q == 1))
                            ins.then_inc(prod, 1)
                            pe.wait_ge(o_ok, n + 1)
                            nc.tensor.matmul(bank[7][:, 0:HS * F], onesP[:, :], o[:, s, :, :].rearrange("p t f -> p (t f)"), start=False, stop=False).then_inc(stat, 1)
                    body(0, True)
                    with nc.tensor.Fori(1, GI) as i:
                        body(i, False)
                    nc.tensor.matmul(bank[7][:, 0:HS * F], zeros_w[:, 0:P], zeros_w[:, 0:HS * F], start=False, stop=True).then_inc(stat_end, 1)

                @block.scalar
                def _(act):
                    A = nc.scalar

                    def body(i, first):
                        for s in range(2):
                            n = 2 * i + s
                            act.wait_ge(turned, n + 1)
                            for b, (t0, t1) in enumerate(CH):
                                ins = A.copy(catT[:, t0:t1, :].rearrange("p t q -> p (t q)"), bank[b][:, 0:(t1 - t0) * P])
                            ins.then_inc(copied, 1)
                            for j, (t0, t1) in enumerate(GROUPS):
                                act.wait_ge(z_ok, 4 * n + j + 1)
                                if not (first and s == 0):
                                    act.wait_ge(z_used, n)
                                A.mul(y[:, t0 * HF:t1 * HF], bank[2 + j][:, 0:(t1 - t0) * HF], SLOPE).then_inc(y_ok, 1)
                            act.wait_ge(d_ok, n + 1)
                            A.activation(d[:, :, :, :], d[:, :, :, :], ACT.Exp).then_inc(e_ok, 1)
                            for j, (k0, k1) in enumerate(AC):
                                act.wait_ge(aT, 4 * n + j + 1)
                                A.copy(aggT[:, :, :, :].rearrange("p t q c -> p (t q c)")[:, k0 * P:k1 * P], bank[j % 2][:, 0:(k1 - k0) * P]).then_inc(aT_copied, 1)
                    body(0, True)
                    with A.Fori(1, GI) as i:
                        body(i, False)

                @block.vector
                def _(dve):
                    v = nc.vector

                    def body(i, first):
                        for s in range(2):
                            n = 2 * i + s
                            at = bass.ds(i * BODY + s * HS, HS)
                            sm_ = sums[:, s, :, :]
                            heads = lambda ap: ap.unsqueeze(2).to_broadcast((P, HS, HEADS))
                            dve.wait_ge(loads[s], 48 * (i + 1))
                            v.tensor_tensor(cat[:, s, :, F:2 * F], cat[:, s, :, F:2 * F], inv_cnt[:, at].unsqueeze(2).to_broadcast((P, HS, F)), ALU.mult).then_inc(scaled, 1)
                            v.tensor_tensor(me[:, :, :], sm_[:, :, HF + HEADS:GATW], heads(no_edge[:, at]), ALU.add)
                            for j, (t0, t1) in enumerate(GROUPS):
                                dve.wait_ge(y_ok, 4 * n + j + 1)
                                ins = v.tensor_tensor(z[:, t0 * HF:t1 * HF], bank[2 + j][:, 0:(t1 - t0) * HF], y[:, t0 * HF:t1 * HF], ALU.max)
                            ins.then_inc(z_used, 1)
                            v.drain()
                            zz = z[:, :].rearrange("p (t c) -> p t c", t=HS)
                            v.tensor_tensor(zz, zz, attb[:, :].unsqueeze(1).to_broadcast((P, HS, HF)), ALU.mult)
                            v.drain()
                            v.tensor_reduce(own[:, :, :], z[:, :].rearrange("p (t h f) -> p t h f", t=HS, h=HEADS), AX.X, ALU.add)
                            v.drain()
                            v.tensor_tensor(mm[:, :, :], me[:, :, :], own[:, :, :], ALU.max)
                            v.drain()
                            v.tensor_tensor(d[:, 0, :, :], me[:, :, :], mm[:, :, :], ALU.subtract)
                            v.tensor_tensor(d[:, 1, :, :], own[:, :, :], mm[:, :, :], ALU.subtract).then_inc(d_ok, 1)
                            dve.wait_ge(e_ok, n + 1)
                            v.tensor_tensor(den[:, :, :], sm_[:, :, HF:HF + HEADS], d[:, 0, :, :], ALU.mult)
                            v.drain()
                            v.tensor_tensor(den[:, :, :], den[:, :, :], d[:, 1, :, :], ALU.add)
                            v.drain()
                            v.tensor_scalar(den[:, :, :], den[:, :, :], SM_EPS, None, ALU.add)
                            v.drain()
                            v.reciprocal(den[:, :, :], den[:, :, :])
                            v.drain()
                            for q in range(2):
                                v.tensor_tensor(cc[:, q, :, :], d[:, q, :, :], den[:, :, :], ALU.mult)
                            v.drain()
                            num = sm_[:, :, 0:HF].rearrange("p t (h f) -> p t h f", h=HEADS)
                            z4 = z[:, :].rearrange("p (t h f) -> p t h f", t=HS, h=HEADS)
                            for h in range(HEADS):
                                v.tensor_tensor(num[:, :, h, :], num[:, :, h, :], cc[:, 0, :, h:h + 1].to_broadcast((P, HS, F)), ALU.mult)
                                v.tensor_tensor(z4[:, :, h, :], cat[:, s, :, 0:F], cc[:, 1, :, h:h + 1].to_broadcast((P, HS, F)), ALU.mult)
                            v.drain()
                            v.tensor_tensor(sm_[:, :, 0:HF], sm_[:, :, 0:HF], zz, ALU.add).then_inc(agg_ok, 1)
                            dve.wait_ge(prod, n + 1)
                            v.sem_inc(used, 1)
                            if not first:
                                dve.wait_ge(st_s[s], 16 * i)
                                dve.wait_ge(stat, n - 1)
                            v.tensor_scalar(o[:, s, :, :].rearrange("p t f -> p (t f)"), bank[6][:, 0:HS * F], 1.0 / HEADS, None, ALU.mult)
                            v.drain()
                            v.tensor_tensor(o[:, s, :, :], o[:, s, :, :], b2[:, :].unsqueeze(1).to_broadcast((P, HS, F)), ALU.add)
                            v.drain()
                            v.tensor_tensor(o[:, s, :, :], o[:, s, :, :], real[:, at].unsqueeze(2).to_broadcast((P, HS, F)), ALU.mult).then_inc(o_ok, 1)
                    body(0, True)
                    with v.Fori(1, GI) as i:
                        body(i, False)
                    dve.wait_ge(stat_end, 1)
                    v.tensor_reduce(mu[:, :], bank[7][:, 0:HS * F].rearrange("p (t f) -> p f t", t=HS), AX.X, ALU.add)
                    v.drain()
                    v.tensor_scalar(mu[:, :], mu[:, :], 1.0 / N, None, ALU.mult)

        def variance(tag):
            with nc.cleanup_on_exit(), ExitStack() as c, nc.Block() as block:
                tb = lambda name, shape, dt=f32: c.enter_context(nc.sbuf_tensor(tag + name, shape, dt))
                sm = lambda name: nc.alloc_semaphore(tag + name)
                o = tb("o", [P, 2, HS, F]); dev = tb("dev", [P, 2, HS, F]); sq = tb("sq", [P, 2, HS, F]); var = tb("var", [P, 2, F])
                o_in = [sm(f"o_in{s}") for s in range(2)]
                dev_ok, sq_ok, summed, done, v_ok, sd_ok = (sm(n) for n in ("dev_ok", "sq_ok", "summed", "done", "v_ok", "sd_ok"))

                @block.sync
                def _(sp):
                    def body(i, first):
                        for s in range(2):
                            if not first:
                                sp.wait_ge(dev_ok, 2 * i + s - 1)
                            sp.dma_start(o[:, s, :, :], tiles(gat_out[bass.ds((i * BODY + s * HS) * P, HS * P), :])).then_inc(o_in[s], 16)
                    body(0, True)
                    with nc.sync.Fori(1, GI) as i:
                        body(i, False)

                @block.vector
                def _(dve):
                    v = nc.vector

                    def body(i, first):
                        for s in range(2):
                            dve.wait_ge(o_in[s], 16 * (i + 1))
                            if not first:
                                dve.wait_ge(sq_ok, 2 * i + s - 1)
                            v.tensor_tensor(dev[:, s, :, :], o[:, s, :, :], mu[:, :].unsqueeze(1).to_broadcast((P, HS, F)), ALU.subtract)
                            v.drain()
                            v.tensor_tensor(dev[:, s, :, :], dev[:, s, :, :], real[:, bass.ds(i * BODY + s * HS, HS)].unsqueeze(2).to_broadcast((P, HS, F)), ALU.mult).then_inc(dev_ok, 1)
                    body(0, True)
                    with v.Fori(1, GI) as i:
                        body(i, False)
                    dve.wait_ge(done, 1)
                    v.tensor_reduce(var[:, 0, :], bank[7][:, 0:HS * F].rearrange("p (t f) -> p f t", t=HS), AX.X, ALU.add).then_inc(v_ok, 1)
                    dve.wait_ge(sd_ok, 1)
                    v.reciprocal(var[:, 0, :], var[:, 1, :])
                    v.drain()
                    v.tensor_tensor(bn_a[:, :], gamma[:, :], var[:, 0, :], ALU.mult)

                @block.scalar
                def _(act):
                    def body(i, first):
                        for s in range(2):
                            act.wait_ge(dev_ok, 2 * i + s + 1)
                            if not first:
                                act.wait_ge(summed, 2 * i + s - 1)
                            nc.scalar.activation(sq[:, s, :, :], dev[:, s, :, :], ACT.Square).then_inc(sq_ok, 1)
                    body(0, True)
                    with nc.scalar.Fori(1, GI) as i:
                        body(i, False)
                    act.wait_ge(v_ok, 1)
                    nc.scalar.activation(var[:, 1, :], var[:, 0, :], ACT.Sqrt, bias=eps[:, 0:1], scale=1.0 / N).then_inc(sd_ok, 1)

                @block.tensor
                def _(pe):
                    nc.tensor.matmul(bank[7][:, 0:HS * F], zeros_w[:, 0:P], zeros_w[:, 0:HS * F], start=True, stop=False)
                    with nc.tensor.Fori(0, GI) as i:
                        for s in range(2):
                            pe.wait_ge(sq_ok, 2 * i + s + 1)
                            nc.tensor.matmul(bank[7][:, 0:HS * F], onesP[:, :], sq[:, s, :, :].rearrange("p t f -> p (t f)"), start=False, stop=False).then_inc(summed, 1)
                    nc.tensor.matmul(bank[7][:, 0:HS * F], zeros_w[:, 0:P], zeros_w[:, 0:HS * F], start=False, stop=True).then_inc(done, 1)

        def plan():
            with nc.cleanup_on_exit(), ExitStack() as c, nc.Block() as block:
                tb = lambda name, shape, dt=f32: c.enter_context(nc.sbuf_tensor("pl_" + name, shape, dt))
                sm = lambda name: nc.alloc_semaphore("pl_" + name)
                key = tb("key", [R, NBLK * P]); nxt = tb("nxt", [R, NBLK * P]); down = tb("down", [P, 1])
                tot = tb("tot", [P, T]); one = tb("one", [P, T]); cum = tb("cum", [P, T]); first = tb("first", [P, T])
                tile_i = tb("tile_i", [P, 2, T], i32); tile_at = tb("tile_at", [P, 2, T])
                early = tb("early", [P, NS]); late = tb("late", [P, NS]); mx = tb("mx", [P, 4])
                invr = tb("invr", [R, NBLK * P])
                keys_in, iotas, tot_ok, down_ok, down_sum, inv_ok, inv_sb, inv_out = (
                    sm(n) for n in ("keys_in", "iotas", "tot_ok", "down_ok", "down_sum", "inv_ok", "inv_sb", "inv_out"))

                @block.sync
                def _(sp):
                    blk = lambda lo: dst_rows[lo:lo + NP].rearrange("(b r p) -> r b p", r=R, p=P)
                    for to, lo in ((key, 0), (nxt, 1)):
                        sp.dma_start(to[:, :].rearrange("r (b p) -> r b p", p=P), blk(lo)).then_inc(keys_in, 16)
                    sp.wait_ge(inv_sb, 1)
                    sp.dma_start(inv_row.rearrange("(b r p) -> r b p", r=R, p=P), invr[:, :].rearrange("r (b p) -> r b p", p=P)).then_inc(inv_out, 16)
                    sp.wait_ge(inv_out, 16)

                @block.gpsimd
                def _(pool):
                    nc.gpsimd.iota(tile_i[:, 0, :], pattern=[[P, T]], base=0, channel_multiplier=0)
                    nc.gpsimd.iota(tile_i[:, 1, :].rearrange("p (n t) -> p n t", t=HS), pattern=[[0, NS], [P, HS]], base=0, channel_multiplier=0).then_inc(iotas, 1)

                @block.tensor
                def _(pe):
                    nc.tensor.matmul(bank[0][:, 0:T], onesP[:, :], cnt[:, :], start=True, stop=True).then_inc(tot_ok, 1)
                    for b in range(NBLK):
                        ins = nc.tensor.transpose(bank[4][0:R, b * P:(b + 1) * P], inv_cnt[:, b * R:(b + 1) * R], ident[:, :])
                    ins.then_inc(inv_ok, 1)
                    pe.wait_ge(down_ok, 1)
                    nc.tensor.matmul(bank[1][:, 0:1], onesP[0:R, :], down[0:R, :], start=True, stop=True).then_inc(down_sum, 1)

                @block.vector
                def _(dve):
                    v = nc.vector
                    slots = lambda ap: ap.rearrange("p (n t) -> p n t", t=HS)
                    v.memset(one[:, :], 1.0)
                    dve.wait_ge(keys_in, 32)
                    v.tensor_tensor(nxt[:, :], key[:, :], nxt[:, :], ALU.is_gt)
                    dve.wait_ge(iotas, 1)
                    v.tensor_copy(tile_at[:, :, :], tile_i[:, :, :])
                    v.drain()
                    v.tensor_reduce(down[0:R, :], nxt[:, :], AX.X, ALU.add).then_inc(down_ok, 1)
                    dve.wait_ge(tot_ok, 1)
                    v.tensor_copy(tot[:, :], bank[0][:, 0:T])
                    v.drain()
                    v.tensor_tensor_scan(cum[:, :], one[:, :], tot[:, :], 0.0, ALU.mult, ALU.add)
                    v.drain()
                    v.tensor_tensor(first[:, :], cum[:, :], tot[:, :], ALU.subtract)
                    v.drain()
                    begin = slots(first[:, :])[:, :, 0]
                    beginb = begin.unsqueeze(2).to_broadcast((P, NS, HS))
                    v.tensor_tensor(slots(tot[:, :]), slots(first[:, :]), beginb, ALU.subtract)
                    v.tensor_tensor(slots(cum[:, :]), slots(cum[:, :]), beginb, ALU.subtract)
                    v.drain()
                    v.tensor_tensor(tot[:, :], tot[:, :], tile_at[:, 1, :], ALU.subtract)
                    v.tensor_tensor(cum[:, :], cum[:, :], tile_at[:, 1, :], ALU.subtract)
                    v.drain()
                    v.tensor_scalar(tot[:, :], tot[:, :], -1.0, None, ALU.mult)
                    v.drain()
                    v.tensor_reduce(early[:, :], slots(tot[:, :]), AX.X, ALU.max)
                    v.tensor_reduce(late[:, :], slots(cum[:, :]), AX.X, ALU.max)
                    v.drain()
                    v.tensor_tensor(late[:, :], late[:, :], early[:, :], ALU.add)
                    v.tensor_tensor(tot[:, 0:NS], begin, early[:, :], ALU.subtract)
                    v.drain()
                    v.tensor_scalar(starts[:, :], tot[0:1, 0:NS], float(FRONT), 0.0, ALU.add, ALU.max)
                    v.tensor_scalar(late[:, :], late[:, :], float(BAND * P), None, ALU.is_gt)
                    v.tensor_scalar(early[:, :], early[:, :], float(FRONT), None, ALU.is_gt)
                    v.drain()
                    for j, cond in enumerate((early, late)):
                        v.tensor_reduce(mx[:, j:j + 1], cond[:, 0:NS], AX.X, ALU.add)
                    dve.wait_ge(down_sum, 1)
                    v.tensor_copy(mx[:, 2:3], bank[1][:, 0:1])
                    v.drain()
                    v.tensor_reduce(down[:, :], mx[:, 0:3], AX.X, ALU.add)
                    v.drain()
                    v.tensor_scalar(fast[:, :], down[0:1, :], 0.0, None, ALU.is_equal)
                    dve.wait_ge(inv_ok, 1)
                    v.tensor_copy(invr[:, :], bank[4][0:R, 0:NBLK * P]).then_inc(inv_sb, 1)

        def window_numbers():
            with nc.cleanup_on_exit(), ExitStack() as c, nc.Block() as block:
                tb = lambda name, shape, dt=f32: c.enter_context(nc.sbuf_tensor("wn_" + name, shape, dt))
                sm = lambda name: nc.alloc_semaphore("wn_" + name)
                GS = min(14, NS)
                NG = NS // GS
                tile_i = tb("tile_i", [P, T], i32); tile_at = tb("tile_at", [P, T])
                winr = tb("winr", [GS * WT, 3, NG, P]); winT = tb("winT", [P, NS, WT])
                iotas, wins_in, winT_ok = sm("iotas"), sm("wins_in"), sm("winT_ok")

                @block.sync
                def _(sp):
                    for j, of in enumerate((dst_win, type_win, src_win)):
                        sp.dma_start(winr[:, j, :, :], of.rearrange("(g n p) -> n g p", g=NG, p=P)).then_inc(wins_in, 16)

                @block.gpsimd
                def _(pool):
                    nc.gpsimd.iota(tile_i[:, :], pattern=[[P, T]], base=0, channel_multiplier=0).then_inc(iotas, 1)

                @block.tensor
                def _(pe):
                    pe.wait_ge(wins_in, 48)
                    for j in range(3):
                        for g in range(NG):
                            ins = nc.tensor.transpose(bank[2 + j][:, g * GS * WT:(g + 1) * GS * WT], winr[:, j, g, :], ident[0:GS * WT, 0:GS * WT])
                    ins.then_inc(winT_ok, 1)

                @block.vector
                def _(dve):
                    v = nc.vector
                    dve.wait_ge(iotas, 1)
                    v.tensor_copy(tile_at[:, :], tile_i[:, :])
                    dve.wait_ge(winT_ok, 1)
                    v.tensor_copy(winT[:, :, :].rearrange("p n q -> p (n q)"), bank[2][:, 0:NS * WT])
                    v.tensor_scalar(rel_w[:, 0, :], bank[3][:, 0:NS * WT], 0.0, None, ALU.is_equal)
                    v.tensor_scalar(rel_w[:, 1, :], bank[3][:, 0:NS * WT], 0.0, None, ALU.not_equal)
                    v.tensor_copy(src_w[:, :], bank[4][:, 0:NS * WT])
                    v.drain()
                    ids = edge_id[:, 0:NS * HS * BAND].rearrange("p (n t q) -> p n t q", t=HS, q=BAND)
                    at = tile_at[:, :].rearrange("p (n t) -> p n t", t=HS)
                    for q in range(BAND):
                        v.tensor_tensor(ids[:, :, :, q], winT[:, :, q:q + HS], at, ALU.subtract)

        def clear_sums():
            with nc.cleanup_on_exit(), ExitStack() as c, nc.Block() as block:
                zero = c.enter_context(nc.sbuf_tensor("cl_zero", [P, 28 * F], f32))
                ready, zeroed = nc.alloc_semaphore("cl_ready"), nc.alloc_semaphore("cl_zeroed")

                @block.vector
                def _(dve):
                    nc.vector.memset(zero[:, :], 0.0).then_inc(ready, 1)

                @block.sync
                def _(sp):
                    sp.wait_ge(ready, 1)
                    wide = sums_w.rearrange("(g p r) f -> g p (r f)", p=P, r=14)
                    narrow = sums_n.rearrange("(g p r) f -> g p (r f)", p=P, r=28)
                    for g in range(wide.shape[0]):
                        sp.dma_start(wide[g], zero[:, 0:14 * 2 * F]).then_inc(zeroed, 16)
                    for g in range(narrow.shape[0]):
                        sp.dma_start(narrow[g], zero[:, 0:28 * F]).then_inc(zeroed, 16)
                    sp.wait_ge(zeroed, 16 * (wide.shape[0] + narrow.shape[0]))

        def normalise(dve, j, s, tl, xn, bs, ln, var_ok, sd_ok, ln_ok, conv, meanwhile=None):
            v = nc.vector
            """The layer norm's scale and shift of each row, from halves' means and squares."""
            L = lambda r: ln[:, s, r, :]
            for t in range(HS):
                v.bn_stats(bs[:, s, t, :], xn[:, s, t, :])
            v.drain()
            v.tensor_tensor(L(0), bs[:, s, :, 1], bs[:, s, :, 4], ALU.add)
            v.tensor_tensor(L(1), bs[:, s, :, 1], bs[:, s, :, 4], ALU.subtract)
            v.tensor_tensor(L(2), bs[:, s, :, 2], bs[:, s, :, 5], ALU.add)
            v.drain()
            v.tensor_tensor(L(1), L(1), L(1), ALU.mult)
            v.drain()
            v.scalar_tensor_tensor(L(3), L(1), F / 4.0, L(2), ALU.mult, ALU.add).then_inc(var_ok[s], 1)
            if meanwhile is not None:
                meanwhile()
            dve.wait_ge(sd_ok[s], j + 1)
            v.reciprocal(L(5), L(4))
            v.drain()
            ins = v.scalar_tensor_tensor(L(6), L(0), -0.5, L(5), ALU.mult, ALU.mult)
            if conv:
                v.drain()
                v.tensor_tensor(L(0), L(5), rs_send[:, tl], ALU.mult)
                ins = v.tensor_tensor(L(1), L(6), rs_send[:, tl], ALU.mult)
            ins.then_inc(ln_ok[s], 1)

        def first_norm(tag):
            with nc.cleanup_on_exit(), ExitStack() as c, nc.Block() as block:
                tb = lambda name, shape, dt=f32: c.enter_context(nc.sbuf_tensor(tag + name, shape, dt))
                two = lambda name: [nc.alloc_semaphore(f"{tag}{name}{s}") for s in range(2)]
                g = tb("g", [P, 2, HS, F]); bs = tb("bs", [P, 2, HS, 6]); ln = tb("ln", [P, 2, 8, HS])
                var_ok, sd_ok, ln_ok, g_ok, stored, go = two("var_ok"), two("sd_ok"), two("ln_ok"), two("g_ok"), two("stored"), nc.alloc_semaphore(tag + "go")

                copied, copied2 = nc.alloc_semaphore(tag + "copied"), nc.alloc_semaphore(tag + "copied2")
                window = lambda ap, at: ap[bass.ds(at, WR)].rearrange("(q p) -> q p", p=P)

                @block.gpsimd
                def _(pool):
                    with nc.gpsimd.Fori(0, NS) as n:
                        begin = nc.gpsimd.value_load(starts[0:1, bass.ds(n, 1)], min_val=0, max_val=FRONT + NP)
                        pool.dma_start(window(type_win, n * WR), window(type_all, begin)).then_inc(copied2, 16)
                    pool.wait_ge(copied2, 16 * NS)

                @block.sync
                def _(sp):
                    with nc.sync.Fori(0, NS) as n:
                        begin = nc.sync.value_load(starts[0:1, bass.ds(n, 1)], min_val=0, max_val=FRONT + NP)
                        for to, of in ((dst_win, dst_all), (src_win, src_all)):
                            sp.dma_start(window(to, n * WR), window(of, begin)).then_inc(copied, 16)
                    sp.wait_ge(copied, 32 * NS)

                @block.scalar
                def _(act):
                    A = nc.scalar

                    def root(j, s):
                        act.wait_ge(var_ok[s], j + 1)
                        A.activation(ln[:, s, 4, :], ln[:, s, 3, :], ACT.Sqrt, bias=eps[:, 0:1], scale=1.0 / F).then_inc(sd_ok[s], 1)

                    def rows(j, s, first):
                        act.wait_ge(ln_ok[s], j + 1)
                        if not first:
                            act.wait_ge(stored[s], 16 * j)
                            A.sem_inc(go, 1)
                        for t in range(HS):
                            ins = A.activation(g[:, s, t, :], x_sb[:, bass.ds(j * BODY + s * HS + t, 1), :].rearrange("p o f -> p (o f)"),
                                               ACT.Relu, bias=ln[:, s, 1, t:t + 1], scale=ln[:, s, 0, t:t + 1])
                        ins.then_inc(g_ok[s], 1)
                        act.wait_ge(g_ok[s], j + 1)
                        A.sem_inc(go, 1)
                        act.dma_start(tiles(node_g[bass.ds((j * BODY + s * HS) * P, HS * P), :]), g[:, s, :, :]).then_inc(stored[s], 16)

                    def body(j, first, last):
                        root(j, 1)
                        rows(j, 0, first)
                        if not last:
                            root(j + 1, 0)
                        rows(j, 1, first)
                    root(0, 0)
                    body(0, True, False)
                    with A.Fori(1, GI - 1) as j:
                        body(j, False, False)
                    body(GI - 1, False, True)
                    for s in range(2):
                        act.wait_ge(stored[s], 16 * GI)

                @block.vector
                def _(dve):
                    v = nc.vector
                    L = lambda s, r: ln[:, s, r, :]

                    def variances(j, s):
                        for t in range(HS):
                            v.bn_stats(bs[:, s, t, :], x_sb[:, bass.ds(j * BODY + s * HS + t, 1), :].rearrange("p o f -> p (o f)"))
                        v.drain()
                        v.tensor_tensor(L(s, 7), bs[:, s, :, 1], bs[:, s, :, 4], ALU.add)
                        v.tensor_tensor(L(s, 2), bs[:, s, :, 1], bs[:, s, :, 4], ALU.subtract)
                        v.tensor_tensor(L(s, 3), bs[:, s, :, 2], bs[:, s, :, 5], ALU.add)
                        v.drain()
                        v.tensor_tensor(L(s, 2), L(s, 2), L(s, 2), ALU.mult)
                        v.drain()
                        v.scalar_tensor_tensor(L(s, 3), L(s, 2), F / 4.0, L(s, 3), ALU.mult, ALU.add).then_inc(var_ok[s], 1)

                    def scales(j, s, first):
                        tl = bass.ds(j * BODY + s * HS, HS)
                        dve.wait_ge(sd_ok[s], j + 1)
                        v.reciprocal(L(s, 5), L(s, 4))
                        v.drain()
                        if not first:
                            dve.wait_ge(g_ok[s], j)
                            v.sem_inc(go, 1)
                        v.tensor_tensor(L(s, 0), L(s, 5), norm[:, tl], ALU.mult)
                        v.drain()
                        v.scalar_tensor_tensor(L(s, 1), L(s, 7), -0.5, L(s, 0), ALU.mult, ALU.mult).then_inc(ln_ok[s], 1)

                    def body(j, first, last):
                        variances(j, 1)
                        scales(j, 0, first)
                        if not last:
                            variances(j + 1, 0)
                        scales(j, 1, first)
                    variances(0, 0)
                    body(0, True, False)
                    with v.Fori(1, GI - 1) as j:
                        body(j, False, False)
                    body(GI - 1, False, True)

        def layer(tag, kind, table_in, table_out, k=0):
            with nc.cleanup_on_exit(), ExitStack() as c, nc.Block() as block:
                tb = lambda name, shape, dt=f32: c.enter_context(nc.sbuf_tensor(tag + name, shape, dt))
                sm = lambda name: nc.alloc_semaphore(tag + name)
                two = lambda name: [sm(f"{name}{s}") for s in range(2)]
                typed, conv, sage = kind == "typed", kind == "conv", kind == "sage"
                final = typed and k == 2
                norms = not typed
                M = F if sage else 2 * F
                src_st = tb("src_st", [P, 2, WT], i32)
                win = tb("win", [P, 2, WT, F]) if typed else None
                msg = tb("msg", [P, 2, WT, M])
                S = tb("S", [P, 2, BAND * HS, P])
                own = None if conv else tb("own", [P, 2, HS, 2 * F if sage else F])
                inv_r = tb("inv_r", [P, 2, HS * P]) if conv else None
                aT = tb("aT", [P, 2, HS * P])
                loopT = aT
                hT = tb("hT", [F, 2, HS * P]) if typed else None
                o = tb("o", [P, 2, HS, F])
                xn = lent(alpha, 2 * HS * F, lambda shape: tb("xn", shape)); h = lent(amax, 2 * HS * F, lambda shape: tb("h", shape))
                g = tb("g", [P, 2, HS, F]) if conv else None
                bs = tb("bs", [P, 2, HS, 6]); ln = tb("ln", [P, 2, 8, HS])
                gathered, src_ok, win_in, S_ok, msg_ok = two("gathered"), two("src_ok"), two("win_in"), two("S_ok"), two("msg_ok")
                agg_ok, aT_ok, loop_ok, loop_out, prod, o_free = two("agg_ok"), two("aT_ok"), two("loop_ok"), two("loop_out"), two("prod"), two("o_free")
                x_ok, x_kept, var_ok, sd_ok, ln_ok, h_ok, stored, go = two("x_ok"), two("x_kept"), two("var_ok"), two("sd_ok"), two("ln_ok"), two("h_ok"), two("stored"), sm("go")
                n_win = {"conv": 2, "sage": 2, "typed": 1}[kind]
                n_out = 2 if conv else 1
                PER = 16 * WT
                CH = [(0, 4), (4, HS)]

                @block.gpsimd
                def _(pool):
                    def gather(i, s, first):
                        if not first:
                            pool.wait_ge(gathered[s], PER * i)
                            pool.sem_inc(go, 1)
                        nc.gpsimd.tensor_copy(src_st[:, s, :], src_w[:, bass.ds((2 * i + s) * WT, WT)]).then_inc(src_ok[s], 1)
                        pool.wait_ge(src_ok[s], i + 1)
                        if not first:
                            pool.wait_ge(msg_ok[s] if typed else agg_ok[s], i)
                        pool.sem_inc(go, 1)
                        for q in range(WT):
                            to = win[:, s, q, :] if typed else msg[:, s, q, 0:F]
                            pool.indirect_dma_start(out=to, out_offset=None, in_=table_in,
                                                    in_offset=bass.IndirectOffsetOnAxis(ap=src_st[:, s, q:q + 1], axis=0)).then_inc(gathered[s], 16)
                    for s in range(2):
                        gather(0, s, True)
                    with nc.gpsimd.Fori(1, GI) as i:
                        for s in range(2):
                            gather(i, s, False)

                @block.sync
                def _(sp):
                    def windows(j, s, first):
                        n = 2 * j + s
                        if conv:
                            begin = nc.sync.value_load(starts[0:1, bass.ds(n, 1)], min_val=0, max_val=FRONT + NP)
                        at = bass.ds((j * BODY + s * HS) * P, HS * P)
                        if not first:
                            sp.wait_ge(agg_ok[s], j)
                            if conv:
                                sp.wait_ge(loop_ok[s], j)
                        if conv:
                            sp.dma_start(msg[:, s, :, F:2 * F], tiles(attr_all[bass.ds(begin, WR), :])).then_inc(win_in[s], 16)
                            sp.dma_start(inv_r[F:2 * F, s, :], inv_row[at].rearrange("(o n) -> o n", o=1).to_broadcast((F, HS * P))).then_inc(win_in[s], 16)
                        if typed:
                            sp.dma_start(own[:, s, :, :], tiles(table_in[at, :])).then_inc(win_in[s], 16)
                        if sage:
                            sp.dma_start(own[:, s, :, 0:F], tiles(table_in[at, :])).then_inc(win_in[s], 16)
                            sp.dma_start(own[:, s, :, F:2 * F], tiles(node_h[at, :])).then_inc(win_in[s], 16)

                    for s in range(2):
                        windows(0, s, True)
                    with nc.sync.Fori(1, GI) as j:
                        for s in range(2):
                            windows(j, s, False)

                @block.tensor
                def _(pe):
                    def sums(j, s, first):
                        pe.wait_ge(S_ok[s], j + 1)
                        pe.wait_ge(msg_ok[s] if typed else gathered[s], j + 1 if typed else PER * (j + 1))
                        pe.wait_ge(win_in[s], 16 * n_win * (j + 1))
                        if not first:
                            pe.wait_ge(aT_ok[s], j)
                            if conv:
                                pe.wait_ge(loop_ok[s], j)
                        if typed and not (first and s == 0):
                            pe.wait_ge(aT_ok[1 - s], j + s)
                        pe.sem_inc(go, 1)
                        for b, (t0, t1) in enumerate(CH):
                            for t in range(t0, t1):
                                col = slice((t - t0) * P, (t - t0 + 1) * P)
                                to = bank[2 * s + b][0:M, col]
                                qs = range(BAND)
                                if sage:
                                    nc.tensor.matmul(bank[2 * s + b][F:2 * F, col], own[:, s, t, F:2 * F], ident[:, :], start=True, stop=True)
                                    nc.tensor.matmul(to, own[:, s, t, 0:F], ident[:, :], start=True, stop=False)
                                for q in qs:
                                    ins = nc.tensor.matmul(to, msg[:, s, t + q, :], S[:, s, BAND * t + q, :], start=(q == 0 and not sage), stop=(q == BAND - 1))
                                if typed:
                                    ins = nc.tensor.transpose(bank[4 + b][0:F, col], own[:, s, t, :], ident[:, :])
                        ins.then_inc(agg_ok[s], 1)

                    def products(j, s, first):
                        pe.wait_ge(aT_ok[s], j + 1)
                        if not first:
                            pe.wait_ge(o_free[s], j)
                        pe.sem_inc(go, 1)
                        for t in range(HS):
                            po = bank[6 + s][:, t * F:(t + 1) * F]
                            a_t = lambda lo, hi: aT[lo:hi, s, t * P:(t + 1) * P]
                            if conv:
                                ins = nc.tensor.matmul(po, a_t(0, F), W0[:, :], start=True, stop=True)
                            if sage:
                                nc.tensor.matmul(po, a_t(F, 2 * F), W1s[F:2 * F, :], start=True, stop=True)
                                ins = nc.tensor.matmul(bank[4 + s][:, t * F:(t + 1) * F], a_t(0, F), W1s[0:F, :], start=True, stop=True)
                            if typed:
                                nc.tensor.matmul(po, a_t(0, 2 * F), W3[:, k, :], start=True, stop=False)
                                ins = nc.tensor.matmul(po, hT[:, s, t * P:(t + 1) * P], Ws3[:, k, :], start=False, stop=True)
                        ins.then_inc(prod[s], 1)

                    sums(0, 0, True)

                    def body(j, first, last):
                        sums(j, 1, first)
                        products(j, 0, first)
                        if not last:
                            sums(j + 1, 0, False)
                        products(j, 1, first)
                    body(0, True, False)
                    with nc.tensor.Fori(1, GI - 1) as j:
                        body(j, False, False)
                    body(GI - 1, False, True)

                @block.scalar
                def _(act):
                    A = nc.scalar

                    def evacuate(j, s, first):
                        act.wait_ge(agg_ok[s], j + 1)
                        if not first:
                            act.wait_ge(prod[s], j)
                        rows = F if conv else 2 * F
                        for b, (t0, t1) in enumerate(CH):
                            ins = A.copy(aT[0:rows, s, t0 * P:t1 * P], bank[2 * s + b][0:rows, 0:(t1 - t0) * P])
                            if typed:
                                ins = A.copy(hT[:, s, t0 * P:t1 * P], bank[4 + b][0:F, 0:(t1 - t0) * P])
                        ins.then_inc(aT_ok[s], 1)

                    def rows_out(j, s, first):
                        n = 2 * j + s
                        at = bass.ds((j * BODY + s * HS) * P, HS * P)
                        if norms:
                            act.wait_ge(x_ok[s], j + 1)
                            A.copy(x_sb[:, bass.ds(j * BODY + s * HS, HS), :], xn[:, s, :, :]).then_inc(x_kept[s], 1)
                            act.wait_ge(var_ok[s], j + 1)
                            A.activation(ln[:, s, 4, :], ln[:, s, 3, :], ACT.Sqrt, bias=eps[:, 0:1], scale=1.0 / F).then_inc(sd_ok[s], 1)
                        act.wait_ge(o_free[s] if typed and not final else ln_ok[s], j + 1)
                        if not first:
                            act.wait_ge(stored[s], 16 * n_out * j)
                            A.sem_inc(go, 1)
                        if norms:
                            for t in range(HS):
                                ins = A.activation(h[:, s, t, :], xn[:, s, t, :], ACT.Relu, bias=ln[:, s, 6, t:t + 1], scale=ln[:, s, 5, t:t + 1])
                                if conv:
                                    ins = A.activation(g[:, s, t, :], xn[:, s, t, :], ACT.Relu, bias=ln[:, s, 1, t:t + 1], scale=ln[:, s, 0, t:t + 1])
                        elif final:
                            ins = A.copy(h[:, s, :, :], o[:, s, :, :])
                        else:
                            ins = A.activation(h[:, s, :, :], o[:, s, :, :], ACT.Relu)
                        ins.then_inc(h_ok[s], 1)
                        act.wait_ge(h_ok[s], j + 1)
                        if not final:
                            if conv:
                                act.dma_start(tiles(node_h[at, :]), h[:, s, :, :]).then_inc(stored[s], 16)
                                act.dma_start(tiles(table_out[at, :]), g[:, s, :, :]).then_inc(stored[s], 16)
                            else:
                                act.dma_start(tiles(table_out[at, :]), h[:, s, :, :]).then_inc(stored[s], 16)
                        elif isinstance(j, int) and j == GI - 1 and j * BODY + s * HS + HS > FULL:
                            to = FULL - (j * BODY + s * HS)
                            if to > 0:
                                act.dma_start(tiles(out[(FULL - to) * P:FULL * P, :]), h[:, s, 0:to, :]).then_inc(stored[s], 16)
                            if REM:
                                act.dma_start(out[FULL * P:N, :], h[0:REM, s, to, :]).then_inc(stored[s], 16)
                        else:
                            act.dma_start(tiles(out[at, :]), h[:, s, :, :]).then_inc(stored[s], 16)
                        if conv:
                            act.wait_ge(loop_ok[s], j + 1)
                            act.dma_start(loop_rows[:, at], loopT[F:2 * F, s, :]).then_inc(loop_out[s], 16)

                    evacuate(0, 0, True)

                    def body(j, first, last):
                        evacuate(j, 1, first)
                        rows_out(j, 0, first)
                        if not last:
                            evacuate(j + 1, 0, False)
                        rows_out(j, 1, first)
                    body(0, True, False)
                    with A.Fori(1, GI - 1) as j:
                        body(j, False, False)
                    body(GI - 1, False, True)
                    for s in range(2):
                        n = FULL - ((GI - 1) * BODY + s * HS)
                        last = 1 if n >= HS else (1 if n > 0 else 0) + (1 if REM else 0)
                        act.wait_ge(stored[s], 16 * (GI - 1 + last) if final else 16 * n_out * GI)
                        if conv:
                            act.wait_ge(loop_out[s], 16 * GI)

                @block.vector
                def _(dve):
                    v = nc.vector
                    def matrices(j, s, first):
                        n = 2 * j + s
                        if not first:
                            dve.wait_ge(agg_ok[s], j)
                        v.tensor_tensor(S[:, s, :, :], node_id[:, :].unsqueeze(1).to_broadcast((P, BAND * HS, P)),
                                        edge_id[:, bass.ds(n * BAND * HS, BAND * HS)].unsqueeze(2).to_broadcast((P, BAND * HS, P)), ALU.is_equal).then_inc(S_ok[s], 1)
                        if typed:
                            dve.wait_ge(gathered[s], PER * (j + 1))
                            for r in range(2):
                                ins = v.tensor_tensor(msg[:, s, :, r * F:(r + 1) * F], win[:, s, :, :],
                                                      rel_w[:, r, bass.ds(n * WT, WT)].unsqueeze(2).to_broadcast((P, WT, F)), ALU.mult)
                            ins.then_inc(msg_ok[s], 1)

                    def update(j, s, first):
                        tl = bass.ds(j * BODY + s * HS, HS)
                        wide = lambda ap: ap.unsqueeze(2).to_broadcast((P, HS, F))
                        rowb = lambda ap: ap.unsqueeze(1).to_broadcast((P, HS, F))
                        po = bank[6 + s][:, 0:HS * F].rearrange("p (t f) -> p t f", t=HS)
                        if conv:
                            dve.wait_ge(agg_ok[s], j + 1)
                            if not first:
                                dve.wait_ge(loop_out[s], 16 * j)
                            for b, (t0, t1) in enumerate(CH):
                                ins = v.tensor_tensor(loopT[F:2 * F, s, t0 * P:t1 * P], bank[2 * s + b][F:2 * F, 0:(t1 - t0) * P],
                                                      inv_r[F:2 * F, s, t0 * P:t1 * P], ALU.mult)
                            ins.then_inc(loop_ok[s], 1)
                        dve.wait_ge(prod[s], j + 1)
                        if not first and norms:
                            dve.wait_ge(x_kept[s], j)
                            dve.wait_ge(h_ok[s], j)
                        if not first and typed:
                            dve.wait_ge(h_ok[s], j)
                        if typed:
                            if final:
                                v.tensor_tensor(xn[:, s, :, :], po, rowb(b3[:, k, :]), ALU.add).then_inc(o_free[s], 1)
                                v.drain()
                                v.tensor_tensor(o[:, s, :, :], xn[:, s, :, :], x_sb[:, tl, :], ALU.add).then_inc(ln_ok[s], 1)
                            else:
                                v.tensor_tensor(o[:, s, :, :], po, rowb(b3[:, k, :]), ALU.add).then_inc(o_free[s], 1)
                            return
                        if conv:
                            v.tensor_tensor(o[:, s, :, :], po, wide(norm[:, tl]), ALU.mult).then_inc(o_free[s], 1)
                            v.drain()
                            v.tensor_tensor(o[:, s, :, :], o[:, s, :, :], rowb(b0[:, :]), ALU.add)
                            v.drain()
                            v.scalar_tensor_tensor(xn[:, s, :, :], o[:, s, :, :], 0.0, x_sb[:, tl, :], ALU.max, ALU.add).then_inc(x_ok[s], 1)
                        if sage:
                            pu = bank[4 + s][:, 0:HS * F].rearrange("p (t f) -> p t f", t=HS)
                            v.tensor_tensor(o[:, s, :, :], pu, wide(upd_scale[:, tl]), ALU.mult)
                            v.drain()
                            v.tensor_tensor(o[:, s, :, :], o[:, s, :, :], po, ALU.add).then_inc(o_free[s], 1)
                            v.drain()
                            v.tensor_tensor(o[:, s, :, :], o[:, s, :, :], rowb(b1[:, :]), ALU.add)
                            v.drain()
                            v.tensor_tensor(xn[:, s, :, :], o[:, s, :, :], x_sb[:, tl, :], ALU.add).then_inc(x_ok[s], 1)
                        v.drain()
                        normalise(dve, j, s, tl, xn, bs, ln, var_ok, sd_ok, ln_ok, conv)

                    for s in range(2):
                        matrices(0, s, True)

                    def body(j, first, last):
                        for s in range(2):
                            if not last:
                                matrices(j + 1, s, False)
                            update(j, s, first)
                    body(0, True, False)
                    with v.Fori(1, GI - 1) as j:
                        body(j, False, False)
                    body(GI - 1, False, True)

        def attention_weights():
            with nc.cleanup_on_exit(), ExitStack() as c, nc.Block() as block:
                tb = lambda name, shape, dt=f32: c.enter_context(nc.sbuf_tensor("aw_" + name, shape, dt))
                brb = tb("brb", [P, HF]); part = tb("part", [P, 2, HF]); halves = tb("halves", [P, 2, 2]); blc = tb("blc", [F, HEADS + 1])
                zeroed, loaded = nc.alloc_semaphore("aw_zeroed"), nc.alloc_semaphore("aw_loaded")
                n_loads = 11

                @block.sync
                def _(sp):
                    sp.wait_ge(zeroed, 1)
                    column = lambda v: v.rearrange("(f o) -> f o", o=1)
                    with nc.allow_non_contiguous_dma(reason="a few columns of weights"):
                        for h in range(HEADS):
                            sp.dma_start(attp[(h % 2) * F:(h % 2 + 1) * F, h // 2, h:h + 1], column(a["L2_gnn_att"][h])).then_inc(loaded, 16)
                        for j, name in enumerate(("L2_gnn_b_l", "L2_gnn_b_r")):
                            sp.dma_start(halves[:, j, :], a[name].rearrange("(q p) -> p q", p=P)).then_inc(loaded, 16)
                        sp.dma_start(blc[:, 0:HEADS], a["L2_gnn_b_l"].rearrange("(h f) -> f h", f=F)).then_inc(loaded, 16)
                        sp.dma_start(blc[:, HEADS:], column(a["L2_gnn_bias"])).then_inc(loaded, 16)
                        sp.dma_start(bn_col[:, 0:1], column(a["L2_gnn_gamma"])).then_inc(loaded, 16)
                        sp.dma_start(bn_col[:, 1:2], column(a["L2_gnn_beta"])).then_inc(loaded, 16)
                    sp.dma_start(brb[:, :], a["L2_gnn_b_r"].rearrange("(o f) -> o f", o=1).to_broadcast((P, HF))).then_inc(loaded, 16)

                @block.vector
                def _(dve):
                    v = nc.vector
                    heads = lambda ap: ap.rearrange("p (h f) -> p h f", h=HEADS)
                    v.memset(attp[:, :, :], 0.0).then_inc(zeroed, 1)
                    dve.wait_ge(loaded, 16 * n_loads)
                    v.tensor_scalar(attc[:, :, :], attp[:, :, :], (1.0 - SLOPE) / 2, None, ALU.mult)
                    v.tensor_tensor(b_col[:, 0:2], halves[:, 0, :], halves[:, 1, :], ALU.add)
                    v.tensor_tensor(brb[:, :], brb[:, :], blb[:, :], ALU.add)
                    v.tensor_reduce(o_col[:, :], blc[:, 0:HEADS], AX.X, ALU.add)
                    v.drain()
                    v.scalar_tensor_tensor(o_col[:, :], o_col[:, :], 1.0 / HEADS, blc[:, HEADS:], ALU.mult, ALU.add)
                    v.tensor_scalar(b_col[:, 2:4], b_col[:, 0:2], SLOPE, None, ALU.mult)
                    for j, w in enumerate((brb, Wself)):
                        v.scalar_tensor_tensor(part[:, j, :], w[:, :], (1.0 + SLOPE) / 2, attb[:, :], ALU.mult, ALU.mult)
                    v.drain()
                    for j, to in enumerate((a_const, Vself)):
                        v.tensor_reduce(to[:, :], heads(part[:, j, :]), AX.X, ALU.add)

        def attention(tag):
            with nc.cleanup_on_exit(), ExitStack() as c, nc.Block() as block:
                tb = lambda name, shape, dt=f32: c.enter_context(nc.sbuf_tensor(tag + name, shape, dt))
                sm = lambda name: nc.alloc_semaphore(tag + name)
                two = lambda name: [sm(f"{name}{s}") for s in range(2)]
                E8 = 2 * HEADS
                win = lent(alpha, 2 * WT * F, lambda shape: tb("win", shape))
                own = lent(amax, 2 * HS * F, lambda shape: tb("own", shape))
                parts = tb("parts", [P, WT, 3, HF], bf16)
                idle = early[:, :]
                need = 4 * HS * P + 12 * NS + 348 + 2 * HS * F
                if idle.shape[1] < need:
                    idle = tb("idle", [P, need])[:, :]
                taken = [0]

                def carve(shape, dt=f32):
                    n = 1
                    for k in shape[1:]:
                        n *= k
                    lo, taken[0] = taken[0], taken[0] + (n if dt == f32 else n // 2)
                    view = idle[0:shape[0], lo:taken[0]]
                    view = view if dt == f32 else view.bitcast(dt)
                    names = "abc"[0:len(shape) - 1]
                    return view.rearrange(f"p ({' '.join(names)}) -> p {' '.join(names)}", **dict(zip(names, shape[1:])))
                agg = carve([P, HS, HEADS, F]); aggT = carve([P, 2, HS * P])
                exp_parts = carve([P, WT, 3, E8], bf16); ex_rest = tb("ex_rest", [P, WT, E8])
                score = carve([P, HS, HEADS]); me = carve([P, HS, HEADS]); mm = carve([P, HS, HEADS])
                den = carve([P, 2, HS, HEADS]); d = carve([P, 2, HS, HEADS]); cc = carve([P, 2, HS, HEADS])
                stats = carve([F, 2 * NS, 6])
                mine = [zeros_w[:, :].rearrange("p (t f) -> p t f", f=F), carve([P, HS, F]), carve([P, HS, F]), tb("mine", [P, HS, F])]
                shared = tb("shared", [P, 2, WR])
                oT = shared[0:F, :, 0:HS * P]; exw = shared[F:F + E8, :, :]
                exs = tb("exs", [P, WT, E8])
                msg = tb("msg", [P, HEADS, WT, F])
                S = tb("S", [P, BAND * HS, P], bf16)
                catT = tb("catT", [P, 2, HS * P]); az = tb("az", [P, 2, HS * P])
                mv = tb("mv", [F, 4])
                loads, stored = two("loads"), two("stored")
                hi_ok, rest_ok, parts_ok = sm("hi_ok"), sm("rest_ok"), sm("parts_ok")
                (madeA, readA, madeC, readC, ex_made, exs_ok, msg_ok, S_ok, own_made, sums_ok, small_read, d_ok, e_ok, c_ok, mine_ok, agg_ok,
                 aT_made, aT_read, stat_ok, var_ok, sd_ok, go) = (sm(n) for n in (
                     "madeA", "readA", "madeC", "readC", "ex_made", "exs_ok", "msg_ok", "S_ok", "own_made", "sums_ok", "small_read", "d_ok", "e_ok", "c_ok",
                     "mine_ok", "agg_ok", "aT_made", "aT_read", "stat_ok", "var_ok", "sd_ok", "go"))
                part = lambda k, h: parts[:, :, k, h * F:(h + 1) * F]
                CH = [(0, 4), (4, HS)]
                turned_ex = bank[7][:, 0:WT * E8].rearrange("p (t c) -> p t c", c=E8)
                own_ps = bank[7][:, 64:64 + HS * HEADS].rearrange("p (t h) -> p t h", h=HEADS)
                small_ps = bank[7][:, 128:128 + HS * E8].rearrange("p (t c) -> p t c", c=E8)
                assert N > (NS - 1) * HS * P

                @block.sync
                def _(sp):
                    def load(j, s, first):
                        n = 2 * j + s
                        if not first:
                            sp.wait_ge(mine_ok, n - 1)
                            sp.sem_inc(go, 1)
                            sp.wait_ge(own_made, n - 1)
                            sp.sem_inc(go, 1)
                        begin = nc.sync.value_load(starts[0:1, bass.ds(n, 1)], min_val=0, max_val=FRONT + NP)
                        at = bass.ds((j * BODY + s * HS) * P, HS * P)
                        sp.dma_start(own[:, s, :, :], tiles(node_g[at, :])).then_inc(loads[s], 16)
                        sp.dma_start(catT[F:2 * F, s, :], loop_rows[:, at]).then_inc(loads[s], 16)
                        sp.dma_start(exw[:, s, :], exp_all[:, bass.ds(begin, WR)]).then_inc(loads[s], 16)
                        sp.dma_start(win[:, s, :, :], tiles(edge_all[bass.ds(begin, WR), :])).then_inc(loads[s], 16)
                    for s in range(2):
                        load(0, s, True)
                    with nc.sync.Fori(1, GI) as j:
                        for s in range(2):
                            load(j, s, False)

                @block.gpsimd
                def _(pool):
                    g = nc.gpsimd

                    def messages(j, s, first):
                        n = 2 * j + s
                        pool.wait_ge(exs_ok, n + 1)
                        pool.wait_ge(loads[s], 64 * (j + 1))
                        if not first:
                            pool.wait_ge(parts_ok, n)
                        for h in range(HEADS):
                            g.tensor_tensor(msg[:, h, :, :], win[:, s, :, :], exs[:, :, h:h + 1].to_broadcast((P, WT, F)), ALU.mult).then_inc(msg_ok, 1)
                        for h in range(HEADS):
                            pool.wait_ge(hi_ok, HEADS * n + h + 1)
                            g.tensor_tensor(msg[:, h, :, :], msg[:, h, :, :], part(0, h), ALU.subtract).then_inc(rest_ok, 1)

                    def own_edges(j, s):
                        pool.wait_ge(c_ok, 2 * j + s + 1)
                        for h in range(HEADS):
                            ins = g.tensor_tensor(mine[h][:, :, :], own[:, s, :, :], cc[:, 1, :, h:h + 1].to_broadcast((P, HS, F)), ALU.mult)
                        ins.then_inc(mine_ok, 1)
                    messages(0, 0, True)
                    own_edges(0, 0)
                    messages(0, 1, False)
                    own_edges(0, 1)
                    with g.Fori(1, GI) as j:
                        for s in range(2):
                            messages(j, s, False)
                            own_edges(j, s)

                @block.tensor
                def _(pe):
                    def own_rows(j, s, first):
                        n = 2 * j + s
                        pe.wait_ge(loads[s], 64 * (j + 1))
                        if not first:
                            pe.wait_ge(small_read, n)
                        pe.sem_inc(go, 1)
                        for q in range(WT):
                            ins = nc.tensor.transpose(turned_ex[:, q, :], exw[:, s, q * P:(q + 1) * P], ident[F:F + E8, F:F + E8])
                        ins.then_inc(ex_made, 1)
                        for b, (t0, t1) in enumerate(CH):
                            if not first:
                                if isinstance(j, int) and n == 1:
                                    pe.wait_ge(readA, 4 + b)
                                else:
                                    pe.wait_ge(readC, 2 * n - 3 + b)
                            pe.sem_inc(go, 1)
                            for t in range(t0, t1):
                                ins = nc.tensor.transpose(bank[4 + b][0:F, (t - t0) * P:(t - t0 + 1) * P], own[:, s, t, :], ident[:, :])
                            ins.then_inc(madeA, 1)
                        for q, b, to, seen in ((0, 0, 6, 1), (0, 1, 4, 2), (1, 0, 5, 2), (1, 1, 6, 3)):
                            t0, t1 = CH[b]
                            pe.wait_ge(readA, 6 * n + seen)
                            nc.tensor.matmul(bank[to][:, 0:(t1 - t0) * P], Wself[:, q * P:(q + 1) * P], catT[:, s, t0 * P:t1 * P], start=True, stop=True).then_inc(madeA, 1)
                        pe.wait_ge(readA, 6 * n + 6)
                        pe.wait_ge(exs_ok, n + 1)
                        pe.sem_inc(go, 1)
                        for t in range(HS):
                            col = slice(t * P, (t + 1) * P)
                            nc.tensor.matmul(own_ps[:, t, :], catT[:, s, col], Vself[:, :], start=True, stop=False)
                            nc.tensor.matmul(own_ps[:, t, :], az[:, 0, col], attc[:, 0, :], start=False, stop=False)
                            ins = nc.tensor.matmul(own_ps[:, t, :], az[:, 1, col], attc[:, 1, :], start=False, stop=True)
                        ins.then_inc(own_made, 1)

                    def sums(n, first):
                        pe.wait_ge(parts_ok, n + 1)
                        for b, (t0, t1) in enumerate(CH):
                            pe.wait_ge(S_ok, 2 * n + b + 1)
                            for t in range(t0, t1):
                                for q in range(BAND):
                                    mat, e = S[:, BAND * t + q, :], t + q
                                    for k in range(3):
                                        first_p, last_p = q == 0 and k == 0, q == BAND - 1 and k == 2
                                        nc.tensor.matmul(bank[t // 2][:, (t % 2) * HF:(t % 2 + 1) * HF], mat, parts[:, e, k, :], start=first_p, stop=last_p)
                                        ins = nc.tensor.matmul(small_ps[:, t, :], mat, exp_parts[:, e, k, :], start=first_p, stop=last_p)
                            ins.then_inc(sums_ok, 1)

                    def outputs(m):
                        pe.wait_ge(agg_ok, m + 1)
                        pe.sem_inc(go, 1)
                        for k, (b, q) in enumerate(((0, 0), (0, 1), (1, 0), (1, 1))):
                            t0, t1 = CH[b]
                            for t in range(t0, t1):
                                ins = nc.tensor.transpose(bank[k][:, (t - t0) * P:(t - t0 + 1) * P], agg[:, t, 2 * q:2 * q + 2, :].rearrange("p h f -> p (h f)"), ident[:, :])
                            ins.then_inc(aT_made, 1)
                        for b, (t0, t1) in enumerate(CH):
                            pe.wait_ge(aT_read, 4 * m + 2 * b + 2)
                            pe.sem_inc(go, 1)
                            for q in range(2):
                                ins = nc.tensor.matmul(bank[4 + b][0:F, 0:(t1 - t0) * P], Wst[:, q, :], aggT[:, q, t0 * P:t1 * P], start=(q == 0), stop=(q == 1))
                            ins.then_inc(madeC, 1)

                    own_rows(0, 0, True)
                    sums(0, True)
                    own_rows(0, 1, False)
                    outputs(0)
                    sums(1, False)
                    with nc.tensor.Fori(1, GI) as j:
                        for s in range(2):
                            own_rows(j, s, False)
                            outputs(2 * j + s - 1)
                            sums(2 * j + s, False)
                    outputs(NS - 1)

                @block.scalar
                def _(act):
                    A = nc.scalar

                    def own_rows(j, s, first):
                        n = 2 * j + s
                        if not first:
                            act.wait_ge(own_made, n)
                        for b, (t0, t1) in enumerate(CH):
                            act.wait_ge(madeA, 6 * n + 1 + b)
                            A.copy(catT[0:F, s, t0 * P:t1 * P], bank[4 + b][0:F, 0:(t1 - t0) * P]).then_inc(readA, 1)
                        for k, (q, b, to) in enumerate(((0, 0, 6), (0, 1, 4), (1, 0, 5), (1, 1, 6))):
                            t0, t1 = CH[b]
                            act.wait_ge(madeA, 6 * n + 3 + k)
                            A.activation(az[:, q, t0 * P:t1 * P], bank[to][:, 0:(t1 - t0) * P], ACT.Abs, bias=b_col[:, q:q + 1], scale=1.0).then_inc(readA, 1)

                    def exps(n):
                        act.wait_ge(d_ok, n + 1)
                        A.activation(d[:, :, :, :], d[:, :, :, :], ACT.Exp).then_inc(e_ok, 1)

                    def outputs(i, s, m, first):
                        for k, (b, q) in enumerate(((0, 0), (0, 1), (1, 0), (1, 1))):
                            t0, t1 = CH[b]
                            act.wait_ge(aT_made, 4 * m + k + 1)
                            A.copy(aggT[:, q, t0 * P:t1 * P], bank[k][:, 0:(t1 - t0) * P]).then_inc(aT_read, 1)
                        if not first:
                            act.wait_ge(stored[s], 16 * i)
                            act.wait_ge(stat_ok, m - 1)
                        for b, (t0, t1) in enumerate(CH):
                            act.wait_ge(madeC, 2 * m + b + 1)
                            A.activation(oT[:, s, t0 * P:t1 * P], bank[4 + b][0:F, 0:(t1 - t0) * P], ACT.Identity, bias=o_col[:, 0:1], scale=1.0 / HEADS).then_inc(readC, 1)
                        act.wait_ge(readC, 2 * m + 2)
                        act.sem_inc(go, 1)
                        act.dma_start(gat_rows[:, bass.ds((i * BODY + s * HS) * P, HS * P)], oT[:, s, :]).then_inc(stored[s], 16)

                    own_rows(0, 0, True)
                    exps(0)
                    own_rows(0, 1, False)
                    outputs(0, 0, 0, True)
                    exps(1)

                    def body(j, first):
                        own_rows(j, 0, False)
                        outputs(j - 1, 1, 2 * j - 1, first)
                        exps(2 * j)
                        own_rows(j, 1, False)
                        outputs(j, 0, 2 * j, False)
                        exps(2 * j + 1)
                    body(1, True)
                    with A.Fori(2, GI) as j:
                        body(j, False)
                    outputs(GI - 1, 1, NS - 1, False)
                    act.wait_ge(var_ok, 1)
                    A.activation(mv[:, 2:3], mv[:, 1:2], ACT.Sqrt, bias=eps[0:F, 0:1]).then_inc(sd_ok, 1)
                    for s in range(2):
                        act.wait_ge(stored[s], 16 * GI)

                @block.vector
                def _(dve):
                    v = nc.vector

                    def matrices(n, first):
                        for b, (t0, t1) in enumerate(CH):
                            if not first:
                                dve.wait_ge(sums_ok, 2 * n - 1 + b)
                            k = BAND * (t1 - t0)
                            v.tensor_tensor(S[:, BAND * t0:BAND * t1, :], node_id[:, :].unsqueeze(1).to_broadcast((P, k, P)),
                                            edge_id[:, bass.ds(n * BAND * HS + BAND * t0, k)].unsqueeze(2).to_broadcast((P, k, P)), ALU.is_equal).then_inc(S_ok, 1)

                    def exponentials(n, first):
                        dve.wait_ge(ex_made, n + 1)
                        if not first:
                            dve.wait_ge(msg_ok, HEADS * n)
                        v.tensor_copy(exs[:, :, :], turned_ex).then_inc(exs_ok, 1)

                    def splits(n, first):
                        v.drain()
                        if not first:
                            dve.wait_ge(sums_ok, 2 * n)
                        for h in range(HEADS):
                            dve.wait_ge(msg_ok, HEADS * n + h + 1)
                            v.tensor_copy(part(0, h), msg[:, h, :, :]).then_inc(hi_ok, 1)
                        v.tensor_copy(exp_parts[:, :, 0, :], exs[:, :, :])
                        v.drain()
                        v.tensor_tensor(ex_rest[:, :, :], exs[:, :, :], exp_parts[:, :, 0, :], ALU.subtract)
                        v.drain()
                        v.tensor_copy(exp_parts[:, :, 1, :], ex_rest[:, :, :])
                        v.drain()
                        v.tensor_tensor(exp_parts[:, :, 2, :], ex_rest[:, :, :], exp_parts[:, :, 1, :], ALU.subtract)
                        for h in range(HEADS):
                            dve.wait_ge(rest_ok, HEADS * n + h + 1)
                            v.tensor_copy(part(1, h), msg[:, h, :, :])
                            v.drain()
                            v.tensor_tensor(part(2, h), msg[:, h, :, :], part(1, h), ALU.subtract)
                        v.drain()
                        v.sem_inc(parts_ok, 1)

                    def weights(j, s, first, following):
                        n = 2 * j + s
                        tl = bass.ds(j * BODY + s * HS, HS)
                        dve.wait_ge(own_made, n + 1)
                        dve.wait_ge(sums_ok, 2 * n + 2)
                        v.tensor_tensor(score[:, :, :], own_ps, a_const[:, :].unsqueeze(1).to_broadcast((P, HS, HEADS)), ALU.add)
                        v.tensor_tensor(me[:, :, :], small_ps[:, :, HEADS:E8], no_edge[:, tl].unsqueeze(2).to_broadcast((P, HS, HEADS)), ALU.add)
                        v.tensor_copy(den[:, 0, :, :], small_ps[:, :, 0:HEADS]).then_inc(small_read, 1)
                        v.drain()
                        v.tensor_tensor(mm[:, :, :], me[:, :, :], score[:, :, :], ALU.max)
                        v.drain()
                        v.tensor_tensor(d[:, 0, :, :], me[:, :, :], mm[:, :, :], ALU.subtract)
                        v.tensor_tensor(d[:, 1, :, :], score[:, :, :], mm[:, :, :], ALU.subtract).then_inc(d_ok, 1)
                        dve.wait_ge(e_ok, n + 1)
                        v.tensor_tensor(den[:, 0, :, :], den[:, 0, :, :], d[:, 0, :, :], ALU.mult)
                        v.drain()
                        v.scalar_tensor_tensor(den[:, 1, :, :], den[:, 0, :, :], SM_EPS, d[:, 1, :, :], ALU.add, ALU.add)
                        v.drain()
                        v.reciprocal(den[:, 0, :, :], den[:, 1, :, :])
                        v.drain()
                        v.tensor_tensor(cc[:, :, :, :], d[:, :, :, :], den[:, 0:1, :, :].to_broadcast((P, 2, HS, HEADS)), ALU.mult).then_inc(c_ok, 1)
                        if following is not None:
                            exponentials(following, False)
                        v.drain()
                        if not first:
                            dve.wait_ge(aT_made, 4 * n)
                        for t in range(0, HS, 2):
                            k = min(2, HS - t)
                            v.tensor_tensor(agg[:, t:t + k, :, :].rearrange("p t h f -> p (t h) f"), bank[t // 2][:, 0:k * HF].rearrange("p (g f) -> p g f", f=F),
                                            cc[:, 0, t:t + k, :].rearrange("p t h -> p (t h)").unsqueeze(2).to_broadcast((P, k * HEADS, F)), ALU.mult)
                        v.drain()
                        dve.wait_ge(mine_ok, n + 1)
                        for h in range(HEADS):
                            ins = v.tensor_tensor(agg[:, :, h, :], agg[:, :, h, :], mine[h][:, :, :], ALU.add)
                        ins.then_inc(agg_ok, 1)

                    def moments(s, m, last):
                        width = N - (NS - 1) * HS * P if last else HS * P
                        half = HS * P // 2
                        dve.wait_ge(readC, 2 * m + 2)
                        for k in range(2):
                            lo, hi = k * half, min((k + 1) * half, width)
                            if hi > lo:
                                v.bn_stats(stats[:, bass.ds(2 * m + k, 1), :].rearrange("p o c -> p (o c)"), oT[:, s, lo:hi])
                        v.drain()
                        v.sem_inc(stat_ok, 1)

                    def step(j, s, first):
                        n = 2 * j + s
                        last = isinstance(j, int) and n == NS - 1
                        weights(j, s, first, None if last else n + 1)
                        if not last:
                            matrices(n + 1, False)
                            splits(n + 1, False)
                        if not first:
                            moments(1 - s, n - 1, False)
                    exponentials(0, True)
                    matrices(0, True)
                    splits(0, True)
                    step(0, 0, True)
                    step(0, 1, False)
                    with v.Fori(1, GI - 1) as j:
                        for s in range(2):
                            step(j, s, False)
                    step(GI - 1, 0, False)
                    step(GI - 1, 1, False)
                    moments(1, NS - 1, True)
                    used = 2 * NS if N - (NS - 1) * HS * P > HS * P // 2 else 2 * NS - 1
                    v.bn_aggr(mv[:, 0:2], stats[:, 0:used, :].rearrange("p k c -> p (k c)"))
                    v.drain()
                    v.sem_inc(var_ok, 1)
                    dve.wait_ge(sd_ok, 1)
                    v.reciprocal(mv[:, 3:4], mv[:, 2:3])
                    v.drain()
                    v.tensor_tensor(bn_col[:, 0:1], bn_col[:, 0:1], mv[:, 3:4], ALU.mult)
                    v.drain()
                    v.tensor_tensor(mv[:, 2:3], mv[:, 0:1], bn_col[:, 0:1], ALU.mult)
                    v.drain()
                    v.tensor_tensor(bn_col[:, 1:2], bn_col[:, 1:2], mv[:, 2:3], ALU.subtract)

        def batch_norm(tag):
            with nc.cleanup_on_exit(), ExitStack() as c, nc.Block() as block:
                tb = lambda name, shape, dt=f32: c.enter_context(nc.sbuf_tensor(tag + name, shape, dt))
                sm = lambda name: nc.alloc_semaphore(tag + name)
                two = lambda name: [sm(f"{name}{s}") for s in range(2)]
                oT = tb("oT", [F, 2, HS * P]); rT = tb("rT", [F, 2, HS * P])
                xn = tb("xn", [P, 2, HS, F]); h = tb("h", [P, 2, HS, F])
                bs = tb("bs", [P, 2, HS, 6]); ln = tb("ln", [P, 2, 8, HS])
                loaded, r_ok, turned, x_ok, x_kept, var_ok, sd_ok, ln_ok, h_ok, stored, go = (
                    two("loaded"), two("r_ok"), two("turned"), two("x_ok"), two("x_kept"), two("var_ok"), two("sd_ok"), two("ln_ok"), two("h_ok"), two("stored"), sm("go"))

                @block.sync
                def _(sp):
                    def body(j, first):
                        for s in range(2):
                            if not first:
                                sp.wait_ge(r_ok[s], j)
                            sp.dma_start(oT[:, s, :], gat_rows[:, bass.ds((j * BODY + s * HS) * P, HS * P)]).then_inc(loaded[s], 16)
                    body(0, True)
                    with nc.sync.Fori(1, GI) as j:
                        body(j, False)

                @block.gpsimd
                def _(pool):
                    with nc.gpsimd.Fori(0, GI) as j:
                        for s in range(2):
                            pool.wait_ge(x_ok[s], j + 1)
                            nc.gpsimd.tensor_copy(x_sb[:, bass.ds(j * BODY + s * HS, HS), :], xn[:, s, :, :]).then_inc(x_kept[s], 1)

                @block.tensor
                def _(pe):
                    def body(j, first):
                        for s in range(2):
                            pe.wait_ge(r_ok[s], j + 1)
                            if not first:
                                pe.wait_ge(x_ok[s], j)
                            pe.sem_inc(go, 1)
                            for t in range(HS):
                                ins = nc.tensor.transpose(bank[s][:, t * F:(t + 1) * F], rT[:, s, t * P:(t + 1) * P], ident[0:F, 0:F])
                            ins.then_inc(turned[s], 1)
                    body(0, True)
                    with nc.tensor.Fori(1, GI) as j:
                        body(j, False)

                @block.scalar
                def _(act):
                    A = nc.scalar

                    def rows_out(j, s, first):
                        act.wait_ge(var_ok[s], j + 1)
                        A.activation(ln[:, s, 4, :], ln[:, s, 3, :], ACT.Sqrt, bias=eps[:, 0:1], scale=1.0 / F).then_inc(sd_ok[s], 1)
                        act.wait_ge(ln_ok[s], j + 1)
                        if not first:
                            act.wait_ge(stored[s], 16 * j)
                        for t in range(HS):
                            ins = A.activation(h[:, s, t, :], xn[:, s, t, :], ACT.Relu, bias=ln[:, s, 6, t:t + 1], scale=ln[:, s, 5, t:t + 1])
                        ins.then_inc(h_ok[s], 1)
                        act.wait_ge(h_ok[s], j + 1)
                        A.sem_inc(go, 1)
                        act.dma_start(tiles(node_g[bass.ds((j * BODY + s * HS) * P, HS * P), :]), h[:, s, :, :]).then_inc(stored[s], 16)

                    for s in range(2):
                        rows_out(0, s, True)
                    with A.Fori(1, GI) as j:
                        for s in range(2):
                            rows_out(j, s, False)
                    for s in range(2):
                        act.wait_ge(stored[s], 16 * GI)

                @block.vector
                def _(dve):
                    v = nc.vector

                    def affine(j, s, first):
                        dve.wait_ge(loaded[s], 16 * (j + 1))
                        if not first:
                            dve.wait_ge(turned[s], j)
                        v.tensor_scalar(rT[:, s, :], oT[:, s, :], bn_col[:, 0:1], bn_col[:, 1:2], ALU.mult, ALU.add).then_inc(r_ok[s], 1)

                    def body(j, first, last):
                        for s in range(2):
                            tl = bass.ds(j * BODY + s * HS, HS)
                            dve.wait_ge(turned[s], j + 1)
                            if not first:
                                dve.wait_ge(x_kept[s], j)
                                dve.wait_ge(h_ok[s], j)
                            v.scalar_tensor_tensor(xn[:, s, :, :], bank[s][:, 0:HS * F].rearrange("p (t f) -> p t f", t=HS), 0.0, x_sb[:, tl, :], ALU.max, ALU.add).then_inc(x_ok[s], 1)
                            v.drain()
                            normalise(dve, j, s, tl, xn, bs, ln, var_ok, sd_ok, ln_ok, False, None if last else lambda: affine(j + 1, s, False))
                    for s in range(2):
                        affine(0, s, True)
                    body(0, True, False)
                    with v.Fori(1, GI - 1) as j:
                        body(j, False, False)
                    body(GI - 1, False, True)

        prepare()
        attention_weights()
        plan()
        first_norm("n0")
        window_numbers()
        regular = nc.values_load(fast[0:1, 0:1], min_val=0, max_val=1)
        with nc.If(regular):
            layer("l0", "conv", node_g, node_g2)
            layer("l1", "sage", node_g2, node_g)
            edge_scores("fs")
            segment_max("fm", True)
            attention("fa")
            batch_norm("fb")
            for k in range(3):
                layer(f"l{3 + k}", "typed", (node_g, node_g2, node_g)[k], (node_g2, node_g, None)[k], k)
        with nc.Else():
            clear_sums()
            edge_sums("e0", "wide", 2 * F, sums_w)
            nodes("n1", "conv")
            edge_sums("e1", "plain", F, sums_n)
            nodes("n2", "sage")
            edge_scores("es")
            segment_max("sm", False)
            edge_sums("e2", "gat", GATW, sums_a)
            attend("at")
            variance("bv")
            nodes("n3", "bn")
            for k in range(3):
                edge_sums(f"f{k}", "typed", 2 * F, sums_w)
                nodes(f"r{k}", "rel", k)


INPUTS = ["x", "src", "dst", "edge_attr_64", "edge_type_2", "L0_gnn_weight", "L0_gnn_bias", "L1_gnn_W", "L1_gnn_b",
          "L2_gnn_W_l", "L2_gnn_b_l", "L2_gnn_W_r", "L2_gnn_b_r", "L2_gnn_W_e", "L2_gnn_att", "L2_gnn_bias",
          "L2_gnn_gamma", "L2_gnn_beta", "L3_gnn_W0", "L3_gnn_Ws0", "L3_gnn_b0", "L3_gnn_W1", "L3_gnn_Ws1",
          "L3_gnn_b1", "L3_gnn_W2", "L3_gnn_Ws2", "L3_gnn_b2"]


def kernel(**inputs):
    import numpy as np
    import concourse.bacc as bacc
    from concourse.bass_utils import run_bass_kernel_spmd

    nc = bacc.Bacc("TRN2", target_bir_lowering=False, num_devices=1)
    arrays, args = {}, {}
    for name in INPUTS:
        v = np.ascontiguousarray(inputs[name])
        arrays[f"in_{name}"] = v
        args[name] = nc.dram_tensor(f"in_{name}", v.shape, mybir.dt.from_np(v.dtype), kind="ExternalInput").ap()
    shape = tuple(inputs["x"].shape)
    result = nc.dram_tensor("result", shape, mybir.dt.float32, kind="ExternalOutput").ap()
    build_gnn(nc, args, result)
    return run_bass_kernel_spmd(nc, [arrays], core_ids=[0]).results[0]["result"]
```
